# Optimizing a Trainium2 kernel written in Bass

```python
import numpy as np
import jax
import jax.numpy as jnp

def _softmax(x, axis=-1):
    return jax.nn.softmax(x, axis=axis)

def _gelu(x):
    return jax.nn.gelu(x, approximate=True)

def _silu(x):
    return jax.nn.silu(x)

def _sigmoid(x):
    return jax.nn.sigmoid(x)

def _layernorm(x, axis=-1, eps=1e-05):
    m = jnp.mean(x, axis=axis, keepdims=True)
    v = jnp.var(x, axis=axis, keepdims=True)
    return (x - m) / jnp.sqrt(v + eps)

def _scatter_add(tgt, idx, src, axis=0):
    return tgt.at[idx].add(src)

def _segment_sum(src, seg, n):
    return jax.ops.segment_sum(src, seg, n)
kernel_name = 'mk_adaln_attn_ffn_d2_seqx_r8_b0e8b5'

def setup_inputs(seed: int=0):
    np.random.seed(seed)
    _w = jnp.asarray

    def _rec_inputs():
        import jax
        import jax.numpy as jnp
        _rk = jax.random.key(seed)
        x = -0.0002928 + 1 * jax.random.normal(jax.random.fold_in(_rk, 1), (32, 32, 128), jnp.float32)
        _lenS = 32 - jax.random.randint(jax.random.fold_in(_rk, 7), (32,), 0, max(1, 32 // 4) + 1, jnp.int32)
        _lenS2 = 32 - jax.random.randint(jax.random.fold_in(_rk, 8), (32,), 0, max(1, 32 // 4) + 1, jnp.int32)
        cond_256 = -0.106481 + 1.03144 * jax.random.normal(jax.random.fold_in(_rk, 12), (32, 32), jnp.float32)
        _validS = jnp.arange(32)[None, :] < _lenS[:, None]
        _validS2 = jnp.arange(32)[None, :] < _lenS2[:, None]
        _causal = jnp.tril(jnp.ones((32, 32), dtype=bool))
        mask_SxS_bk1 = jnp.broadcast_to(_validS[0:1, :], (32, 32))
        return (x, cond_256, mask_SxS_bk1)
    x, cond_256, mask_SxS_bk1 = _rec_inputs()

    def _L0_cond_setup():
        import jax, jax.numpy as jnp
        import numpy as np
        EPS = 1e-06
        key = jax.random.key(seed)
        ks = jax.random.split(key, 8)
        B, S, E, C = (2, 256, 128, 32)
        x = jax.random.normal(ks[0], (B, S, E), dtype=jnp.float32)
        mask = jnp.triu(jnp.ones((S, S), dtype=bool), k=1)
        conditioning = jax.random.normal(ks[1], (B, C), dtype=jnp.float32)
        sc = 1.0 / np.sqrt(E)
        Wq = jax.random.normal(ks[2], (E, E), dtype=jnp.float32) * sc
        Wk = jax.random.normal(ks[3], (E, E), dtype=jnp.float32) * sc
        Wv = jax.random.normal(ks[4], (E, E), dtype=jnp.float32) * sc
        Wo = jax.random.normal(ks[5], (E, E), dtype=jnp.float32) * sc
        rms_scale = jnp.ones((E,), dtype=jnp.float32)
        Wc = jax.random.normal(ks[6], (2 * E, C), dtype=jnp.float32) * 0.02
        bc = jax.random.normal(ks[7], (2 * E,), dtype=jnp.float32) * 0.02
        return {'x': x, 'mask': mask, 'conditioning': conditioning, 'Wq': Wq, 'Wk': Wk, 'Wv': Wv, 'Wo': Wo, 'rms_scale': rms_scale, 'Wc': Wc, 'bc': bc}
    _L0_cond_all = _L0_cond_setup()
    _L0_cond_in = {k: v for k, v in _L0_cond_all.items() if k in ('Wq', 'Wk', 'Wv', 'Wo', 'rms_scale', 'Wc', 'bc')}
    del _L0_cond_all

    def _L0_attn_setup():
        import jax, jax.numpy as jnp
        import numpy as np
        DIM = 128
        HEADS = 16
        HEAD_DIM = 64
        ROT = 32
        BASE = 10000.0
        SEQ = 256
        BATCH = 2

        def _rotate_half(t):
            x1, x2 = (t[..., :ROT // 2], t[..., ROT // 2:])
            return jnp.concatenate([-x2, x1], axis=-1)

        def _apply_rope(t, cos, sin):
            t_rot, t_pass = (t[..., :ROT], t[..., ROT:])
            t_rot = t_rot * cos + _rotate_half(t_rot) * sin
            return jnp.concatenate([t_rot, t_pass], axis=-1)
        key = jax.random.key(seed)
        k1, k2, k3, k4 = jax.random.split(key, 4)
        s = 0.02
        return {'x': jax.random.normal(k1, (BATCH, SEQ, DIM), dtype=jnp.float32), 'w_q': jax.random.normal(k2, (DIM, HEADS * HEAD_DIM), dtype=jnp.float32) * s, 'w_kv': jax.random.normal(k3, (DIM, 2 * HEADS * HEAD_DIM), dtype=jnp.float32) * s, 'w_out': jax.random.normal(k4, (HEADS * HEAD_DIM, DIM), dtype=jnp.float32) * s}
    _L0_attn_all = _L0_attn_setup()
    _L0_attn_in = {k: v for k, v in _L0_attn_all.items() if k in ('w_q', 'w_kv', 'w_out')}
    del _L0_attn_all

    def _L0_cond2_setup():
        import jax, jax.numpy as jnp
        import numpy as np
        EPS = 1e-08

        def hamilton(q1, q2):
            w1, x1, y1, z1 = (q1[..., i, :] for i in range(4))
            w2, x2, y2, z2 = (q2[..., i, :] for i in range(4))
            w = w1 * w2 - x1 * x2 - y1 * y2 - z1 * z2
            x = w1 * x2 + x1 * w2 + y1 * z2 - z1 * y2
            y = w1 * y2 - x1 * z2 + y1 * w2 + z1 * x2
            z = w1 * z2 + x1 * y2 - y1 * x2 + z1 * w2
            return jnp.stack([w, x, y, z], axis=-2)

        def _normalize(q):
            return q / jnp.sqrt(jnp.sum(q * q, axis=0, keepdims=True) + EPS)
        key = jax.random.key(seed)
        k1, k2, k3, k4 = jax.random.split(key, 4)
        B, T, d_model = (4, 512, 128)
        quat_dim = d_model // 4
        x = jax.random.normal(k1, (B, T, d_model), dtype=jnp.float32)
        q_left = jax.random.normal(k2, (4, quat_dim), dtype=jnp.float32)
        q_right = jax.random.normal(k3, (4, quat_dim), dtype=jnp.float32)
        spectral_gate = jax.random.uniform(k4, (1, 1, 1, quat_dim), dtype=jnp.float32)
        return {'x': x, 'q_left': q_left, 'q_right': q_right, 'spectral_gate': spectral_gate}
    _L0_cond2_all = _L0_cond2_setup()
    _L0_cond2_in = {k: v for k, v in _L0_cond2_all.items() if k in ('q_right', 'spectral_gate')}
    del _L0_cond2_all

    def _L0_ffn_setup():
        import jax, jax.numpy as jnp
        import numpy as np
        N_EMBD = 128
        NUM_EXPERTS = 8
        TOP_K = 2
        D_FF = 4 * N_EMBD
        B, S = (4, 256)
        key = jax.random.key(seed)
        ks = jax.random.split(key, 7)
        scale = lambda fan_in: 1.0 / np.sqrt(fan_in)
        x = jax.random.normal(ks[0], (B, S, N_EMBD), dtype=jnp.float32)
        W_router = jax.random.normal(ks[1], (N_EMBD, NUM_EXPERTS), dtype=jnp.float32) * scale(N_EMBD)
        b_router = jnp.zeros((NUM_EXPERTS,), dtype=jnp.float32)
        W1 = jax.random.normal(ks[2], (NUM_EXPERTS, N_EMBD, D_FF), dtype=jnp.float32) * scale(N_EMBD)
        b1 = jnp.zeros((NUM_EXPERTS, D_FF), dtype=jnp.float32)
        W2 = jax.random.normal(ks[3], (NUM_EXPERTS, D_FF, N_EMBD), dtype=jnp.float32) * scale(D_FF)
        b2 = jnpp = jnp.zeros((NUM_EXPERTS, N_EMBD), dtype=jnp.float32)
        return {'x': x, 'W_router': W_router, 'b_router': b_router, 'W1': W1, 'b1': b1, 'W2': W2, 'b2': b2}
    _L0_ffn_all = _L0_ffn_setup()
    _L0_ffn_in = {k: v for k, v in _L0_ffn_all.items() if k in ('W_router', 'b_router', 'W1', 'b1', 'W2', 'b2')}
    del _L0_ffn_all

    def _L1_cond_setup():
        import jax, jax.numpy as jnp
        import numpy as np
        TOP_K = 2
        EPS = 1e-06
        B, S, H, G, E, M = (2, 256, 128, 32, 8, 256)
        key = jax.random.key(seed)
        ks = jax.random.split(key, 16)
        s_h = 1.0 / np.sqrt(H)
        s_g = 1.0 / np.sqrt(G)
        s_m = 1.0 / np.sqrt(M)
        return {'x': jax.random.normal(ks[0], (B, S, H), jnp.float32), 'genre_embed': jax.random.normal(ks[1], (B, 1, G), jnp.float32), 'rms_w': jnp.ones((H,), jnp.float32), 'wg_W': jax.random.normal(ks[2], (H, E), jnp.float32) * s_h, 'wg_b': jnp.zeros((E,), jnp.float32), 'gg_W': jax.random.normal(ks[3], (G, E), jnp.float32) * s_g, 'gg_b': jnp.zeros((E,), jnp.float32), 'W1': jax.random.normal(ks[4], (E, H, M), jnp.float32) * s_h, 'b1': jnp.zeros((E, M), jnp.float32), 'W2': jax.random.normal(ks[5], (E, M, M), jnp.float32) * s_m, 'b2': jnp.zeros((E, M), jnp.float32), 'W3': jax.random.normal(ks[6], (E, M, H), jnp.float32) * s_m, 'b3': jnp.zeros((E, H), jnp.float32)}
    _L1_cond_all = _L1_cond_setup()
    _L1_cond_in = {k: v for k, v in _L1_cond_all.items() if k in ('rms_w', 'wg_W', 'wg_b', 'gg_W', 'gg_b', 'W1', 'b1', 'W2', 'b2', 'W3', 'b3')}
    del _L1_cond_all

    def _L1_attn_setup():
        import jax, jax.numpy as jnp
        import numpy as np
        D_MODEL = 128
        H = 8
        S = 128
        HD = 128
        LV = 12
        B = 2
        T = 256

        def _level_structure(t, num_levels):
            idx = np.arange(t)
            d = idx[:, None] - idx[None, :]
            lvl = np.where(d <= 0, 0, np.floor(np.log2(np.maximum(d, 1))).astype(np.int64) + 1)
            lvl = np.minimum(lvl, num_levels - 1)
            mask = d >= 0
            return (jnp.asarray(lvl), jnp.asarray(mask))
        key = jax.random.key(seed)
        ks = jax.random.split(key, 8)
        sd = 1.0 / np.sqrt(D_MODEL)
        return {'x': jax.random.normal(ks[0], (B, T, D_MODEL), jnp.float32), 'Wq': jax.random.normal(ks[1], (H * S, D_MODEL), jnp.float32) * sd, 'Wk': jax.random.normal(ks[2], (H * S, D_MODEL), jnp.float32) * sd, 'Wv': jax.random.normal(ks[3], (H * HD, D_MODEL), jnp.float32) * sd, 'Wg': jax.random.normal(ks[4], (H, D_MODEL), jnp.float32) * sd, 'bg': jnp.zeros((H,), jnp.float32), 'Wdl': jax.random.normal(ks[5], (H * LV, D_MODEL), jnp.float32) * sd, 'Lparam': jnp.ones((H, LV), jnp.float32), 'Wo': jax.random.normal(ks[6], (D_MODEL, H * HD), jnp.float32) / np.sqrt(H * HD), 'ln_g': jnp.ones((D_MODEL,), jnp.float32), 'ln_b': jnp.zeros((D_MODEL,), jnp.float32)}
    _L1_attn_all = _L1_attn_setup()
    _L1_attn_in = {k: v for k, v in _L1_attn_all.items() if k in ('Wq', 'Wk', 'Wv', 'Wg', 'bg', 'Wdl', 'Lparam', 'Wo', 'ln_g', 'ln_b')}
    del _L1_attn_all

    def _L1_cond2_setup():
        import jax, jax.numpy as jnp
        import numpy as np
        EPS = 1e-06
        key = jax.random.key(seed)
        ks = jax.random.split(key, 8)
        B, S, E, C = (2, 256, 128, 32)
        x = jax.random.normal(ks[0], (B, S, E), dtype=jnp.float32)
        mask = jnp.triu(jnp.ones((S, S), dtype=bool), k=1)
        conditioning = jax.random.normal(ks[1], (B, C), dtype=jnp.float32)
        sc = 1.0 / np.sqrt(E)
        Wq = jax.random.normal(ks[2], (E, E), dtype=jnp.float32) * sc
        Wk = jax.random.normal(ks[3], (E, E), dtype=jnp.float32) * sc
        Wv = jax.random.normal(ks[4], (E, E), dtype=jnp.float32) * sc
        Wo = jax.random.normal(ks[5], (E, E), dtype=jnp.float32) * sc
        rms_scale = jnp.ones((E,), dtype=jnp.float32)
        Wc = jax.random.normal(ks[6], (2 * E, C), dtype=jnp.float32) * 0.02
        bc = jax.random.normal(ks[7], (2 * E,), dtype=jnp.float32) * 0.02
        return {'x': x, 'mask': mask, 'conditioning': conditioning, 'Wq': Wq, 'Wk': Wk, 'Wv': Wv, 'Wo': Wo, 'rms_scale': rms_scale, 'Wc': Wc, 'bc': bc}
    _L1_cond2_all = _L1_cond2_setup()
    _L1_cond2_in = {k: v for k, v in _L1_cond2_all.items() if k in ('Wq', 'Wk', 'Wv', 'Wo', 'rms_scale', 'Wc', 'bc')}
    del _L1_cond2_all

    def _L1_ffn_setup():
        import jax, jax.numpy as jnp
        import numpy as np
        B, S, D_MODEL, D_HIDDEN = (4, 256, 128, 512)

        def act_quant(x):
            scale = 127.0 / jnp.clip(jnp.max(jnp.abs(x), axis=-1, keepdims=True), 1e-05)
            return jnp.clip(jnp.round(x * scale), -128, 127) / scale

        def weight_quant(w):
            scale = 1.0 / jnp.clip(jnp.mean(jnp.abs(w)), 1e-05)
            return jnp.clip(jnp.round(w * scale), -1, 1) / scale

        def bit_linear(x, w):
            xq = x + jax.lax.stop_gradient(act_quant(x) - x)
            wq = w + jax.lax.stop_gradient(weight_quant(w) - w)
            return jnp.einsum('bsd,hd->bsh', xq, wq)

        def depthwise_conv1d(x_bcl, w, b):
            y = jax.lax.conv_general_dilated(x_bcl, w, window_strides=(1,), padding=[(1, 1)], dimension_numbers=('NCH', 'OIH', 'NCH'), feature_group_count=x_bcl.shape[1])
            return y + b[None, :, None]
        key = jax.random.key(seed)
        ks = jax.random.split(key, 5)
        lim1 = 1.0 / np.sqrt(D_MODEL)
        lim2 = 1.0 / np.sqrt(D_HIDDEN)
        limc = 1.0 / np.sqrt(3.0)
        return {'x': jax.random.normal(ks[0], (B, S, D_MODEL), dtype=jnp.float32), 'w1': jax.random.uniform(ks[1], (D_HIDDEN, D_MODEL), jnp.float32, -lim1, lim1), 'conv_w': jax.random.uniform(ks[2], (D_HIDDEN, 1, 3), jnp.float32, -limc, limc), 'conv_b': jax.random.uniform(ks[3], (D_HIDDEN,), jnp.float32, -limc, limc), 'w2': jax.random.uniform(ks[4], (D_MODEL, D_HIDDEN), jnp.float32, -lim2, lim2)}
    _L1_ffn_all = _L1_ffn_setup()
    _L1_ffn_in = {k: v for k, v in _L1_ffn_all.items() if k in ('w1', 'conv_w', 'conv_b', 'w2')}
    del _L1_ffn_all
    return {'x': x, 'cond_256': cond_256, 'mask_SxS_bk1': mask_SxS_bk1, 'L0_cond_Wq': _L0_cond_in['Wq'], 'L0_cond_Wk': _L0_cond_in['Wk'], 'L0_cond_Wv': _L0_cond_in['Wv'], 'L0_cond_Wo': _L0_cond_in['Wo'], 'L0_cond_rms_scale': _L0_cond_in['rms_scale'], 'L0_cond_Wc': _L0_cond_in['Wc'], 'L0_cond_bc': _L0_cond_in['bc'], 'L0_attn_w_q': _L0_attn_in['w_q'], 'L0_attn_w_kv': _L0_attn_in['w_kv'], 'L0_attn_w_out': _L0_attn_in['w_out'], 'L0_cond2_q_right': _L0_cond2_in['q_right'], 'L0_cond2_spectral_gate': _L0_cond2_in['spectral_gate'], 'L0_ffn_W_router': _L0_ffn_in['W_router'], 'L0_ffn_b_router': _L0_ffn_in['b_router'], 'L0_ffn_W1': _L0_ffn_in['W1'], 'L0_ffn_b1': _L0_ffn_in['b1'], 'L0_ffn_W2': _L0_ffn_in['W2'], 'L0_ffn_b2': _L0_ffn_in['b2'], 'L1_cond_rms_w': _L1_cond_in['rms_w'], 'L1_cond_wg_W': _L1_cond_in['wg_W'], 'L1_cond_wg_b': _L1_cond_in['wg_b'], 'L1_cond_gg_W': _L1_cond_in['gg_W'], 'L1_cond_gg_b': _L1_cond_in['gg_b'], 'L1_cond_W1': _L1_cond_in['W1'], 'L1_cond_b1': _L1_cond_in['b1'], 'L1_cond_W2': _L1_cond_in['W2'], 'L1_cond_b2': _L1_cond_in['b2'], 'L1_cond_W3': _L1_cond_in['W3'], 'L1_cond_b3': _L1_cond_in['b3'], 'L1_attn_Wq': _L1_attn_in['Wq'], 'L1_attn_Wk': _L1_attn_in['Wk'], 'L1_attn_Wv': _L1_attn_in['Wv'], 'L1_attn_Wg': _L1_attn_in['Wg'], 'L1_attn_bg': _L1_attn_in['bg'], 'L1_attn_Wdl': _L1_attn_in['Wdl'], 'L1_attn_Lparam': _L1_attn_in['Lparam'], 'L1_attn_Wo': _L1_attn_in['Wo'], 'L1_attn_ln_g': _L1_attn_in['ln_g'], 'L1_attn_ln_b': _L1_attn_in['ln_b'], 'L1_cond2_Wq': _L1_cond2_in['Wq'], 'L1_cond2_Wk': _L1_cond2_in['Wk'], 'L1_cond2_Wv': _L1_cond2_in['Wv'], 'L1_cond2_Wo': _L1_cond2_in['Wo'], 'L1_cond2_rms_scale': _L1_cond2_in['rms_scale'], 'L1_cond2_Wc': _L1_cond2_in['Wc'], 'L1_cond2_bc': _L1_cond2_in['bc'], 'L1_ffn_w1': _L1_ffn_in['w1'], 'L1_ffn_conv_w': _L1_ffn_in['conv_w'], 'L1_ffn_conv_b': _L1_ffn_in['conv_b'], 'L1_ffn_w2': _L1_ffn_in['w2']}

def reference(x, cond_256, mask_SxS_bk1, L0_cond_Wq, L0_cond_Wk, L0_cond_Wv, L0_cond_Wo, L0_cond_rms_scale, L0_cond_Wc, L0_cond_bc, L0_attn_w_q, L0_attn_w_kv, L0_attn_w_out, L0_cond2_q_right, L0_cond2_spectral_gate, L0_ffn_W_router, L0_ffn_b_router, L0_ffn_W1, L0_ffn_b1, L0_ffn_W2, L0_ffn_b2, L1_cond_rms_w, L1_cond_wg_W, L1_cond_wg_b, L1_cond_gg_W, L1_cond_gg_b, L1_cond_W1, L1_cond_b1, L1_cond_W2, L1_cond_b2, L1_cond_W3, L1_cond_b3, L1_attn_Wq, L1_attn_Wk, L1_attn_Wv, L1_attn_Wg, L1_attn_bg, L1_attn_Wdl, L1_attn_Lparam, L1_attn_Wo, L1_attn_ln_g, L1_attn_ln_b, L1_cond2_Wq, L1_cond2_Wk, L1_cond2_Wv, L1_cond2_Wo, L1_cond2_rms_scale, L1_cond2_Wc, L1_cond2_bc, L1_ffn_w1, L1_ffn_conv_w, L1_ffn_conv_b, L1_ffn_w2):
    import jax
    import jax.numpy as jnp

    def _L0_cond_ref(x, mask, conditioning, Wq, Wk, Wv, Wo, rms_scale, Wc, bc):
        import jax, jax.numpy as jnp
        import numpy as np
        EPS = 1e-06
        B, S, E = x.shape
        H = 16
        D = E // H
        scale = D ** (-0.5)

        def proj(W):
            return (x @ W.T).reshape(B, S, H, D).transpose(0, 2, 1, 3)
        q, k, v = (proj(Wq), proj(Wk), proj(Wv))
        scores = jnp.einsum('bhsd,bhtd->bhst', q, k) * scale
        scores = jnp.where(mask[None, None, :, :], -jnp.inf, scores)
        attn = jax.nn.softmax(scores, axis=-1)
        out = jnp.einsum('bhst,bhtd->bhsd', attn, v)
        out = out.transpose(0, 2, 1, 3).reshape(B, S, E)
        out = out @ Wo.T
        rms = jnp.sqrt(jnp.mean(out * out, axis=-1, keepdims=True) + EPS)
        xn = out / rms * rms_scale
        mod = jax.nn.silu(conditioning) @ Wc.T + bc
        shift, sc = jnp.split(mod, 2, axis=-1)
        xn = xn * (1.0 + sc[:, None, :]) + shift[:, None, :]
        return xn

    def _L0_attn_ref(x, w_q, w_kv, w_out):
        import jax, jax.numpy as jnp
        import numpy as np
        DIM = 128
        HEADS = 16
        HEAD_DIM = 64
        ROT = 32
        BASE = 10000.0
        SEQ = 256
        BATCH = 2

        def _rotate_half(t):
            x1, x2 = (t[..., :ROT // 2], t[..., ROT // 2:])
            return jnp.concatenate([-x2, x1], axis=-1)

        def _apply_rope(t, cos, sin):
            t_rot, t_pass = (t[..., :ROT], t[..., ROT:])
            t_rot = t_rot * cos + _rotate_half(t_rot) * sin
            return jnp.concatenate([t_rot, t_pass], axis=-1)
        b, n, _ = x.shape
        q = (x @ w_q).reshape(b, n, HEADS, HEAD_DIM).transpose(0, 2, 1, 3)
        k, v = jnp.split(x @ w_kv, 2, axis=-1)
        k = k.reshape(b, n, HEADS, HEAD_DIM).transpose(0, 2, 1, 3)
        v = v.reshape(b, n, HEADS, HEAD_DIM).transpose(0, 2, 1, 3)
        inv_freq = 1.0 / BASE ** (jnp.arange(0, ROT, 2, dtype=jnp.float32) / ROT)
        freqs = jnp.arange(n, dtype=jnp.float32)[:, None] * inv_freq[None, :]
        freqs = jnp.concatenate([freqs, freqs], axis=-1)
        cos, sin = (jnp.cos(freqs), jnp.sin(freqs))
        q = _apply_rope(q, cos, sin)
        k = _apply_rope(k, cos, sin)
        scale = HEAD_DIM ** (-0.5)
        scores = jnp.einsum('bhid,bhjd->bhij', q, k) * scale
        causal_mask = jnp.tril(jnp.ones((n, n), dtype=bool))
        scores = jnp.where(causal_mask, scores, jnp.finfo(scores.dtype).min)
        attn = jax.nn.softmax(scores, axis=-1)
        out = jnp.einsum('bhij,bhjd->bhid', attn, v)
        out = out.transpose(0, 2, 1, 3).reshape(b, n, HEADS * HEAD_DIM)
        return out @ w_out

    def _L0_cond2_ref(x, q_left, q_right, spectral_gate):
        import jax, jax.numpy as jnp
        import numpy as np
        EPS = 1e-08

        def hamilton(q1, q2):
            w1, x1, y1, z1 = (q1[..., i, :] for i in range(4))
            w2, x2, y2, z2 = (q2[..., i, :] for i in range(4))
            w = w1 * w2 - x1 * x2 - y1 * y2 - z1 * z2
            x = w1 * x2 + x1 * w2 + y1 * z2 - z1 * y2
            y = w1 * y2 - x1 * z2 + y1 * w2 + z1 * x2
            z = w1 * z2 + x1 * y2 - y1 * x2 + z1 * w2
            return jnp.stack([w, x, y, z], axis=-2)

        def _normalize(q):
            return q / jnp.sqrt(jnp.sum(q * q, axis=0, keepdims=True) + EPS)
        B, T, d_model = x.shape
        quat_dim = d_model // 4
        x_quat = x.reshape(B, T, 4, quat_dim)
        x_spectral = jnp.fft.fft(x_quat, axis=1)
        x_filtered = jnp.fft.ifft(x_spectral * spectral_gate, axis=1).real.astype(x.dtype)
        q_left_n = _normalize(q_left)
        q_right_n = _normalize(q_right)
        conj_sign = jnp.array([1.0, -1.0, -1.0, -1.0], dtype=x.dtype)[:, None]
        q_right_conj = q_right_n * conj_sign
        x_right = hamilton(x_filtered, q_right_conj)
        x_rotated = hamilton(q_left_n, x_right)
        return x_rotated.reshape(B, T, d_model)

    def _L0_ffn_ref(x, W_router, b_router, W1, b1, W2, b2):
        import jax, jax.numpy as jnp
        import numpy as np
        N_EMBD = 128
        NUM_EXPERTS = 8
        TOP_K = 2
        D_FF = 4 * N_EMBD
        B, S = (4, 256)
        Bv, Sv, D = x.shape
        flat_x = x.reshape(-1, D)
        T = flat_x.shape[0]
        logits = flat_x @ W_router + b_router
        top_vals, top_idx = jax.lax.top_k(logits, TOP_K)
        neg_inf = jnp.full_like(logits, -jnp.inf)
        sparse_logits = neg_inf.at[jnp.arange(T)[:, None], top_idx].set(top_vals)
        router_weights = jax.nn.softmax(sparse_logits, axis=-1)
        final_output = jnp.zeros_like(flat_x)
        for e in range(NUM_EXPERTS):
            expert_mask = jnp.any(top_idx == e, axis=-1)
            h = jax.nn.relu(flat_x @ W1[e] + b1[e])
            y = h @ W2[e] + b2[e]
            w = router_weights[:, e] * expert_mask.astype(x.dtype)
            final_output = final_output + y * w[:, None]
        return final_output.reshape(Bv, Sv, D)

    def _L1_cond_ref(x, genre_embed, rms_w, wg_W, wg_b, gg_W, gg_b, W1, b1, W2, b2, W3, b3):
        import jax, jax.numpy as jnp
        import numpy as np
        TOP_K = 2
        EPS = 1e-06
        E = W1.shape[0]
        var = jnp.mean(x * x, axis=-1, keepdims=True)
        xn = rms_w * (x * jax.lax.rsqrt(var + EPS))
        gate = xn @ wg_W + wg_b + (genre_embed @ gg_W + gg_b)
        gate_w = jax.nn.softmax(gate, axis=-1)
        topk_w, topk_i = jax.lax.top_k(gate_w, TOP_K)
        cw = jnp.sum(jax.nn.one_hot(topk_i, E, dtype=x.dtype) * topk_w[..., None], axis=-2)
        h1 = jax.nn.relu(jnp.einsum('bsh,ehm->bsem', x, W1) + b1)
        h2 = jax.nn.relu(jnp.einsum('bsem,emn->bsen', h1, W2) + b2)
        out_e = jnp.einsum('bsen,enh->bseh', h2, W3) + b3
        return jnp.einsum('bseh,bse->bsh', out_e, cw)

    def _L1_attn_ref(x, Wq, Wk, Wv, Wg, bg, Wdl, Lparam, Wo, ln_g, ln_b):
        import jax, jax.numpy as jnp
        import numpy as np
        D_MODEL = 128
        H = 8
        S = 128
        HD = 128
        LV = 12
        B = 2
        T = 256

        def _level_structure(t, num_levels):
            idx = np.arange(t)
            d = idx[:, None] - idx[None, :]
            lvl = np.where(d <= 0, 0, np.floor(np.log2(np.maximum(d, 1))).astype(np.int64) + 1)
            lvl = np.minimum(lvl, num_levels - 1)
            mask = d >= 0
            return (jnp.asarray(lvl), jnp.asarray(mask))
        b, t, _ = x.shape
        q = (x @ Wq.T).reshape(b, t, H, S)
        k = (x @ Wk.T).reshape(b, t, H, S)
        v = (x @ Wv.T).reshape(b, t, H, HD)
        g = -jax.nn.softplus(x @ Wg.T + bg)
        dl = (x @ Wdl.T).reshape(b, t, H, LV)
        lam = jax.nn.softplus(dl + Lparam[None, None])
        G = jnp.cumsum(g, axis=1)
        lvl, mask = _level_structure(t, LV)
        scale = 1.0 / np.sqrt(S)
        scores = jnp.einsum('bthd,bshd->bhts', q, k) * scale
        Gh = G.transpose(0, 2, 1)
        logdecay = Gh[:, :, :, None] - Gh[:, :, None, :]
        logdecay = jnp.where(mask[None, None], logdecay, -jnp.inf)
        decay = jnp.exp(logdecay)
        lvl_oh = jax.nn.one_hot(lvl, LV, dtype=x.dtype)
        lamw = jnp.einsum('bthl,tsl->bhts', lam, lvl_oh)
        A = scores * decay * lamw
        y = jnp.einsum('bhts,bshd->bthd', A, v).reshape(b, t, H * HD)
        out = y @ Wo.T + x
        mu = out.mean(-1, keepdims=True)
        var = out.var(-1, keepdims=True)
        return (out - mu) * jax.lax.rsqrt(var + 1e-05) * ln_g + ln_b

    def _L1_cond2_ref(x, mask, conditioning, Wq, Wk, Wv, Wo, rms_scale, Wc, bc):
        import jax, jax.numpy as jnp
        import numpy as np
        EPS = 1e-06
        B, S, E = x.shape
        H = 16
        D = E // H
        scale = D ** (-0.5)

        def proj(W):
            return (x @ W.T).reshape(B, S, H, D).transpose(0, 2, 1, 3)
        q, k, v = (proj(Wq), proj(Wk), proj(Wv))
        scores = jnp.einsum('bhsd,bhtd->bhst', q, k) * scale
        scores = jnp.where(mask[None, None, :, :], -jnp.inf, scores)
        attn = jax.nn.softmax(scores, axis=-1)
        out = jnp.einsum('bhst,bhtd->bhsd', attn, v)
        out = out.transpose(0, 2, 1, 3).reshape(B, S, E)
        out = out @ Wo.T
        rms = jnp.sqrt(jnp.mean(out * out, axis=-1, keepdims=True) + EPS)
        xn = out / rms * rms_scale
        mod = jax.nn.silu(conditioning) @ Wc.T + bc
        shift, sc = jnp.split(mod, 2, axis=-1)
        xn = xn * (1.0 + sc[:, None, :]) + shift[:, None, :]
        return xn

    def _L1_ffn_ref(x, w1, conv_w, conv_b, w2):
        import jax, jax.numpy as jnp
        import numpy as np
        B, S, D_MODEL, D_HIDDEN = (4, 256, 128, 512)

        def act_quant(x):
            scale = 127.0 / jnp.clip(jnp.max(jnp.abs(x), axis=-1, keepdims=True), 1e-05)
            return jnp.clip(jnp.round(x * scale), -128, 127) / scale

        def weight_quant(w):
            scale = 1.0 / jnp.clip(jnp.mean(jnp.abs(w)), 1e-05)
            return jnp.clip(jnp.round(w * scale), -1, 1) / scale

        def bit_linear(x, w):
            xq = x + jax.lax.stop_gradient(act_quant(x) - x)
            wq = w + jax.lax.stop_gradient(weight_quant(w) - w)
            return jnp.einsum('bsd,hd->bsh', xq, wq)

        def depthwise_conv1d(x_bcl, w, b):
            y = jax.lax.conv_general_dilated(x_bcl, w, window_strides=(1,), padding=[(1, 1)], dimension_numbers=('NCH', 'OIH', 'NCH'), feature_group_count=x_bcl.shape[1])
            return y + b[None, :, None]
        h = bit_linear(x, w1)
        h = depthwise_conv1d(h.transpose(0, 2, 1), conv_w, conv_b)
        h = h.transpose(0, 2, 1)
        h = jax.nn.silu(h)
        return bit_linear(h, w2)
    x = x + _L0_attn_ref(_L0_cond_ref(x, mask_SxS_bk1, cond_256, L0_cond_Wq, L0_cond_Wk, L0_cond_Wv, L0_cond_Wo, L0_cond_rms_scale, L0_cond_Wc, L0_cond_bc), L0_attn_w_q, L0_attn_w_kv, L0_attn_w_out)
    x = x + _L0_ffn_ref(_L0_cond2_ref(x, cond_256, L0_cond2_q_right, L0_cond2_spectral_gate), L0_ffn_W_router, L0_ffn_b_router, L0_ffn_W1, L0_ffn_b1, L0_ffn_W2, L0_ffn_b2)
    x = x + _L1_attn_ref(_L1_cond_ref(x, cond_256[:, None, :], L1_cond_rms_w, L1_cond_wg_W, L1_cond_wg_b, L1_cond_gg_W, L1_cond_gg_b, L1_cond_W1, L1_cond_b1, L1_cond_W2, L1_cond_b2, L1_cond_W3, L1_cond_b3), L1_attn_Wq, L1_attn_Wk, L1_attn_Wv, L1_attn_Wg, L1_attn_bg, L1_attn_Wdl, L1_attn_Lparam, L1_attn_Wo, L1_attn_ln_g, L1_attn_ln_b)
    x = x + _L1_ffn_ref(_L1_cond2_ref(x, mask_SxS_bk1, cond_256, L1_cond2_Wq, L1_cond2_Wk, L1_cond2_Wv, L1_cond2_Wo, L1_cond2_rms_scale, L1_cond2_Wc, L1_cond2_bc), L1_ffn_w1, L1_ffn_conv_w, L1_ffn_conv_b, L1_ffn_w2)
    return x

_drawn_inputs = setup_inputs


def setup_inputs(seed=0):
    import zlib

    import numpy as np

    out = dict(_drawn_inputs(seed))
    spreads = {'L0_cond_rms_scale': (1.0, 0.2),
     'L0_ffn_b_router': (0.0, 0.1),
     'L0_ffn_b1': (0.0, 0.1),
     'L0_ffn_b2': (0.0, 0.1),
     'L1_cond_rms_w': (1.0, 0.2),
     'L1_cond_wg_b': (0.0, 0.1),
     'L1_cond_gg_b': (0.0, 0.1),
     'L1_cond_b1': (0.0, 0.1),
     'L1_cond_b2': (0.0, 0.1),
     'L1_cond_b3': (0.0, 0.1),
     'L1_attn_bg': (0.0, 0.8),
     'L1_attn_Lparam': (1.0, 0.6),
     'L1_attn_ln_g': (1.0, 0.2),
     'L1_attn_ln_b': (0.0, 0.1),
     'L1_cond2_rms_scale': (1.0, 0.6)}
    factors = {'L0_attn_w_q': 10.667,
     'L1_attn_Wg': 6.778,
     'L1_attn_Wdl': 3.683,
     'L1_cond2_Wc': 8.0,
     'L1_cond2_bc': 36.351}
    for name, (base, spread) in spreads.items():
        noise = np.random.default_rng([zlib.crc32(name.encode()), seed]).standard_normal(out[name].shape)
        drawn = base * np.exp(spread * noise) if base else spread * noise
        out[name] = jnp.asarray(drawn.astype(out[name].dtype))
    for name, factor in factors.items():
        out[name] = (out[name] * factor).astype(out[name].dtype)
    return out
```

```python
from contextlib import ExitStack

import numpy as np

import concourse.bass as bass
from concourse import mybir

F32 = mybir.dt.float32
BF16 = mybir.dt.bfloat16
I32 = mybir.dt.int32
U32 = mybir.dt.uint32
U8 = mybir.dt.uint8
ALU = mybir.AluOpType
ACT = mybir.ActivationFunctionType
X = mybir.AxisListType.X

P = 128
B, S, E = 32, 32, 128
C = 32
TOK = B * S
TILES = TOK // P
SEQ = P // S
BANK = 512
HALF = 4 * BANK
CH, CD = 16, 8
AH, AD, ROT = 16, 64, 32
LH, LD = 8, 128
LEVELS = (S - 1).bit_length() + 1
NSMALL = LH + LH * LEVELS
EXPERTS = 8
FF0 = 512
FF1 = 256
HID = 512
ROUND = 1.5 * 2.0 ** 23
QMAX = 127.0
MASKED = -3.0e38

CONST, _at = {}, 0
for _name, _width in (("ident", P), ("ones", P), ("upto", P), ("headmask", CH), ("causal", S),
                      ("cos", S), ("sin", S), ("negafter", S), ("diag4", S), ("sign_r", 4),
                      ("sign_l", 4), ("iota", EXPERTS)):
    CONST[_name] = (_at, _at + _width)
    _at += _width
NCONST = _at


def constants():
    p = np.arange(P)
    t, seq = p % S, p // S
    c = {}
    c["ident"] = np.eye(P)
    c["ones"] = np.ones((P, P))
    c["upto"] = (seq[:, None] == seq[None, :]) & (t[:, None] <= t[None, :])
    c["headmask"] = (p[:, None] // CD) == np.arange(CH)[None, :]
    c["causal"] = np.where(np.arange(S)[None, :] <= t[:, None], 0.0, MASKED)
    inv = (np.float32(1.0) / np.power(np.float32(10000.0),
                                      np.arange(0, ROT, 2, dtype=np.float32) / np.float32(ROT))).astype(np.float32)
    ang = np.arange(S, dtype=np.float32)[:, None] * inv[None, :]
    d = p % AD
    rot = d < ROT
    a = ang[:, d % (ROT // 2)].T.astype(np.float64)
    c["cos"] = np.where(rot[:, None], np.cos(a), 1.0)
    c["sin"] = np.where(rot[:, None], np.where(d[:, None] < ROT // 2, -np.sin(a), np.sin(a)), 0.0)
    c["negafter"] = -1.0 * (t[:, None] > np.arange(S)[None, :])
    c["diag4"] = t[:, None] == np.arange(S)[None, :]
    right = np.array([[1, 1, 1, 1], [-1, 1, -1, 1], [-1, 1, 1, -1], [-1, -1, 1, 1]], float)
    left = np.array([[1, 1, 1, 1], [-1, 1, 1, -1], [-1, -1, 1, 1], [-1, 1, -1, 1]], float)
    comp = np.arange(4)
    conj = np.where((comp[:, None] ^ comp[None, :]) == 0, 1.0, -1.0)
    c["sign_r"] = (right * conj)[p // S]
    c["sign_l"] = left[p // S]
    c["iota"] = np.broadcast_to(np.arange(EXPERTS), (P, EXPERTS))
    table = np.concatenate([np.asarray(c[n], np.float32) for n in CONST], axis=1)
    dist = t[:, None] - np.arange(S)[None, :]
    level = np.where(dist <= 0, 0, np.floor(np.log2(np.maximum(dist, 1))).astype(int) + 1)
    masks = np.stack([(level == n) & (dist >= 0) for n in range(LEVELS)], 1).astype(np.int32)
    return np.ascontiguousarray(table), np.ascontiguousarray(masks.reshape(P, LEVELS * S))


def build(nc, d):
    ctx = ExitStack()
    with ctx:
        def sb(name, shape, dt=F32):
            return ctx.enter_context(nc.sbuf_tensor(name, shape, dt))

        def sem(name):
            return ctx.enter_context(nc.semaphore(name))

        PS = ctx.enter_context(nc.psum_tensor("PS", [P, 2 * HALF], F32))

        def bank(slot, n, lo=0, hi=BANK):
            return PS[:, slot * HALF + n * BANK + lo:slot * HALF + n * BANK + hi]

        const = sb("const", [P, NCONST])
        k = {n: const[:, lo:hi] for n, (lo, hi) in CONST.items()}
        levelmask = sb("levelmask", [P, LEVELS, S], I32)
        xres = sb("xres", [P, TILES, E])
        featT = sb("featT", [P, TOK])
        acc = sb("acc", [P, TILES, E])
        cond_w = [sb(f"cond_w{n}", [P, 4 * E]) for n in range(2)]
        mod_w = [sb(f"mod_w{n}", [C, 2 * E]) for n in range(2)]
        mod_b = [sb(f"mod_b{n}", [P, 2]) for n in range(2)]
        rms_s = [sb(f"rms_s{n}", [P, 1]) for n in range(2)]
        gain = [sb(f"gain{n}", [P, B]) for n in range(2)]
        shift = [sb(f"shift{n}", [P, B]) for n in range(2)]
        condT = sb("condT", [C, B])
        silu = sb("silu", [C, B])
        condx = sb("condx", [C, B, S])
        mask = sb("mask", [P, S // 4], I32)
        maskb = sb("maskb", [P, S])
        wqk = sb("wqk", [P, 2 * AH * AD])
        wv = sb("wv", [P, AH * AD])
        wout = sb("wout", [P, AH * AD // P, E])
        small_w = sb("small_w", [P, NSMALL])
        small_b = sb("small_b", [P, NSMALL])
        ln = sb("ln", [P, 2, E])
        quat = sb("quat", [P, 4])
        quat_all = sb("quat_all", [P, B])
        quat_l = sb("quat_l", [P, 4])
        sgate = sb("sgate", [P, 1])
        rot_r = sb("rot_r", [P, 4, S])
        rot_l = sb("rot_l", [P, 4, S])
        router_w = [sb(f"router_w{n}", [P, EXPERTS]) for n in range(2)]
        router_b = [sb(f"router_b{n}", [P, EXPERTS]) for n in range(2)]
        genre_w = sb("genre_w", [C, EXPERTS])
        genre_b = sb("genre_b", [P, EXPERTS])
        rms1 = sb("rms1", [P, 1])
        genre = sb("genre", [P, TILES, EXPERTS])
        ffn_w = [sb(f"ffn_w{n}", [P, HID]) for n in range(2)]
        ffn_q = [sb(f"ffn_q{n}", [P, HID], BF16) for n in range(2)]
        ffn_t = sb("ffn_t", [P, 2, HID])
        conv = sb("conv", [P, HID // P, 4])
        wsum = sb("wsum", [P, 2])
        wmean = sb("wmean", [P, 2])
        wscale = sb("wscale", [P, 2])
        last_b = [sb(f"last_b{n}", [EXPERTS, E]) for n in range(2)]
        scratch = sb("scratch", [P, 8])
        eps = sb("eps", [P, 3])
        holder = sb("holder", [P, 1])
        ident_b = sb("ident_b", [P, P], BF16)

        loaded = {n: sem(f"loaded_{n}") for n in
                  ("x", "const", "cond", "quat", "attn", "router", "ffn", "wattn1")}
        prep = sem("prep_step")
        prep_act = sem("prep_act_step")
        prep_pe = sem("prep_pe_step")

        with nc.Block() as block:
            @block.sync
            def _(sp):
                sp.dma_start(xres[:], d["x"].rearrange("(n p) e -> p n e", p=P)).then_inc(loaded["x"], 16)
                sp.dma_start(const[:], d["const"]).then_inc(loaded["const"], 16)
                sp.dma_start(levelmask[:], d["levelmask"].rearrange("p (l s) -> p l s", l=LEVELS)).then_inc(loaded["const"], 16)
                for n in range(2):
                    sp.dma_start(cond_w[n][:], d[f"cond_w{n}"]).then_inc(loaded["cond"], 16)
                    sp.dma_start(mod_w[n][:], d[f"mod_w{n}"]).then_inc(loaded["cond"], 16)
                    sp.dma_start(mod_b[n][:], d[f"mod_b{n}"]).then_inc(loaded["cond"], 16)
                    sp.dma_start(rms_s[n][:], d[f"rms_s{n}"]).then_inc(loaded["cond"], 16)
                sp.dma_start(condT[:], d["condT"]).then_inc(loaded["cond"], 16)
                sp.dma_start(mask[:], d["mask"]).then_inc(loaded["cond"], 16)
                sp.dma_start(wqk[:], d["attn0_qk"]).then_inc(loaded["attn"], 16)
                sp.dma_start(wv[:], d["attn0_v"]).then_inc(loaded["attn"], 16)
                sp.dma_start(wout[:], d["attn0_out"].rearrange("(c p) e -> p c e", p=P)).then_inc(loaded["attn"], 16)

            @block.scalar
            def _(act):
                act.dma_start(quat[:], d["quat"]).then_inc(loaded["quat"], 16)
                act.dma_start(quat_all[:], d["quat_all"]).then_inc(loaded["quat"], 16)
                act.dma_start(quat_l[:], d["quat_l"]).then_inc(loaded["quat"], 16)
                act.dma_start(sgate[:], d["sgate"]).then_inc(loaded["quat"], 16)
                for n in range(2):
                    act.dma_start(router_w[n][:], d[f"router_w{n}"]).then_inc(loaded["router"], 16)
                    act.dma_start(router_b[n][:], d[f"router_b{n}"]).then_inc(loaded["router"], 16)
                act.dma_start(genre_w[:], d["genre_w"]).then_inc(loaded["router"], 16)
                act.dma_start(genre_b[:], d["genre_b"]).then_inc(loaded["router"], 16)
                act.dma_start(rms1[:], d["rms1"]).then_inc(loaded["router"], 16)
                for n in range(2):
                    act.dma_start(ffn_w[n][:], d[f"ffn_w{n}"]).then_inc(loaded["ffn"], 16)
                act.dma_start(conv[:], d["conv"].rearrange("p (c k) -> p c k", k=4)).then_inc(loaded["ffn"], 16)
                for n in range(2):
                    act.dma_start(last_b[n][:], d[f"moe{n}_last_b"]).then_inc(loaded["router"], 16)
                act.dma_start(small_w[:], d["small_w"]).then_inc(loaded["router"], 16)
                act.dma_start(small_b[:], d["small_b"]).then_inc(loaded["router"], 16)
                act.dma_start(ln[:], d["ln"].rearrange("p (a e) -> p a e", a=2)).then_inc(loaded["router"], 16)
                act.wait_ge(prep, 3)
                act.activation(scratch[:, 2:4], scratch[:, 0:2], ACT.Ln, bias=eps[:, 1:2]).then_inc(prep_act, 1)
                act.wait_ge(prep_act, 1)
                act.activation(scratch[:, 4:6], scratch[:, 2:4], ACT.Exp, scale=-0.5).then_inc(prep_act, 1)
                act.wait_ge(loaded["cond"], 16 * 10)
                act.activation(silu[:], condT[:], ACT.Exp, scale=-1.0).then_inc(prep_act, 1)

            @block.vector
            def _(dve):
                n = 0
                nc.vector.memset(eps[:, 0:1], 1e-6)
                nc.vector.memset(eps[:, 2:3], 1e-5)
                nc.vector.memset(eps[:, 1:2], 1e-8).then_inc(prep, 1)
                dve.wait_ge(loaded["quat"], 64)
                dve.wait_ge(loaded["const"], 32)
                nc.vector.tensor_tensor_reduce(out=rot_r[:, 0, 0:4], in0=quat[:], in1=quat[:], scale=1.0, scalar=0.0,
                                               op0=ALU.mult, op1=ALU.add, accum_out=scratch[:, 0:1]).then_inc(prep, 1)
                nc.vector.tensor_tensor_reduce(out=rot_l[:, 0, :], in0=quat_all[:], in1=quat_all[:], scale=1.0, scalar=0.0,
                                               op0=ALU.mult, op1=ALU.add, accum_out=scratch[:, 1:2]).then_inc(prep, 1)
                dve.wait_ge(prep_act, 2)
                nc.vector.scalar_tensor_tensor(out=quat[:], in0=quat[:], scalar=scratch[:, 4:5], in1=k["sign_r"],
                                               op0=ALU.mult, op1=ALU.mult).then_inc(prep, 1)
                nc.vector.scalar_tensor_tensor(out=quat_l[:], in0=quat_l[:], scalar=scratch[:, 5:6], in1=k["sign_l"],
                                               op0=ALU.mult, op1=ALU.mult).then_inc(prep, 1)
                dve.wait_ge(prep, 5)
                nc.vector.tensor_scalar(quat[:], quat[:], sgate[:, 0:1], None, ALU.mult).then_inc(prep, 1)
                dve.wait_ge(prep, 6)
                for q, r in ((quat, rot_r), (quat_l, rot_l)):
                    nc.vector.tensor_tensor(r[:], k["diag4"].unsqueeze(1).to_broadcast([P, 4, S]),
                                            q[:].unsqueeze(2).to_broadcast([P, 4, S]), ALU.mult).then_inc(prep, 1)
                dve.wait_ge(loaded["cond"], 16 * 10)
                nc.vector.tensor_scalar(maskb[:], mask[:].bitcast(U8), MASKED, None, ALU.mult).then_inc(prep, 1)
                dve.wait_ge(prep_act, 3)
                nc.vector.tensor_scalar(silu[:], silu[:], 1.0, None, ALU.add).then_inc(prep, 1)
                dve.wait_ge(prep, 10)
                nc.vector.reciprocal(silu[:], silu[:]).then_inc(prep, 1)
                dve.wait_ge(prep, 11)
                nc.vector.tensor_tensor(silu[:], silu[:], condT[:], ALU.mult).then_inc(prep, 1)
                nc.vector.tensor_copy(condx[:], condT[:].unsqueeze(2).to_broadcast([C, B, S])).then_inc(prep, 1)
                dve.wait_ge(loaded["router"], 16 * 12)
                nc.vector.tensor_scalar(router_w[1][:], router_w[1][:], rms1[:, 0:1], None, ALU.mult).then_inc(prep, 1)
                nc.vector.tensor_tensor(genre_b[:], genre_b[:], router_b[1][:], ALU.add).then_inc(prep, 1)
                dve.wait_ge(loaded["ffn"], 48)
                for n in range(2):
                    nc.vector.tensor_reduce(wsum[:, n:n + 1], ffn_w[n][:], X, ALU.add, apply_absolute_value=True).then_inc(prep, 1)
                dve.wait_ge(prep_pe, 1)
                for n in range(2):
                    nc.vector.tensor_scalar(shift[n][:], bank(0, 0, 64 * n, 64 * n + 32), mod_b[n][:, 0:1], None, ALU.add).then_inc(prep, 1)
                    nc.vector.tensor_scalar(gain[n][:], bank(0, 0, 64 * n + 32, 64 * n + 64), mod_b[n][:, 1:2], 1.0, ALU.add, ALU.add).then_inc(prep, 1)
                dve.wait_ge(prep, 21)
                for n in range(2):
                    nc.vector.tensor_scalar(gain[n][:], gain[n][:], rms_s[n][:, 0:1], None, ALU.mult).then_inc(prep, 1)
                nc.vector.tensor_tensor(genre[:], bank(0, 1, 0, 64).rearrange("p (n e) -> p n e", e=EXPERTS),
                                        genre_b[:].unsqueeze(1).to_broadcast([P, TILES, EXPERTS]), ALU.add).then_inc(prep, 1)
                nc.vector.tensor_scalar(wmean[:], bank(0, 1, 64, 66), 1.0 / (E * HID), 1e-5, ALU.mult, ALU.max).then_inc(prep, 1)
                dve.wait_ge(prep, 25)
                nc.vector.reciprocal(wscale[:], wmean[:]).then_inc(prep, 1)
                dve.wait_ge(prep, 26)
                nc.vector.tensor_copy(ident_b[:], k["ident"])
                for n in range(2):
                    nc.vector.tensor_scalar(ffn_t[:, n, :], ffn_w[n][:], wscale[:, n:n + 1], ROUND, ALU.mult, ALU.add).then_inc(prep, 1)
                dve.wait_ge(prep, 28)
                for n in range(2):
                    nc.vector.tensor_scalar(ffn_t[:, n, :], ffn_t[:, n, :], ROUND, 1.0, ALU.subtract, ALU.min).then_inc(prep, 1)
                dve.wait_ge(prep, 30)
                for n in range(2):
                    nc.vector.tensor_scalar(ffn_q[n][:], ffn_t[:, n, :], -1.0, None, ALU.max).then_inc(prep, 1)

            @block.tensor
            def _(pe):
                pe.wait_ge(prep, 15)
                pe.wait_ge(loaded["router"], 16 * 12)
                for n in range(2):
                    nc.tensor.matmul(bank(0, 0, 64 * n, 64 * n + 32), mod_w[n][:, 0:E], silu[:], start=True, stop=True)
                    nc.tensor.matmul(bank(0, 0, 64 * n + 32, 64 * n + 64), mod_w[n][:, E:2 * E], silu[:], start=True, stop=True)
                for n in range(TILES):
                    nc.tensor.matmul(bank(0, 1, 8 * n, 8 * n + 8), condx[:, SEQ * n:SEQ * n + SEQ, :], genre_w[:], start=True, stop=True)
                pe.wait_ge(prep, 17)
                nc.tensor.matmul(bank(0, 1, 64, 66), k["ones"], wsum[:], start=True, stop=True).then_inc(prep_pe, 1)

        cond_sems = {}

        def conditioning(layer):
            pre = f"cond{layer}_"
            with ExitStack() as own:
                def lsb(name, shape, dt=F32):
                    return [own.enter_context(nc.sbuf_tensor(f"{pre}{name}{s}", shape, dt)) for s in range(2)]

                def lsem(name):
                    if name not in cond_sems:
                        cond_sems[name] = sem("cond_" + name)
                    return cond_sems[name]

                xst, xs = lsb("xst", [P, E]), lsb("xs", [P, P])
                qkv = lsb("qkv", [P, 3 * P])
                kbd = lsb("kbd", [P, CH, P])
                sm, pr = lsb("sm", [P, CH, S]), lsb("pr", [P, CH, S])
                ptbd = lsb("ptbd", [P, CH, P])
                mx, sums, rec = lsb("mx", [P, CH]), lsb("sums", [P, CH]), lsb("rec", [P, CH])
                o, oT, zn, c1 = lsb("o", [P, E]), lsb("oT", [P, P]), lsb("zn", [P, E]), lsb("c1", [P, P])
                st = lsb("st", [P, 4])
                tile_free = lsem("tile_free")
                x_staged, xT_ps, xT_ready = lsem("x_staged"), lsem("xT_ps"), lsem("xT_ready")
                qkv_ps, qkv_ready, kbd_ready = lsem("qkv_ps"), lsem("qkv_ready"), lsem("kbd_ready")
                scores_ps, scores_ready, probs_ready = lsem("scores_ps"), lsem("scores_ready"), lsem("probs_ready")
                probsT_ready, o_ps, o_ready = lsem("probsT_ready"), lsem("o_ps"), lsem("o_ready")
                oT_ps, oT_ready, z_ps = lsem("oT_ps"), lsem("oT_ready"), lsem("z_ps")
                rstd_ready, zn_ready, znT_ps = lsem("rstd_ready"), lsem("zn_ready"), lsem("znT_ps")
                dve_step, act_step, zeroed = lsem("dve_step"), lsem("act_step"), lsem("zeroed")
                DVE_STEPS, ACT_STEPS = 2 * 10, 2 * 2
                scale = float(CD) ** -0.5
                first = layer * (TILES // 2)
                before = layer * TILES

                with nc.Block() as block:
                    @block.sync
                    def _(sp):
                        if layer == 0:
                            sp.sem_inc(tile_free, 2)

                    @block.gpsimd
                    def _(pool):
                        for s in range(2):
                            nc.gpsimd.memset(ptbd[s][:], 0.0).then_inc(zeroed, 1)
                        with pool.Fori(first, first + TILES // 2) as i:
                            for s in range(2):
                                pool.wait_ge(tile_free, 2 * i + s + 1)
                                nc.gpsimd.tensor_copy(xst[s][:], xres[:, bass.ds(2 * i + s - before, 1), :].rearrange("p a e -> p (a e)")).then_inc(x_staged, 1)
                            for s in range(2):
                                pool.wait_ge(qkv_ready, 2 * i + s + 1)
                                nc.gpsimd.tensor_tensor(kbd[s][:], qkv[s][:, P:2 * P].unsqueeze(1).to_broadcast([P, CH, P]),
                                                        k["headmask"].unsqueeze(2).to_broadcast([P, CH, P]), ALU.mult).then_inc(kbd_ready, 1)

                    @block.tensor
                    def _(pe):
                        w = cond_w[layer]
                        with pe.Fori(first, first + TILES // 2) as i:
                            for s in range(2):
                                pe.wait_ge(x_staged, 2 * i + s + 1)
                                nc.tensor.transpose(bank(s, 0, 0, P), xst[s][:], k["ident"]).then_inc(xT_ps, 1)
                            for s in range(2):
                                pe.wait_ge(xT_ready, 2 * i + s + 1)
                                nc.tensor.matmul(bank(s, 1, 0, P), w[:, 0:E], xs[s][:], start=True, stop=True)
                                nc.tensor.matmul(bank(s, 1, P, 2 * P), w[:, E:2 * E], xs[s][:], start=True, stop=True)
                                nc.tensor.matmul(bank(s, 1, 2 * P, 3 * P), xs[s][:], w[:, 2 * E:3 * E], start=True, stop=True).then_inc(qkv_ps, 1)
                            for s in range(2):
                                pe.wait_ge(kbd_ready, 2 * i + s + 1)
                                for b in range(SEQ):
                                    mm = nc.tensor.matmul(bank(s, 2)[S * b:S * b + S, :], qkv[s][:, S * b:S * b + S],
                                                          kbd[s][:, :, S * b:S * b + S], start=True, stop=True)
                                mm.then_inc(scores_ps, 1)
                            for s in range(2):
                                pe.wait_ge(probsT_ready, 2 * i + s + 1)
                                for h in range(CH):
                                    mm = nc.tensor.matmul(bank(s, 3, CD * h, CD * h + CD), ptbd[s][:, h, :],
                                                          qkv[s][:, 2 * P + CD * h:2 * P + CD * h + CD], start=True, stop=True)
                                mm.then_inc(o_ps, 1)
                            for s in range(2):
                                pe.wait_ge(o_ready, 2 * i + s + 1)
                                nc.tensor.transpose(bank(s, 3, P, 2 * P), o[s][:], k["ident"]).then_inc(oT_ps, 1)
                            for s in range(2):
                                pe.wait_ge(oT_ready, 2 * i + s + 1)
                                nc.tensor.matmul(bank(s, 0, P, 2 * P), oT[s][:], w[:, 3 * E:4 * E], start=True, stop=True).then_inc(z_ps, 1)
                            for s in range(2):
                                pe.wait_ge(zn_ready, 2 * i + s + 1)
                                nc.tensor.transpose(bank(s, 0, 2 * P, 3 * P), zn[s][:], k["ident"]).then_inc(znT_ps, 1)

                    @block.scalar
                    def _(act):
                        with act.Fori(first, first + TILES // 2) as i:
                            for s in range(2):
                                act.wait_ge(xT_ps, 2 * i + s + 1)
                                nc.scalar.activation(xs[s][:], bank(s, 0, 0, P), ACT.Copy).then_inc(xT_ready, 1)
                            for s in range(2):
                                act.wait_ge(qkv_ps, 2 * i + s + 1)
                                nc.scalar.activation(qkv[s][:], bank(s, 1, 0, 3 * P), ACT.Copy).then_inc(qkv_ready, 1)
                            for s in range(2):
                                act.wait_ge(scores_ready, 2 * i + s + 1)
                                nc.scalar.activation(pr[s][:], sm[s][:], ACT.Exp).then_inc(probs_ready, 1)
                            for s in range(2):
                                act.wait_ge(oT_ps, 2 * i + s + 1)
                                nc.scalar.activation(oT[s][:], bank(s, 3, P, 2 * P), ACT.Copy).then_inc(oT_ready, 1)
                            for s in range(2):
                                act.wait_ge(z_ps, 2 * i + s + 1)
                                nc.scalar.activation(zn[s][:], bank(s, 0, P, 2 * P), ACT.Square, accum_out=st[s][:, 0:1]).then_inc(act_step, 1)
                            for s in range(2):
                                act.wait_ge(act_step, ACT_STEPS * i + s + 1)
                                nc.scalar.activation(st[s][:, 1:2], st[s][:, 0:1], ACT.Ln, bias=eps[:, 0:1], scale=1.0 / E).then_inc(act_step, 1)
                            for s in range(2):
                                act.wait_ge(act_step, ACT_STEPS * i + 2 + s + 1)
                                nc.scalar.activation(st[s][:, 2:3], st[s][:, 1:2], ACT.Exp, scale=-0.5).then_inc(rstd_ready, 1)

                    @block.vector
                    def _(dve):
                        dve.wait_ge(zeroed, 2 * (layer + 1))
                        with dve.Fori(first, first + TILES // 2) as i:
                            for s in range(2):
                                dve.wait_ge(scores_ps, 2 * i + s + 1)
                                nc.vector.scalar_tensor_tensor(out=sm[s][:], in0=bank(s, 2).rearrange("p (h t) -> p h t", t=S), scalar=scale,
                                                               in1=maskb[:].unsqueeze(1).to_broadcast([P, CH, S]),
                                                               op0=ALU.mult, op1=ALU.add).then_inc(dve_step, 1)
                            for s in range(2):
                                dve.wait_ge(dve_step, DVE_STEPS * i + s + 1)
                                nc.vector.tensor_reduce(mx[s][:], sm[s][:], X, ALU.max).then_inc(dve_step, 1)
                            for s in range(2):
                                dve.wait_ge(dve_step, DVE_STEPS * i + 2 + s + 1)
                                nc.vector.tensor_tensor(sm[s][:], sm[s][:], mx[s][:].unsqueeze(2).to_broadcast([P, CH, S]), ALU.subtract).then_inc(scores_ready, 1)
                            for s in range(2):
                                dve.wait_ge(probs_ready, 2 * i + s + 1)
                                nc.vector.tensor_reduce(sums[s][:], pr[s][:], X, ALU.add).then_inc(dve_step, 1)
                                for b in range(SEQ):
                                    last = nc.vector.transpose(ptbd[s][S * b:S * b + S, :, S * b:S * b + S], pr[s][S * b:S * b + S, :, :])
                                last.then_inc(probsT_ready, 1)
                            for s in range(2):
                                dve.wait_ge(dve_step, DVE_STEPS * i + 4 + s + 1)
                                nc.vector.reciprocal(rec[s][:], sums[s][:]).then_inc(dve_step, 1)
                            for s in range(2):
                                dve.wait_ge(dve_step, DVE_STEPS * i + 6 + s + 1)
                                dve.wait_ge(o_ps, 2 * i + s + 1)
                                nc.vector.tensor_tensor(o[s][:].rearrange("p (h c) -> p h c", c=CD), bank(s, 3, 0, P).rearrange("p (h c) -> p h c", c=CD),
                                                        rec[s][:].unsqueeze(2).to_broadcast([P, CH, CD]), ALU.mult).then_inc(o_ready, 1)
                            for s in range(2):
                                dve.wait_ge(rstd_ready, 2 * i + s + 1)
                                nc.vector.tensor_scalar(zn[s][:], bank(s, 0, P, 2 * P), st[s][:, 2:3], None, ALU.mult).then_inc(zn_ready, 1)
                            for s in range(2):
                                dve.wait_ge(znT_ps, 2 * i + s + 1)
                                nc.vector.tensor_tensor(c1[s][:].rearrange("p (b t) -> p b t", t=S), bank(s, 0, 2 * P, 3 * P).rearrange("p (b t) -> p b t", t=S),
                                                        gain[layer][:, bass.ds(SEQ * (2 * i + s - before), SEQ)].unsqueeze(2).to_broadcast([P, SEQ, S]), ALU.mult).then_inc(dve_step, 1)
                            for s in range(2):
                                dve.wait_ge(dve_step, DVE_STEPS * i + 8 + s + 1)
                                nc.vector.tensor_tensor(featT[:, bass.ds(P * (2 * i + s - before), P)].rearrange("p (b t) -> p b t", t=S), c1[s][:].rearrange("p (b t) -> p b t", t=S),
                                                        shift[layer][:, bass.ds(SEQ * (2 * i + s - before), SEQ)].unsqueeze(2).to_broadcast([P, SEQ, S]), ALU.add).then_inc(tile_free, 1)
                            for s in range(2):
                                dve.wait_ge(tile_free, 2 + 2 * i + s + 1)
                            dve.sem_inc(dve_step, DVE_STEPS - 10)

        def rotary_attention():
            with ExitStack() as own:
                def lsb(name, shape, dt=F32):
                    return [own.enter_context(nc.sbuf_tensor(f"rot_{name}{s}", shape, dt)) for s in range(2)]

                def lsem(name):
                    return ctx.enter_context(nc.semaphore("rot_" + name))

                NC_ = AH * AD // P
                cs = lsb("cs", [P, P])
                qk = lsb("qk", [P, 2 * NC_, P])
                sh, qc = lsb("sh", [P, 2 * NC_, P]), lsb("qc", [P, 2 * NC_, P])
                v = lsb("v", [P, AH * AD])
                sm = lsb("sm", [P, AH, S])
                ptbd = lsb("ptbd", [P, AH, P])
                oT = lsb("oT", [P, NC_, P])
                mx, sums, rec = lsb("mx", [P, AH]), lsb("sums", [P, AH]), lsb("rec", [P, AH])
                tile_free, zeroed = lsem("tile_free"), lsem("zeroed")
                c_staged, q_ps, k_ps, v_ps = lsem("c_staged"), lsem("q_ps"), lsem("k_ps"), lsem("v_ps")
                q_ready, k_ready, v_ready = lsem("q_ready"), lsem("k_ready"), lsem("v_ready")
                shuffled, sin_ready, qk_ready = lsem("shuffled"), lsem("sin_ready"), lsem("qk_ready")
                low_ps, high_ps, scores_ready = lsem("low_ps"), lsem("high_ps"), lsem("scores_ready")
                probs_ready, probsT_ready = lsem("probs_ready"), lsem("probsT_ready")
                oT_ps, oT_ready, out_ps = lsem("oT_ps"), lsem("oT_ready"), lsem("out_ps")
                dve_step = lsem("dve_step")
                DVE_STEPS = 2 * 6
                scale = float(AD) ** -0.5
                swap = [(n + ROT // 2) % ROT for n in range(ROT)]

                with nc.Block() as block:
                    @block.sync
                    def _(sp):
                        sp.sem_inc(tile_free, 2)

                    @block.gpsimd
                    def _(pool):
                        for s in range(2):
                            nc.gpsimd.memset(ptbd[s][:], 0.0).then_inc(zeroed, 1)
                        with pool.Fori(0, TILES // 2) as i:
                            for s in range(2):
                                pool.wait_ge(tile_free, 2 * i + s + 1)
                                nc.gpsimd.tensor_copy(cs[s][:], featT[:, bass.ds(P * (2 * i + s), P)]).then_inc(c_staged, 1)
                            for s in range(2):
                                pool.wait_ge(shuffled, 2 * i + s + 1)
                                nc.gpsimd.tensor_tensor(sh[s][:].rearrange("p c (b t) -> p (c b) t", t=S), sh[s][:].rearrange("p c (b t) -> p (c b) t", t=S),
                                                        k["sin"].unsqueeze(1).to_broadcast([P, 2 * NC_ * SEQ, S]), ALU.mult).then_inc(sin_ready, 1)

                    @block.tensor
                    def _(pe):
                        pe.wait_ge(loaded["attn"], 48)
                        with pe.Fori(0, TILES // 2) as i:
                            for s in range(2):
                                pe.wait_ge(c_staged, 2 * i + s + 1)
                                for c in range(NC_):
                                    mm = nc.tensor.matmul(bank(s, c // 4, P * (c % 4), P * (c % 4) + P), wqk[:, P * c:P * c + P], cs[s][:], start=True, stop=True)
                                mm.then_inc(q_ps, 1)
                                for c in range(NC_):
                                    mm = nc.tensor.matmul(bank(s, 2 + c // 4, P * (c % 4), P * (c % 4) + P), wqk[:, P * (NC_ + c):P * (NC_ + c) + P], cs[s][:], start=True, stop=True)
                                mm.then_inc(k_ps, 1)
                                pe.wait_ge(q_ready, 2 * i + s + 1)
                                for c in range(2):
                                    mm = nc.tensor.matmul(bank(s, c), cs[s][:], wv[:, BANK * c:BANK * c + BANK], start=True, stop=True)
                                mm.then_inc(v_ps, 1)
                            for s in range(2):
                                pe.wait_ge(qk_ready, 2 * i + s + 1)
                                pe.wait_ge(k_ready, 2 * i + s + 1)
                                pe.wait_ge(v_ready, 2 * i + s + 1)
                                for h in range(AH):
                                    r, c = AD * (h % 2), h // 2
                                    g = h // 8
                                    at = (2 if g == 0 else 0) + h % 2
                                    col = P * (c % 4)
                                    mm = nc.tensor.matmul(bank(s, at, col, col + P), qk[s][r:r + AD, c, :], qk[s][r:r + AD, NC_ + c, :], start=True, stop=True)
                                    if h == 7:
                                        mm.then_inc(low_ps, 1)
                                mm.then_inc(high_ps, 1)
                            for s in range(2):
                                pe.wait_ge(probsT_ready, 2 * i + s + 1)
                                for h in range(AH):
                                    r, c = AD * (h % 2), h // 2
                                    mm = nc.tensor.matmul(bank(s, 2 + c // 4, P * (c % 4), P * (c % 4) + P)[r:r + AD, :], v[s][:, AD * h:AD * h + AD], ptbd[s][:, h, :], start=True, stop=True)
                                mm.then_inc(oT_ps, 1)
                            for s in range(2):
                                pe.wait_ge(oT_ready, 2 * i + s + 1)
                                for c in range(NC_):
                                    mm = nc.tensor.matmul(bank(s, 0, 0, E), oT[s][:, c, :], wout[:, c, :], start=(c == 0), stop=(c == NC_ - 1))
                                mm.then_inc(out_ps, 1)

                    @block.scalar
                    def _(act):
                        with act.Fori(0, TILES // 2) as i:
                            for s in range(2):
                                act.wait_ge(q_ps, 2 * i + s + 1)
                                for c in range(2):
                                    ins = nc.scalar.activation(qk[s][:, 4 * c:4 * c + 4, :].rearrange("p c t -> p (c t)"), bank(s, c), ACT.Copy)
                                ins.then_inc(q_ready, 1)
                                act.wait_ge(k_ps, 2 * i + s + 1)
                                for c in range(2):
                                    ins = nc.scalar.activation(qk[s][:, NC_ + 4 * c:NC_ + 4 * c + 4, :].rearrange("p c t -> p (c t)"), bank(s, 2 + c), ACT.Copy)
                                ins.then_inc(k_ready, 1)
                                act.wait_ge(v_ps, 2 * i + s + 1)
                                for c in range(2):
                                    ins = nc.scalar.activation(v[s][:, BANK * c:BANK * c + BANK], bank(s, c), ACT.Copy)
                                ins.then_inc(v_ready, 1)
                            for s in range(2):
                                act.wait_ge(scores_ready, 2 * i + s + 1)
                                nc.scalar.activation(sm[s][:], sm[s][:], ACT.Exp).then_inc(probs_ready, 1)
                            for s in range(2):
                                act.wait_ge(oT_ps, 2 * i + s + 1)
                                for c in range(2):
                                    ins = nc.scalar.activation(oT[s][:, 4 * c:4 * c + 4, :].rearrange("p c t -> p (c t)"), bank(s, 2 + c), ACT.Copy)
                                ins.then_inc(oT_ready, 1)

                    @block.vector
                    def _(dve):
                        dve.wait_ge(zeroed, 2)
                        with dve.Fori(0, TILES // 2) as i:
                            for s in range(2):
                                dve.wait_ge(k_ready, 2 * i + s + 1)
                                nc.vector.tensor_tensor(qc[s][:].rearrange("p c (b t) -> p (c b) t", t=S), qk[s][:].rearrange("p c (b t) -> p (c b) t", t=S),
                                                        k["cos"].unsqueeze(1).to_broadcast([P, 2 * NC_ * SEQ, S]), ALU.mult).then_inc(dve_step, 1)
                                nc.vector.stream_shuffle(sh[s][:], qk[s][:], swap).then_inc(shuffled, 1)
                            for s in range(2):
                                dve.wait_ge(sin_ready, 2 * i + s + 1)
                                dve.wait_ge(dve_step, DVE_STEPS * i + s + 1)
                                nc.vector.tensor_tensor(qk[s][:], qc[s][:], sh[s][:], ALU.add).then_inc(qk_ready, 1)
                            for s in range(2):
                                for g in range(2):
                                    dve.wait_ge(low_ps if g == 0 else high_ps, 2 * i + s + 1)
                                    for odd in range(2):
                                        src = bank(s, (2 if g == 0 else 0) + odd)
                                        dst = sm[s][:, 8 * g:8 * g + 8, :].rearrange("p (c o) t -> p c o t", o=2)[:, :, odd, :]
                                        for b in range(SEQ):
                                            r = slice(S * b, S * b + S)
                                            ins = nc.vector.scalar_tensor_tensor(
                                                out=dst[r], in0=src[r].rearrange("p (c t) -> p c t", t=P)[:, :, S * b:S * b + S], scalar=scale,
                                                in1=k["causal"][r].unsqueeze(1).to_broadcast([S, 4, S]), op0=ALU.mult, op1=ALU.add)
                                ins.then_inc(dve_step, 1)
                            for s in range(2):
                                dve.wait_ge(dve_step, DVE_STEPS * i + 2 + s + 1)
                                nc.vector.tensor_reduce(mx[s][:], sm[s][:], X, ALU.max).then_inc(dve_step, 1)
                            for s in range(2):
                                dve.wait_ge(dve_step, DVE_STEPS * i + 4 + s + 1)
                                nc.vector.tensor_tensor(sm[s][:], sm[s][:], mx[s][:].unsqueeze(2).to_broadcast([P, AH, S]), ALU.subtract).then_inc(scores_ready, 1)
                            for s in range(2):
                                dve.wait_ge(probs_ready, 2 * i + s + 1)
                                nc.vector.tensor_reduce(sums[s][:], sm[s][:], X, ALU.add).then_inc(dve_step, 1)
                            for s in range(2):
                                dve.wait_ge(dve_step, DVE_STEPS * i + 6 + s + 1)
                                nc.vector.reciprocal(rec[s][:], sums[s][:]).then_inc(dve_step, 1)
                            for s in range(2):
                                dve.wait_ge(dve_step, DVE_STEPS * i + 8 + s + 1)
                                nc.vector.tensor_tensor(sm[s][:], sm[s][:], rec[s][:].unsqueeze(2).to_broadcast([P, AH, S]), ALU.mult).then_inc(dve_step, 1)
                            for s in range(2):
                                dve.wait_ge(dve_step, DVE_STEPS * i + 10 + s + 1)
                                for b in range(SEQ):
                                    last = nc.vector.transpose(ptbd[s][S * b:S * b + S, :, S * b:S * b + S], sm[s][S * b:S * b + S, :, :])
                                last.then_inc(probsT_ready, 1)
                            for s in range(2):
                                dve.wait_ge(out_ps, 2 * i + s + 1)
                                here = xres[:, bass.ds(2 * i + s, 1), :].rearrange("p a e -> p (a e)")
                                nc.vector.tensor_tensor(here, here, bank(s, 0, 0, E), ALU.add).then_inc(tile_free, 1)

        def experts(layer):
            pre = f"moe{layer}_"
            ff = (FF0, FF1)[layer]
            nf = ff // P
            with ExitStack() as own:
                def lsb(name, shape, dt=F32):
                    return own.enter_context(nc.sbuf_tensor(pre + name, shape, dt))

                def lsem(name):
                    return ctx.enter_context(nc.semaphore(pre + name))

                target = (xres, acc)[layer]
                logits = lsb("logits", [P, TILES, EXPERTS])
                top = lsb("top", [P, TILES, 8])
                topi = lsb("topi", [P, TILES, 8], U32)
                topf = lsb("topf", [P, TILES, 2])
                chosen = lsb("chosen", [P, 2, TILES, EXPERTS])
                weight = lsb("weight", [P, TILES, EXPERTS])
                total, rtotal = lsb("total", [P, TILES]), lsb("rtotal", [P, TILES])
                st = lsb("st", [P, TILES, 4])
                sq = lsb("sq", [P, E])
                weightT = lsb("weightT", [EXPERTS, TOK])
                xst = [lsb(f"xst{s}", [P, E]) for s in range(2)]
                xs = [lsb(f"xs{s}", [P, P]) for s in range(2)]
                r1 = [lsb(f"r1{s}", [P, P]) for s in range(2)]
                fs = [lsb(f"fs{s}", [P, P]) for s in range(2)]
                tile_free, x_staged = lsem("tile_free"), lsem("x_staged")
                xT_ps, xT_ready, r1_ps, r1_ready = lsem("xT_ps"), lsem("xT_ready"), lsem("r1_ps"), lsem("r1_ready")
                f_ps, f_ready, logit_ps, feat_ready = lsem("f_ps"), lsem("f_ready"), lsem("logit_ps"), lsem("feat_ready")

                with nc.Block() as block:
                    @block.sync
                    def _(sp):
                        sp.sem_inc(tile_free, 2)

                    @block.gpsimd
                    def _(pool):
                        with pool.Fori(0, TILES // 2) as i:
                            for s in range(2):
                                pool.wait_ge(tile_free, 2 * i + s + 1)
                                nc.gpsimd.tensor_copy(xst[s][:], xres[:, bass.ds(2 * i + s, 1), :].rearrange("p a e -> p (a e)")).then_inc(x_staged, 1)
                            for s in range(2):
                                pool.wait_ge(f_ready, 2 * i + s + 1)
                                nc.gpsimd.tensor_copy(featT[:, bass.ds(P * (2 * i + s), P)], fs[s][:]).then_inc(feat_ready, 1)

                    @block.tensor
                    def _(pe):
                        with pe.Fori(0, TILES // 2) as i:
                            for s in range(2):
                                pe.wait_ge(x_staged, 2 * i + s + 1)
                                nc.tensor.transpose(bank(s, 0, 0, P), xst[s][:], k["ident"]).then_inc(xT_ps, 1)
                            if layer == 0:
                                for s in range(2):
                                    pe.wait_ge(xT_ready, 2 * i + s + 1)
                                    nc.tensor.matmul(bank(s, 1, 0, P), rot_r[:].rearrange("p a s -> p (a s)"), xs[s][:], start=True, stop=True).then_inc(r1_ps, 1)
                                for s in range(2):
                                    pe.wait_ge(r1_ready, 2 * i + s + 1)
                                    nc.tensor.matmul(bank(s, 2, 0, P), rot_l[:].rearrange("p a s -> p (a s)"), r1[s][:], start=True, stop=True).then_inc(f_ps, 1)
                            for s in range(2):
                                pe.wait_ge(f_ready, 2 * i + s + 1)
                                nc.tensor.matmul(bank(s, 3, 0, EXPERTS), fs[s][:], router_w[layer][:], start=True, stop=True).then_inc(logit_ps, 1)

                    @block.scalar
                    def _(act):
                        with act.Fori(0, TILES // 2) as i:
                            if layer == 0:
                                for s in range(2):
                                    act.wait_ge(xT_ps, 2 * i + s + 1)
                                    nc.scalar.activation(xs[s][:], bank(s, 0, 0, P), ACT.Copy).then_inc(xT_ready, 1)
                                for s in range(2):
                                    act.wait_ge(r1_ps, 2 * i + s + 1)
                                    nc.scalar.activation(r1[s][:], bank(s, 1, 0, P), ACT.Copy).then_inc(r1_ready, 1)
                                for s in range(2):
                                    act.wait_ge(f_ps, 2 * i + s + 1)
                                    nc.scalar.activation(fs[s][:], bank(s, 2, 0, P), ACT.Copy).then_inc(f_ready, 1)
                            else:
                                for s in range(2):
                                    act.wait_ge(xT_ps, 2 * i + s + 1)
                                    nc.scalar.activation(fs[s][:], bank(s, 0, 0, P), ACT.Copy).then_inc(f_ready, 1)

                    @block.vector
                    def _(dve):
                        with dve.Fori(0, TILES // 2) as i:
                            for s in range(2):
                                dve.wait_ge(logit_ps, 2 * i + s + 1)
                                dve.wait_ge(feat_ready, 2 * i + s + 1)
                                dst = logits[:, bass.ds(2 * i + s, 1), :].rearrange("p a e -> p (a e)")
                                if layer == 0:
                                    nc.vector.tensor_tensor(dst, bank(s, 3, 0, EXPERTS), router_b[0][:], ALU.add).then_inc(tile_free, 1)
                                else:
                                    nc.vector.tensor_copy(dst, bank(s, 3, 0, EXPERTS)).then_inc(tile_free, 1)

                g_dve, g_act, g_pe = lsem("gate_dve_step"), lsem("gate_act_step"), lsem("gate_pe_step")
                with nc.Block() as block:
                    @block.scalar
                    def _(act):
                        if layer == 1:
                            for n in range(TILES):
                                ins = nc.scalar.activation(sq[:], xres[:, n, :], ACT.Square, accum_out=st[:, n, 0:1])
                                ins.then_inc(g_act, 1)
                                act.wait_ge(g_act, n + 1)
                            nc.scalar.activation(st[:, :, 1], st[:, :, 0], ACT.Ln, bias=eps[:, 0:1], scale=1.0 / E).then_inc(g_act, 1)
                            act.wait_ge(g_act, TILES + 1)
                            nc.scalar.activation(st[:, :, 2], st[:, :, 1], ACT.Exp, scale=-0.5).then_inc(g_act, 1)
                            act.wait_ge(g_dve, 6)
                            nc.scalar.activation(weight[:], logits[:], ACT.Exp).then_inc(g_act, 1)
                        else:
                            act.wait_ge(g_dve, 6)
                            nc.scalar.activation(weight[:], logits[:], ACT.Exp).then_inc(g_act, TILES + 3)
                        for h in range(2):
                            act.wait_ge(g_pe, h + 1)
                            nc.scalar.activation(weightT[:, BANK * h:BANK * h + BANK], bank(0, h)[0:EXPERTS, :], ACT.Copy).then_inc(g_act, 1)

                    @block.vector
                    def _(dve):
                        bc = [P, TILES, EXPERTS]
                        if layer == 1:
                            dve.wait_ge(g_act, TILES + 2)
                            nc.vector.tensor_tensor(logits[:], logits[:], st[:, :, 2:3].to_broadcast(bc), ALU.mult).then_inc(g_dve, 1)
                            dve.wait_ge(g_dve, 1)
                            nc.vector.tensor_tensor(logits[:], logits[:], genre[:], ALU.add).then_inc(g_dve, 1)
                            dve.wait_ge(g_dve, 2)
                        else:
                            nc.vector.memset(total[:], 0.0).then_inc(g_dve, 2)
                        for n in range(TILES):
                            ins = nc.vector.max(top[:, n, :], logits[:, n, :])
                        ins.then_inc(g_dve, 1)
                        dve.wait_ge(g_dve, 3)
                        for n in range(TILES):
                            ins = nc.vector.max_index(topi[:, n, :], top[:, n, :], logits[:, n, :])
                        ins.then_inc(g_dve, 1)
                        dve.wait_ge(g_dve, 4)
                        nc.vector.tensor_copy(topf[:], topi[:, :, 0:2]).then_inc(g_dve, 1)
                        nc.vector.tensor_tensor(logits[:], logits[:], top[:, :, 0:1].to_broadcast(bc), ALU.subtract).then_inc(g_dve, 1)
                        dve.wait_ge(g_dve, 6)
                        for j in range(2):
                            nc.vector.tensor_tensor(chosen[:, j], k["iota"].unsqueeze(1).to_broadcast(bc), topf[:, :, j:j + 1].to_broadcast(bc), ALU.is_equal).then_inc(g_dve, 1)
                        dve.wait_ge(g_dve, 8)
                        nc.vector.tensor_tensor(chosen[:, 0], chosen[:, 0], chosen[:, 1], ALU.add).then_inc(g_dve, 1)
                        dve.wait_ge(g_dve, 9)
                        dve.wait_ge(g_act, TILES + 3)
                        nc.vector.tensor_tensor(chosen[:, 0], chosen[:, 0], weight[:], ALU.mult).then_inc(g_dve, 1)
                        dve.wait_ge(g_dve, 10)
                        nc.vector.tensor_reduce(total[:], chosen[:, 0] if layer == 0 else weight[:], X, ALU.add).then_inc(g_dve, 1)
                        dve.wait_ge(g_dve, 11)
                        nc.vector.reciprocal(rtotal[:], total[:]).then_inc(g_dve, 1)
                        dve.wait_ge(g_dve, 12)
                        nc.vector.tensor_tensor(weight[:], chosen[:, 0], rtotal[:].unsqueeze(2).to_broadcast(bc), ALU.mult).then_inc(g_dve, 1)
                        for h in range(2):
                            dve.wait_ge(g_pe, 3 + h)
                            src = bank(1, h).rearrange("p (n e) -> p n e", e=E)
                            dst = target[:, 4 * h:4 * h + 4, :]
                            if layer == 0:
                                nc.vector.tensor_tensor(dst, dst, src, ALU.add).then_inc(g_dve, 1)
                            else:
                                nc.vector.tensor_copy(dst, src).then_inc(g_dve, 1)

                    @block.tensor
                    def _(pe):
                        pe.wait_ge(g_dve, 13)
                        for n in range(TILES):
                            mm = nc.tensor.transpose(bank(0, n // 4, P * (n % 4), P * (n % 4) + P)[0:EXPERTS, :], weight[:, n, :], k["ident"])
                            if n % 4 == 3:
                                mm.then_inc(g_pe, 1)
                        pe.wait_ge(g_act, TILES + 5)
                        for n in range(TILES):
                            mm = nc.tensor.matmul(bank(1, n // 4, P * (n % 4), P * (n % 4) + P), weightT[:, P * n:P * n + P], last_b[layer][:], start=True, stop=True)
                            if n % 4 == 3:
                                mm.then_inc(g_pe, 1)

                HALVES = TOK // BANK
                if layer == 0:
                    w_shapes = [("w1", 1, ff), ("w2", nf, E)]
                else:
                    w_shapes = [("w1", 1, ff), ("w2", nf, ff), ("w3", nf, E)]
                nb = nf * (2 if layer else 1)
                ws = [[lsb(f"{n}_{s}", [P, a, b]) for n, a, b in w_shapes] for s in range(2)]
                bs = [lsb(f"b_{s}", [P, nb]) for s in range(2)]
                hid = [lsb(f"hid{h}", [P, nf, BANK]) for h in range(HALVES)]
                hid2 = [lsb(f"hid2{h}", [P, nf, BANK]) for h in range(HALVES)] if layer else hid
                w_loaded = [lsem(f"w_loaded{s}") for s in range(2)]
                w_free, hid_ps, hid_ready = lsem("w_free"), lsem("hid_ps"), lsem("hid_ready")
                out_ps, added = lsem("out_ps"), lsem("added")
                UNITS = 2 * HALVES * nf if layer else HALVES * nf
                NB = 4

                with nc.Block() as block:
                    @block.sync
                    def _(sp):
                        sp.sem_inc(w_free, 2)
                        sp.sem_inc(hid_ready, NB)
                        sp.sem_inc(out_ps, HALVES)
                        sp.sem_inc(added, HALVES)
                        with sp.Fori(0, EXPERTS // 2) as i:
                            for s in range(2):
                                sp.wait_ge(w_free, 2 * i + s + 1)
                                for (n, a, b), w in zip(w_shapes, ws[s]):
                                    sp.dma_start(w[:], d[f"moe{layer}_{n}"][bass.ds(2 * i + s, 1)].rearrange("x (c p) f -> p (x c) f", p=P)).then_inc(w_loaded[s], 16)
                                sp.dma_start(bs[s][:], d[f"moe{layer}_b"][bass.ds(2 * i + s, 1)].rearrange("x p f -> p (x f)")).then_inc(w_loaded[s], 16)

                    @block.tensor
                    def _(pe):
                        with pe.Fori(0, EXPERTS // 2) as i:
                            for s in range(2):
                                e = 2 * i + s
                                pe.wait_ge(w_loaded[s], 16 * (len(w_shapes) + 1) * (i + 1))
                                u = 0
                                for h in range(HALVES):
                                    for f in range(nf):
                                        pe.wait_ge(hid_ready, UNITS * e + u + 1)
                                        nc.tensor.matmul(bank(0, u % NB), ws[s][0][:, 0, P * f:P * f + P], featT[:, BANK * h:BANK * h + BANK], start=True, stop=True).then_inc(hid_ps, 1)
                                        u += 1
                                if layer:
                                    for h in range(HALVES):
                                        pe.wait_ge(hid_ready, UNITS * e + NB + nf * (h + 1))
                                        for f in range(nf):
                                            pe.wait_ge(hid_ready, UNITS * e + u + 1)
                                            for c in range(nf):
                                                mm = nc.tensor.matmul(bank(0, u % NB), ws[s][1][:, c, P * f:P * f + P], hid[h][:, c, :], start=(c == 0), stop=(c == nf - 1))
                                            mm.then_inc(hid_ps, 1)
                                            u += 1
                                for h in range(HALVES):
                                    pe.wait_ge(hid_ready, UNITS * e + NB + (UNITS - nf * HALVES) + nf * (h + 1))
                                    pe.wait_ge(added, HALVES * e + h + 1)
                                    for j in range(4):
                                        for c in range(nf):
                                            mm = nc.tensor.matmul(bank(1, h, E * j, E * j + E), hid2[h][:, c, P * j:P * j + P], ws[s][-1][:, c, :], start=(c == 0), stop=(c == nf - 1))
                                    mm.then_inc(out_ps, 1)
                                pe.wait_ge(out_ps, HALVES * e + 2 * HALVES)
                                pe.sem_inc(w_free, 1)

                    @block.scalar
                    def _(act):
                        with act.Fori(0, EXPERTS // 2) as i:
                            for s in range(2):
                                e = 2 * i + s
                                u = 0
                                for stage in range(2 if layer else 1):
                                    last_stage = stage == (1 if layer else 0)
                                    for h in range(HALVES):
                                        if last_stage:
                                            act.wait_ge(out_ps, HALVES * e + h + 1)
                                        for f in range(nf):
                                            act.wait_ge(hid_ps, UNITS * e + u + 1)
                                            nc.scalar.activation((hid2 if last_stage else hid)[h][:, f, :], bank(0, u % NB), ACT.Relu,
                                                                 bias=bs[s][:, nf * stage + f:nf * stage + f + 1]).then_inc(hid_ready, 1)
                                            u += 1

                    @block.vector
                    def _(dve):
                        with dve.Fori(0, EXPERTS // 2) as i:
                            for s in range(2):
                                e = 2 * i + s
                                for h in range(HALVES):
                                    dve.wait_ge(out_ps, HALVES + HALVES * e + h + 1)
                                    dve.wait_ge(added, HALVES * e + h + 1)
                                    for j in range(4):
                                        n = 4 * h + j
                                        ins = nc.vector.scalar_tensor_tensor(out=target[:, n, :], in0=bank(1, h, E * j, E * j + E),
                                                                             scalar=weight[:, n, bass.ds(e, 1)], in1=target[:, n, :],
                                                                             op0=ALU.mult, op1=ALU.add)
                                    ins.then_inc(added, 1)

        def loglinear_attention():
            with ExitStack() as own:
                def lsb(name, shape, dt=F32):
                    return [own.enter_context(nc.sbuf_tensor(f"log_{name}{s}", shape, dt)) for s in range(2)]

                def lsem(name):
                    return ctx.enter_context(nc.semaphore("log_" + name))

                ust, us = lsb("ust", [P, E]), lsb("us", [P, P])
                qk = lsb("qk", [P, 2 * LH, P])
                v = lsb("v", [P, LH * LD])
                sp_z, sp_a = lsb("sp_z", [P, NSMALL]), lsb("sp_a", [P, NSMALL])
                gtri = lsb("gtri", [P, LH, S])
                decay = lsb("decay", [P, LH, S])
                lamw = lsb("lamw", [P, LH, S])
                a = lsb("a", [P, LH, S])
                abd = lsb("abd", [P, LH, P])
                yT = lsb("yT", [P, LH, P])
                out = lsb("out", [P, E])
                bn, mv, st = lsb("bn", [P, 6]), lsb("mv", [P, 2]), lsb("st", [P, 2])
                tile_free, zeroed = lsem("tile_free"), lsem("zeroed")
                u_staged, uT_ps, uT_ready = lsem("u_staged"), lsem("uT_ps"), lsem("uT_ready")
                small_ps, q_ps, k_ps, v_ps = lsem("small_ps"), lsem("q_ps"), lsem("k_ps"), lsem("v_ps")
                q_ready, k_ready, v_ready = lsem("q_ready"), lsem("k_ready"), lsem("v_ready")
                z_abs, z_log, gtri_ready, decay_ps, decay_ready = lsem("z_abs"), lsem("z_log"), lsem("gtri_ready"), lsem("decay_ps"), lsem("decay_ready")
                soft_ready = lsem("soft_ready")
                weight_ready = lsem("weight_ready")
                scores_ps, aT_ready, yT_ps, yT_ready, out_ps = lsem("scores_ps"), lsem("aT_ready"), lsem("yT_ps"), lsem("yT_ready"), lsem("out_ps")
                var_ready, rstd_ready = lsem("var_ready"), lsem("rstd_ready")
                dve_step, act_step, level_set = lsem("dve_step"), lsem("act_step"), lsem("level_set")
                scale = 1.0 / float(np.sqrt(LD))

                with nc.Block() as block:
                    @block.sync
                    def _(sp):
                        sp.sem_inc(tile_free, 2)
                        sp.dma_start(wqk[:], d["attn1_qk"]).then_inc(loaded["wattn1"], 16)
                        sp.dma_start(wv[:], d["attn1_v"]).then_inc(loaded["wattn1"], 16)
                        sp.dma_start(wout[:], d["attn1_out"].rearrange("(c p) e -> p c e", p=P)).then_inc(loaded["wattn1"], 16)

                    @block.gpsimd
                    def _(pool):
                        for s in range(2):
                            nc.gpsimd.memset(abd[s][:], 0.0).then_inc(zeroed, 1)
                            nc.gpsimd.memset(lamw[s][:], 0.0).then_inc(zeroed, 1)
                        with pool.Fori(0, TILES // 2) as i:
                            for s in range(2):
                                pool.wait_ge(tile_free, 2 * i + s + 1)
                                nc.gpsimd.tensor_copy(ust[s][:], acc[:, bass.ds(2 * i + s, 1), :].rearrange("p a e -> p (a e)")).then_inc(u_staged, 1)
                            for s in range(2):
                                pool.wait_ge(soft_ready, 2 * i + s + 1)
                                nc.gpsimd.tensor_tensor(gtri[s][:], sp_z[s][:, 0:LH].unsqueeze(2).to_broadcast([P, LH, S]),
                                                        k["negafter"].unsqueeze(1).to_broadcast([P, LH, S]), ALU.mult).then_inc(gtri_ready, 1)

                    @block.tensor
                    def _(pe):
                        pe.wait_ge(loaded["wattn1"], 48)
                        with pe.Fori(0, TILES // 2) as i:
                            for s in range(2):
                                pe.wait_ge(u_staged, 2 * i + s + 1)
                                nc.tensor.transpose(bank(s, 0, 0, P), ust[s][:], k["ident"]).then_inc(uT_ps, 1)
                            for s in range(2):
                                pe.wait_ge(uT_ready, 2 * i + s + 1)
                                nc.tensor.matmul(bank(s, 0, P, P + NSMALL), us[s][:], small_w[:], start=True, stop=True).then_inc(small_ps, 1)
                            for s in range(2):
                                for c in range(LH):
                                    mm = nc.tensor.matmul(bank(s, 2 + c // 4, P * (c % 4), P * (c % 4) + P), wqk[:, P * c:P * c + P], us[s][:], start=True, stop=True)
                                mm.then_inc(q_ps, 1)
                                pe.wait_ge(gtri_ready, 2 * i + s + 1)
                                nc.tensor.matmul(bank(s, 0, 2 * P, 4 * P), k["upto"], gtri[s][:].rearrange("p h t -> p (h t)"), start=True, stop=True).then_inc(decay_ps, 1)
                                pe.wait_ge(decay_ready, 2 * i + s + 1)
                                pe.wait_ge(q_ready, 2 * i + s + 1)
                                for c in range(LH):
                                    mm = nc.tensor.matmul(bank(s, 2 + c // 4, P * (c % 4), P * (c % 4) + P), wqk[:, P * (LH + c):P * (LH + c) + P], us[s][:], start=True, stop=True)
                                mm.then_inc(k_ps, 1)
                                for c in range(2):
                                    mm = nc.tensor.matmul(bank(s, c), us[s][:], wv[:, BANK * c:BANK * c + BANK], start=True, stop=True)
                                mm.then_inc(v_ps, 1)
                            for s in range(2):
                                pe.wait_ge(k_ready, 2 * i + s + 1)
                                pe.wait_ge(v_ready, 2 * i + s + 1)
                                for h in range(LH):
                                    mm = nc.tensor.matmul(bank(s, 2 + h // 4, P * (h % 4), P * (h % 4) + P), qk[s][:, h, :], qk[s][:, LH + h, :], start=True, stop=True)
                                mm.then_inc(scores_ps, 1)
                            for s in range(2):
                                pe.wait_ge(aT_ready, 2 * i + s + 1)
                                for h in range(LH):
                                    mm = nc.tensor.matmul(bank(s, h // 4, P * (h % 4), P * (h % 4) + P), v[s][:, LD * h:LD * h + LD], abd[s][:, h, :], start=True, stop=True)
                                mm.then_inc(yT_ps, 1)
                            for s in range(2):
                                pe.wait_ge(yT_ready, 2 * i + s + 1)
                                for c in range(LH):
                                    mm = nc.tensor.matmul(bank(s, 2, 0, E), yT[s][:, c, :], wout[:, c, :], start=(c == 0), stop=(c == LH - 1))
                                mm.then_inc(out_ps, 1)

                    @block.scalar
                    def _(act):
                        with act.Fori(0, TILES // 2) as i:
                            for s in range(2):
                                act.wait_ge(uT_ps, 2 * i + s + 1)
                                nc.scalar.activation(us[s][:], bank(s, 0, 0, P), ACT.Copy).then_inc(uT_ready, 1)
                            for s in range(2):
                                act.wait_ge(z_abs, 2 * i + s + 1)
                                nc.scalar.activation(sp_a[s][:], sp_a[s][:], ACT.Exp).then_inc(act_step, 1)
                            for s in range(2):
                                act.wait_ge(act_step, 4 * i + s + 1)
                                nc.scalar.activation(sp_a[s][:], sp_a[s][:], ACT.Ln, bias=1.0).then_inc(z_log, 1)
                            for s in range(2):
                                act.wait_ge(q_ps, 2 * i + s + 1)
                                for c in range(2):
                                    ins = nc.scalar.activation(qk[s][:, 4 * c:4 * c + 4, :].rearrange("p c t -> p (c t)"), bank(s, 2 + c), ACT.Copy)
                                ins.then_inc(q_ready, 1)
                                act.wait_ge(decay_ps, 2 * i + s + 1)
                                nc.scalar.activation(decay[s][:].rearrange("p h t -> p (h t)"), bank(s, 0, 2 * P, 4 * P), ACT.Exp).then_inc(decay_ready, 1)
                                act.wait_ge(k_ps, 2 * i + s + 1)
                                for c in range(2):
                                    ins = nc.scalar.activation(qk[s][:, LH + 4 * c:LH + 4 * c + 4, :].rearrange("p c t -> p (c t)"), bank(s, 2 + c), ACT.Copy)
                                ins.then_inc(k_ready, 1)
                                act.wait_ge(v_ps, 2 * i + s + 1)
                                for c in range(2):
                                    ins = nc.scalar.activation(v[s][:, BANK * c:BANK * c + BANK], bank(s, c), ACT.Copy)
                                ins.then_inc(v_ready, 1)
                            for s in range(2):
                                act.wait_ge(yT_ps, 2 * i + s + 1)
                                for c in range(2):
                                    ins = nc.scalar.activation(yT[s][:, 4 * c:4 * c + 4, :].rearrange("p c t -> p (c t)"), bank(s, c), ACT.Copy)
                                ins.then_inc(yT_ready, 1)
                            for s in range(2):
                                act.wait_ge(var_ready, 2 * i + s + 1)
                                nc.scalar.activation(st[s][:, 0:1], mv[s][:, 1:2], ACT.Ln, bias=eps[:, 2:3]).then_inc(act_step, 1)
                            for s in range(2):
                                act.wait_ge(act_step, 4 * i + 2 + s + 1)
                                nc.scalar.activation(st[s][:, 1:2], st[s][:, 0:1], ACT.Exp, scale=-0.5).then_inc(rstd_ready, 1)

                    @block.vector
                    def _(dve):
                        dve.wait_ge(zeroed, 4)
                        DVE_STEPS = 2 * 8
                        with dve.Fori(0, TILES // 2) as i:
                            for s in range(2):
                                dve.wait_ge(small_ps, 2 * i + s + 1)
                                nc.vector.tensor_tensor(sp_z[s][:], bank(s, 0, P, P + NSMALL), small_b[:], ALU.add).then_inc(dve_step, 1)
                            for s in range(2):
                                dve.wait_ge(dve_step, DVE_STEPS * i + s + 1)
                                nc.vector.scalar_tensor_tensor(out=sp_a[s][:], in0=sp_z[s][:], scalar=-1.0, in1=sp_z[s][:], op0=ALU.mult, op1=ALU.min).then_inc(z_abs, 1)
                            for s in range(2):
                                dve.wait_ge(z_log, 2 * i + s + 1)
                                nc.vector.scalar_tensor_tensor(out=sp_z[s][:], in0=sp_z[s][:], scalar=0.0, in1=sp_a[s][:], op0=ALU.max, op1=ALU.add).then_inc(soft_ready, 1)
                            for n in range(LEVELS):
                                if n == 0:
                                    dve.wait_ge(soft_ready, 2 * i + 2)
                                else:
                                    dve.wait_ge(level_set, 2 * LEVELS * i + 2 * n)
                                nc.vector.memset(holder[:], 0.0)
                                for s in range(2):
                                    nc.vector.copy_predicated(lamw[s][:], levelmask[:, n, :].unsqueeze(1).to_broadcast([P, LH, S]),
                                                              sp_z[s][:, LH * (n + 1):LH * (n + 2)].unsqueeze(2).to_broadcast([P, LH, S])).then_inc(level_set, 1)
                            for s in range(2):
                                dve.wait_ge(level_set, 2 * LEVELS * i + 2 * (LEVELS - 1) + s + 1)
                                dve.wait_ge(decay_ready, 2 * i + s + 1)
                                nc.vector.tensor_tensor(decay[s][:], decay[s][:], lamw[s][:], ALU.mult).then_inc(dve_step, 1)
                            for s in range(2):
                                dve.wait_ge(dve_step, DVE_STEPS * i + 2 + s + 1)
                                dve.wait_ge(scores_ps, 2 * i + s + 1)
                                src = PS[:, s * HALF + 2 * BANK:s * HALF + 4 * BANK].rearrange("p (h t) -> p h t", t=P)
                                for b in range(SEQ):
                                    r = slice(S * b, S * b + S)
                                    ins = nc.vector.scalar_tensor_tensor(out=a[s][r], in0=src[r][:, :, S * b:S * b + S], scalar=scale, in1=decay[s][r],
                                                                         op0=ALU.mult, op1=ALU.mult)
                                ins.then_inc(dve_step, 1)
                            for s in range(2):
                                dve.wait_ge(dve_step, DVE_STEPS * i + 4 + s + 1)
                                for b in range(SEQ):
                                    ins = nc.vector.transpose(abd[s][S * b:S * b + S, :, S * b:S * b + S], a[s][S * b:S * b + S, :, :])
                                ins.then_inc(aT_ready, 1)
                            for s in range(2):
                                dve.wait_ge(out_ps, 2 * i + s + 1)
                                nc.vector.tensor_tensor(out[s][:], bank(s, 2, 0, E), ust[s][:], ALU.add).then_inc(dve_step, 1)
                            for s in range(2):
                                dve.wait_ge(dve_step, DVE_STEPS * i + 6 + s + 1)
                                nc.vector.bn_stats(bn[s][:], out[s][:]).then_inc(dve_step, 1)
                            dve.wait_ge(dve_step, DVE_STEPS * i + 8 + 2)
                            nc.vector.memset(holder[:], 0.0)
                            for s in range(2):
                                nc.vector.bn_aggr(mv[s][:], bn[s][:]).then_inc(var_ready, 1)
                            for s in range(2):
                                dve.wait_ge(rstd_ready, 2 * i + s + 1)
                                nc.vector.tensor_scalar(out[s][:], out[s][:], mv[s][:, 0:1], st[s][:, 1:2], ALU.subtract, ALU.mult).then_inc(dve_step, 1)
                            for s in range(2):
                                dve.wait_ge(dve_step, DVE_STEPS * i + 10 + s + 1)
                                nc.vector.tensor_tensor(out[s][:], out[s][:], ln[:, 0, :], ALU.mult).then_inc(dve_step, 1)
                            for s in range(2):
                                dve.wait_ge(dve_step, DVE_STEPS * i + 12 + s + 1)
                                nc.vector.tensor_tensor(out[s][:], out[s][:], ln[:, 1, :], ALU.add).then_inc(dve_step, 1)
                            for s in range(2):
                                dve.wait_ge(dve_step, DVE_STEPS * i + 14 + s + 1)
                                here = xres[:, bass.ds(2 * i + s, 1), :].rearrange("p a e -> p (a e)")
                                nc.vector.tensor_tensor(here, here, out[s][:], ALU.add).then_inc(tile_free, 1)

        def ternary_ffn():
            with ExitStack() as own:
                def lsb(name, shape, dt=F32):
                    return [own.enter_context(nc.sbuf_tensor(f"ffn_{name}_{s}", shape, dt)) for s in range(2)]

                def lsem(name):
                    return ctx.enter_context(nc.semaphore("ffn_" + name))

                NF = HID // P
                cs = lsb("cs", [P, P])
                xr, xq, xqT = lsb("xr", [P, P]), lsb("xq", [P, P], BF16), lsb("xqT", [P, P], BF16)
                m1, m2 = lsb("m1", [P, 4]), lsb("m2", [P, 4])
                dg, sbc = lsb("dg", [P, P]), lsb("sbc", [P, P])
                hp = lsb("hp", [P, NF, SEQ, S + 2])
                y, ys = lsb("y", [P, NF, SEQ, S]), lsb("ys", [P, NF, P])
                yr, yq, yqT = lsb("yr", [P, HID]), lsb("yq", [P, HID], BF16), lsb("yqT", [P, NF, P], BF16)
                outb = lsb("outb", [P, E])
                tile_free, zeroed, stored = lsem("tile_free"), lsem("zeroed"), [lsem(f"stored{s}") for s in range(2)]
                c_staged, ct_ps, xq_ready, xqT_ps, xqT_ready = lsem("c_staged"), lsem("ct_ps"), lsem("xq_ready"), lsem("xqT_ps"), lsem("xqT_ready")
                diag_ready, sbc_ps, sbc_ready, h_ps, h_ready = lsem("diag_ready"), lsem("sbc_ps"), lsem("sbc_ready"), lsem("h_ps"), lsem("h_ready")
                mid_ready, conv_ready, silu_ready = lsem("mid_ready"), lsem("conv_ready"), lsem("silu_ready")
                yt_ps, yq_ready, yqT_ps, yqT_ready, o_ps, out_ready = lsem("yt_ps"), lsem("yq_ready"), lsem("yqT_ps"), lsem("yqT_ready"), lsem("o_ps"), lsem("out_ready")
                dve_step = lsem("dve_step")

                with nc.Block() as block:
                    @block.sync
                    def _(sp):
                        sp.sem_inc(tile_free, 2)
                        for s in range(2):
                            sp.sem_inc(stored[s], 16)
                        with sp.Fori(0, TILES // 2) as i:
                            for s in range(2):
                                sp.wait_ge(out_ready, 2 * i + s + 1)
                                sp.dma_start(d["out"][bass.ds(2 * i + s, 1)].rearrange("a p e -> p (a e)"), outb[s][:]).then_inc(stored[s], 16)
                        for s in range(2):
                            sp.wait_ge(stored[s], 16 * (TILES // 2 + 1))

                    @block.gpsimd
                    def _(pool):
                        for s in range(2):
                            nc.gpsimd.memset(hp[s][:], 0.0).then_inc(zeroed, 1)
                        with pool.Fori(0, TILES // 2) as i:
                            for s in range(2):
                                pool.wait_ge(tile_free, 2 * i + s + 1)
                                nc.gpsimd.tensor_copy(cs[s][:], featT[:, bass.ds(P * (2 * i + s), P)]).then_inc(c_staged, 1)
                            for s in range(2):
                                pool.wait_ge(xq_ready, 2 * i + s + 1)
                                nc.gpsimd.tensor_tensor(dg[s][:], k["ident"], m1[s][:, 3:4].to_broadcast([P, P]), ALU.mult).then_inc(diag_ready, 1)

                    @block.tensor
                    def _(pe):
                        with pe.Fori(0, TILES // 2) as i:
                            for s in range(2):
                                pe.wait_ge(c_staged, 2 * i + s + 1)
                                nc.tensor.transpose(bank(s, 0, 0, P), cs[s][:], k["ident"]).then_inc(ct_ps, 1)
                            for s in range(2):
                                pe.wait_ge(xq_ready, 2 * i + s + 1)
                                nc.tensor.transpose(bank(s, 3, 0, P // 2).bitcast(BF16), xq[s][:], ident_b[:]).then_inc(xqT_ps, 1)
                            for s in range(2):
                                pe.wait_ge(diag_ready, 2 * i + s + 1)
                                nc.tensor.matmul(bank(s, 0, P, 2 * P), k["ones"], dg[s][:], start=True, stop=True).then_inc(sbc_ps, 1)
                            for s in range(2):
                                pe.wait_ge(xqT_ready, 2 * i + s + 1)
                                for f in range(NF):
                                    mm = nc.tensor.matmul(bank(s, 1, P * f, P * f + P), ffn_q[0][:, P * f:P * f + P], xqT[s][:], start=True, stop=True)
                                mm.then_inc(h_ps, 1)
                            for s in range(2):
                                pe.wait_ge(silu_ready, 2 * i + s + 1)
                                for f in range(NF):
                                    mm = nc.tensor.transpose(bank(s, 2, P * f, P * f + P), ys[s][:, f, :], k["ident"])
                                mm.then_inc(yt_ps, 1)
                            for s in range(2):
                                pe.wait_ge(yq_ready, 2 * i + s + 1)
                                for f in range(NF):
                                    mm = nc.tensor.transpose(bank(s, 3, P // 2 * f, P // 2 * (f + 1)).bitcast(BF16), yq[s][:, P * f:P * f + P], ident_b[:])
                                mm.then_inc(yqT_ps, 1)
                            for s in range(2):
                                pe.wait_ge(yqT_ready, 2 * i + s + 1)
                                for f in range(NF):
                                    mm = nc.tensor.matmul(bank(s, 0, 2 * P, 3 * P), yqT[s][:, f, :], ffn_q[1][:, P * f:P * f + P], start=(f == 0), stop=(f == NF - 1))
                                mm.then_inc(o_ps, 1)

                    @block.scalar
                    def _(act):
                        with act.Fori(0, TILES // 2) as i:
                            for s in range(2):
                                act.wait_ge(xqT_ps, 2 * i + s + 1)
                                nc.scalar.activation(xqT[s][:], bank(s, 3, 0, P // 2).bitcast(BF16), ACT.Copy).then_inc(xqT_ready, 1)
                            for s in range(2):
                                act.wait_ge(sbc_ps, 2 * i + s + 1)
                                nc.scalar.activation(sbc[s][:], bank(s, 0, P, 2 * P), ACT.Copy).then_inc(sbc_ready, 1)
                            for s in range(2):
                                act.wait_ge(h_ready, 2 * i + s + 1)
                                for f in range(NF):
                                    ins = nc.scalar.activation(y[s][:, f], hp[s][:, f, :, 1:S + 1], ACT.Identity, bias=conv[:, f, 3:4], scale=conv[:, f, 1:2])
                                ins.then_inc(mid_ready, 1)
                            for s in range(2):
                                act.wait_ge(conv_ready, 2 * i + s + 1)
                                nc.scalar.activation(ys[s][:].rearrange("p f t -> p (f t)"), y[s][:].rearrange("p f b t -> p (f b t)"), ACT.Silu).then_inc(silu_ready, 1)
                            for s in range(2):
                                act.wait_ge(yqT_ps, 2 * i + s + 1)
                                nc.scalar.activation(yqT[s][:].rearrange("p f t -> p (f t)"), bank(s, 3, 0, P // 2 * NF).bitcast(BF16), ACT.Copy).then_inc(yqT_ready, 1)

                    @block.vector
                    def _(dve):
                        dve.wait_ge(zeroed, 2)
                        DVE_STEPS = 2 * 11

                        with dve.Fori(0, TILES // 2) as i:
                            def quantise(base, ps_ready, src, m, r, q, n, signal):
                                for s in range(2):
                                    dve.wait_ge(ps_ready, 2 * i + s + 1)
                                    nc.vector.tensor_reduce(m[s][:, 0:1], src(s), X, ALU.max, apply_absolute_value=True).then_inc(dve_step, 1)
                                for s in range(2):
                                    dve.wait_ge(dve_step, DVE_STEPS * i + base + s + 1)
                                    nc.vector.tensor_scalar(m[s][:, 1:2], m[s][:, 0:1], 1e-5, 1.0 / QMAX, ALU.max, ALU.mult).then_inc(dve_step, 1)
                                for s in range(2):
                                    dve.wait_ge(dve_step, DVE_STEPS * i + base + 2 + s + 1)
                                    nc.vector.reciprocal(m[s][:, 2:3], m[s][:, 1:2]).then_inc(dve_step, 1)
                                for s in range(2):
                                    dve.wait_ge(dve_step, DVE_STEPS * i + base + 4 + s + 1)
                                    nc.vector.tensor_scalar(r[s][:], src(s), m[s][:, 2:3], ROUND, ALU.mult, ALU.add).then_inc(dve_step, 1)
                                    nc.vector.tensor_scalar(m[s][:, 3:4], m[s][:, 1:2], wmean[:, n:n + 1], None, ALU.mult)
                                for s in range(2):
                                    dve.wait_ge(dve_step, DVE_STEPS * i + base + 6 + s + 1)
                                    nc.vector.tensor_scalar(q[s][:], r[s][:], ROUND, None, ALU.subtract).then_inc(signal, 1)

                            quantise(0, ct_ps, lambda s: bank(s, 0, 0, P), m1, xr, xq, 0, xq_ready)
                            for s in range(2):
                                dve.wait_ge(h_ps, 2 * i + s + 1)
                                dve.wait_ge(sbc_ready, 2 * i + s + 1)
                                nc.vector.tensor_tensor(hp[s][:, :, :, 1:S + 1], bank(s, 1).rearrange("p (f b t) -> p f b t", f=NF, b=SEQ),
                                                        sbc[s][:].rearrange("p (b t) -> p b t", t=S).unsqueeze(1).to_broadcast([P, NF, SEQ, S]), ALU.mult).then_inc(h_ready, 1)
                            for s in range(2):
                                dve.wait_ge(mid_ready, 2 * i + s + 1)
                                for f in range(NF):
                                    ins = nc.vector.scalar_tensor_tensor(out=y[s][:, f], in0=hp[s][:, f, :, 0:S], scalar=conv[:, f, 0:1], in1=y[s][:, f], op0=ALU.mult, op1=ALU.add)
                                ins.then_inc(dve_step, 1)
                            for s in range(2):
                                dve.wait_ge(dve_step, DVE_STEPS * i + 8 + s + 1)
                                for f in range(NF):
                                    ins = nc.vector.scalar_tensor_tensor(out=y[s][:, f], in0=hp[s][:, f, :, 2:S + 2], scalar=conv[:, f, 2:3], in1=y[s][:, f], op0=ALU.mult, op1=ALU.add)
                                ins.then_inc(conv_ready, 1)
                            quantise(10, yt_ps, lambda s: bank(s, 2), m2, yr, yq, 1, yq_ready)
                            for s in range(2):
                                dve.wait_ge(o_ps, 2 * i + s + 1)
                                dve.wait_ge(stored[s], 16 * (i + 1))
                                nc.vector.scalar_tensor_tensor(out=outb[s][:], in0=bank(s, 0, 2 * P, 3 * P), scalar=m2[s][:, 3:4],
                                                               in1=xres[:, bass.ds(2 * i + s, 1), :].rearrange("p a e -> p (a e)"), op0=ALU.mult, op1=ALU.add).then_inc(out_ready, 1)
                            for s in range(2):
                                dve.wait_ge(out_ready, 2 * i + s + 1)
                                dve.sem_inc(tile_free, 1)
                            dve.sem_inc(dve_step, DVE_STEPS - 18)

        stages = [lambda: conditioning(0), rotary_attention, lambda: experts(0), lambda: experts(1),
                  loglinear_attention, lambda: conditioning(1), ternary_ffn]
        for stage in stages:
            stage()


def kernel(**inp):
    import concourse.bacc as _bacc
    from concourse.bass_utils import run_bass_kernel_spmd as _run

    a = {n: np.asarray(v) for n, v in inp.items()}
    cat = np.concatenate
    lay = {"x": a["x"].reshape(TOK, E), "condT": a["cond_256"].T}
    for n, pre in enumerate(("L0_cond_", "L1_cond2_")):
        lay[f"cond_w{n}"] = cat([a[pre + w].T for w in ("Wq", "Wk", "Wv", "Wo")], axis=1)
        lay[f"mod_w{n}"] = a[pre + "Wc"].T
        lay[f"mod_b{n}"] = a[pre + "bc"].reshape(2, E).T
        lay[f"rms_s{n}"] = a[pre + "rms_scale"][:, None]
    lay["mask"] = np.tile(np.ascontiguousarray(a["mask_SxS_bk1"]).view(np.int32), (SEQ, 1))
    lay["attn0_qk"] = cat([a["L0_attn_w_q"], a["L0_attn_w_kv"][:, :AH * AD]], axis=1)
    lay["attn0_v"] = a["L0_attn_w_kv"][:, AH * AD:]
    lay["attn0_out"] = a["L0_attn_w_out"]
    lay["attn1_qk"] = cat([a["L1_attn_Wq"].T, a["L1_attn_Wk"].T], axis=1)
    lay["attn1_v"] = a["L1_attn_Wv"].T
    lay["attn1_out"] = a["L1_attn_Wo"].T
    part = np.arange(4)[:, None] ^ np.arange(4)[None, :]
    lay["quat"] = a["L0_cond2_q_right"][part].transpose(0, 2, 1).reshape(P, 4)
    lay["quat_l"] = a["cond_256"][part].transpose(0, 2, 1).reshape(P, 4)
    lay["quat_all"] = np.tile(a["cond_256"].T, (4, 1))
    lay["sgate"] = np.tile(a["L0_cond2_spectral_gate"].reshape(S, 1), (4, 1))
    rows = lambda v: np.tile(v.reshape(1, -1), (P, 1))
    lay["router_w0"], lay["router_b0"] = a["L0_ffn_W_router"], rows(a["L0_ffn_b_router"])
    lay["router_w1"], lay["router_b1"] = a["L1_cond_wg_W"], rows(a["L1_cond_wg_b"])
    lay["genre_w"], lay["genre_b"] = a["L1_cond_gg_W"], rows(a["L1_cond_gg_b"])
    lay["rms1"] = a["L1_cond_rms_w"][:, None]
    lay["ffn_w0"] = a["L1_ffn_w1"].T
    lay["ffn_w1"] = a["L1_ffn_w2"].T.reshape(HID // P, P, E).transpose(1, 0, 2).reshape(P, HID)
    taps = cat([a["L1_ffn_conv_w"][:, 0, :], a["L1_ffn_conv_b"][:, None]], axis=1)
    lay["conv"] = taps.reshape(HID // P, P, 4).transpose(1, 0, 2).reshape(P, HID // P * 4)
    lay["moe0_b"] = a["L0_ffn_b1"].reshape(EXPERTS, -1, P).transpose(0, 2, 1)
    lay["moe1_b"] = cat([a["L1_cond_b1"], a["L1_cond_b2"]], axis=1).reshape(EXPERTS, -1, P).transpose(0, 2, 1)
    lay["moe0_last_b"], lay["moe1_last_b"] = a["L0_ffn_b2"], a["L1_cond_b3"]
    levels = a["L1_attn_Wdl"].reshape(LH, -1, E)[:, :LEVELS].transpose(1, 0, 2).reshape(LH * LEVELS, E)
    lay["small_w"] = cat([a["L1_attn_Wg"], levels], axis=0).T
    lay["small_b"] = rows(cat([a["L1_attn_bg"], a["L1_attn_Lparam"][:, :LEVELS].T.reshape(-1)]))
    lay["ln"] = rows(cat([a["L1_attn_ln_g"], a["L1_attn_ln_b"]]))
    lay["moe0_w1"], lay["moe0_w2"] = a["L0_ffn_W1"], a["L0_ffn_W2"]
    lay["moe1_w1"], lay["moe1_w2"], lay["moe1_w3"] = a["L1_cond_W1"], a["L1_cond_W2"], a["L1_cond_W3"]
    lay["const"], lay["levelmask"] = constants()

    nc = _bacc.Bacc("TRN2", target_bir_lowering=False, num_devices=1)
    arrays, d = {}, {}
    for name, v in lay.items():
        v = np.ascontiguousarray(v)
        arrays[f"in_{name}_dram"] = v
        d[name] = nc.dram_tensor(f"in_{name}_dram", v.shape, mybir.dt.from_np(v.dtype), kind="ExternalInput").ap()
    d["out"] = nc.dram_tensor("out_dram", (TILES, P, E), F32, kind="ExternalOutput").ap()
    build(nc, d)
    r = _run(nc, [arrays], core_ids=[0])
    return r.results[0]["out_dram"].reshape(B, S, E)
```

```python
from contextlib import ExitStack

import numpy as np

import concourse.bass as bass
from concourse import mybir

F32 = mybir.dt.float32
BF16 = mybir.dt.bfloat16
I32 = mybir.dt.int32
U32 = mybir.dt.uint32
U8 = mybir.dt.uint8
ALU = mybir.AluOpType
ACT = mybir.ActivationFunctionType
X = mybir.AxisListType.X

P = 128
B, S, E = 32, 32, 128
C = 32
TOK = B * S
TILES = TOK // P
SEQ = P // S
BANK = 512
HALF = 4 * BANK
CH, CD = 16, 8
AH, AD, ROT = 16, 64, 32
LH, LD = 8, 128
LEVELS = (S - 1).bit_length() + 1
NSMALL = LH + LH * LEVELS
EXPERTS = 8
FF0 = 512
FF1 = 256
HID = 512
ROUND = 1.5 * 2.0 ** 23
QMAX = 127.0
MASKED = -3.0e38

CONST, _at = {}, 0
for _name, _width in (("ident", P), ("ones", P), ("upto", P), ("headmask", CH), ("causal", S),
                      ("cos", S), ("sin", S), ("negafter", S), ("diag4", S), ("sign_r", 4),
                      ("sign_l", 4), ("iota", EXPERTS)):
    CONST[_name] = (_at, _at + _width)
    _at += _width
NCONST = _at


def columns(*fields):
    at, where = 0, {}
    for name, width in fields:
        where[name] = (at, at + width)
        at += width
    return where, at


FEAT, NFEAT = columns(("mod_b0", 2), ("mod_b1", 2), ("rms_s0", 1), ("rms_s1", 1), ("rms1", 1), ("sgate", 1), ("quat", 4), ("quat_l", 4),
                      ("quat_all", B), ("router_w0", EXPERTS), ("router_w1", EXPERTS), ("small_w", NSMALL), ("conv", HID // P * 4))
COND, NCOND = columns(("condT", B), ("mod_w0", 2 * E), ("mod_w1", 2 * E), ("genre_w", EXPERTS))
ROWS, NROWS = columns(("router_b0", EXPERTS), ("router_b1", EXPERTS), ("genre_b", EXPERTS), ("small_b", NSMALL), ("ln", 2 * E))


def constants():
    p = np.arange(P)
    t, seq = p % S, p // S
    c = {}
    c["ident"] = np.eye(P)
    c["ones"] = np.ones((P, P))
    c["upto"] = (seq[:, None] == seq[None, :]) & (t[:, None] <= t[None, :])
    c["headmask"] = (p[:, None] // CD) == np.arange(CH)[None, :]
    c["causal"] = np.where(np.arange(S)[None, :] <= t[:, None], 0.0, MASKED)
    inv = (np.float32(1.0) / np.power(np.float32(10000.0),
                                      np.arange(0, ROT, 2, dtype=np.float32) / np.float32(ROT))).astype(np.float32)
    ang = np.arange(S, dtype=np.float32)[:, None] * inv[None, :]
    d = p % AD
    rot = d < ROT
    a = ang[:, d % (ROT // 2)].T.astype(np.float64)
    c["cos"] = np.where(rot[:, None], np.cos(a), 1.0)
    c["sin"] = np.where(rot[:, None], np.where(d[:, None] < ROT // 2, -np.sin(a), np.sin(a)), 0.0)
    c["negafter"] = -1.0 * (t[:, None] > np.arange(S)[None, :])
    c["diag4"] = t[:, None] == np.arange(S)[None, :]
    right = np.array([[1, 1, 1, 1], [-1, 1, -1, 1], [-1, 1, 1, -1], [-1, -1, 1, 1]], float)
    left = np.array([[1, 1, 1, 1], [-1, 1, 1, -1], [-1, -1, 1, 1], [-1, 1, -1, 1]], float)
    comp = np.arange(4)
    conj = np.where((comp[:, None] ^ comp[None, :]) == 0, 1.0, -1.0)
    c["sign_r"] = (right * conj)[p // S]
    c["sign_l"] = left[p // S]
    c["iota"] = np.broadcast_to(np.arange(EXPERTS), (P, EXPERTS))
    table = np.concatenate([np.asarray(c[n], np.float32) for n in CONST], axis=1)
    dist = t[:, None] - np.arange(S)[None, :]
    level = np.where(dist <= 0, 0, np.floor(np.log2(np.maximum(dist, 1))).astype(int) + 1)
    masks = np.stack([(level == n) & (dist >= 0) for n in range(LEVELS)], 1).astype(np.int32)
    return np.ascontiguousarray(table), np.ascontiguousarray(masks.reshape(P, LEVELS * S))


def build(nc, d):
    ctx = ExitStack()
    with ctx:
        def sb(name, shape, dt=F32):
            return ctx.enter_context(nc.sbuf_tensor(name, shape, dt))

        def sem(name):
            return ctx.enter_context(nc.semaphore(name))

        PS = ctx.enter_context(nc.psum_tensor("PS", [P, 2 * HALF], F32))

        def bank(slot, n, lo=0, hi=BANK):
            return PS[:, slot * HALF + n * BANK + lo:slot * HALF + n * BANK + hi]

        const = sb("const", [P, NCONST])
        k = {n: const[:, lo:hi] for n, (lo, hi) in CONST.items()}
        levelmask = sb("levelmask", [P, LEVELS, S], I32)
        xres = sb("xres", [P, TILES, E])
        featT = sb("featT", [P, TOK])
        acc = sb("acc", [P, TILES, E])
        cond_w = [sb(f"cond_w{n}", [P, 4 * E]) for n in range(2)]
        feat, cond, rows = sb("feat", [P, NFEAT]), sb("cond", [C, NCOND]), sb("rows", [P, NROWS])
        part = {n: t[:, lo:hi] for t, where in ((feat, FEAT), (cond, COND), (rows, ROWS)) for n, (lo, hi) in where.items()}
        mod_w, mod_b, rms_s = ([part[f"{n}{l}"] for l in range(2)] for n in ("mod_w", "mod_b", "rms_s"))
        router_w, router_b = ([part[f"{n}{l}"] for l in range(2)] for n in ("router_w", "router_b"))
        condT, genre_w, genre_b, rms1, sgate = part["condT"], part["genre_w"], part["genre_b"], part["rms1"], part["sgate"]
        quat, quat_l, quat_all = part["quat"], part["quat_l"], part["quat_all"]
        small_w, small_b = part["small_w"], part["small_b"]
        conv = part["conv"].rearrange("p (c k) -> p c k", k=4)
        ln = part["ln"].rearrange("p (a e) -> p a e", a=2)
        gain = [sb(f"gain{n}", [P, B]) for n in range(2)]
        shift = [sb(f"shift{n}", [P, B]) for n in range(2)]
        silu = sb("silu", [C, B])
        condx = sb("condx", [C, B, S])
        mask = sb("mask", [P, S // 4], I32)
        maskb = sb("maskb", [P, S])
        wqk = sb("wqk", [P, 2 * AH * AD])
        wv = sb("wv", [P, AH * AD])
        wout = sb("wout", [P, AH * AD // P, E])
        rot_r = sb("rot_r", [P, 4, S])
        rot_l = sb("rot_l", [P, 4, S])
        genre = sb("genre", [P, TILES, EXPERTS])
        ffn_w = [sb(f"ffn_w{n}", [P, HID]) for n in range(2)]
        ffn_q = [sb(f"ffn_q{n}", [P, HID], BF16) for n in range(2)]
        ffn_t = sb("ffn_t", [P, 2, HID])
        wsum = sb("wsum", [P, 2])
        wmean = sb("wmean", [P, 2])
        wscale = sb("wscale", [P, 2])
        last_b = [sb(f"last_b{n}", [P, EXPERTS, E]) for n in range(2)]
        squares = sb("squares", [P, B])
        scratch = sb("scratch", [P, 4])
        eps = sb("eps", [P, 2])
        ident_b = sb("ident_b", [P, P], BF16)
        w_shapes = ([("w1", 1, FF0), ("w2", FF0 // P, E)], [("w1", 1, FF1), ("w2", FF1 // P, FF1), ("w3", FF1 // P, E)])
        hidden_layers = (1, 2)
        ws = [[[sb(f"moe{l}_{n}_{s}", [P, a, b]) for n, a, b in w_shapes[l]] for s in range(2)] for l in range(2)]
        bs = [[sb(f"moe{l}_b_{s}", [P, hidden_layers[l] * (FF0, FF1)[l] // P]) for s in range(2)] for l in range(2)]
        w_loaded = [[sem(f"moe{l}_w_loaded{s}") for s in range(2)] for l in range(2)]

        def load_expert(sp, layer, e, s):
            for (n, a, b), w in zip(w_shapes[layer], ws[layer][s]):
                sp.dma_start(w[:], d[f"moe{layer}_{n}"][bass.ds(e, 1)].rearrange("x (c p) f -> p (x c) f", p=P)).then_inc(w_loaded[layer][s], 16)
            sp.dma_start(bs[layer][s][:], d[f"moe{layer}_b"][bass.ds(e, 1)].rearrange("x p f -> p (x f)")).then_inc(w_loaded[layer][s], 16)

        class Own:
            def __init__(self):
                self.count = 0

            def next(self):
                self.count += 1
                return self.count

        loaded = {n: sem(f"loaded_{n}") for n in ("x", "const", "cond_w0", "small", "attn", "late", "wattn1")}
        prep = sem("prep_step")
        silu_exp, modulated, normed, summed = sem("silu_exp"), sem("modulated"), sem("normed"), sem("summed")

        with nc.Block() as block:
            @block.sync
            def _(sp):
                sp.dma_start(const[:], d["const"]).then_inc(loaded["const"], 16)
                sp.dma_start(xres[:], d["x"].rearrange("(n p) e -> p n e", p=P)).then_inc(loaded["x"], 16)
                sp.dma_start(cond_w[0][:], d["cond_w0"]).then_inc(loaded["cond_w0"], 16)
                sp.dma_start(wqk[:], d["attn0_qk"]).then_inc(loaded["attn"], 16)
                sp.dma_start(wv[:], d["attn0_v"]).then_inc(loaded["attn"], 16)
                sp.dma_start(wout[:], d["attn0_out"].rearrange("(c p) e -> p c e", p=P)).then_inc(loaded["attn"], 16)
                for s in range(2):
                    load_expert(sp, 0, s, s)
                sp.dma_start(last_b[0][:], d["moe0_last_b"].rearrange("p (e f) -> p e f", f=E)).then_inc(loaded["late"], 16)
                for n in range(2):
                    sp.dma_start(ffn_w[n][:], d[f"ffn_w{n}"]).then_inc(loaded["late"], 16)
                sp.dma_start(cond_w[1][:], d["cond_w1"]).then_inc(loaded["late"], 16)
                sp.dma_start(levelmask[:], d["levelmask"].rearrange("p (l s) -> p l s", l=LEVELS)).then_inc(loaded["late"], 16)
                sp.dma_start(last_b[1][:], d["moe1_last_b"].rearrange("p (e f) -> p e f", f=E)).then_inc(loaded["late"], 16)

            @block.scalar
            def _(act):
                act.dma_start(cond[:], d["cond"]).then_inc(loaded["small"], 16)
                act.dma_start(feat[:], d["feat"]).then_inc(loaded["small"], 16)
                act.dma_start(mask[:], d["mask"]).then_inc(loaded["small"], 16)
                act.dma_start(rows[:], d["rows"]).then_inc(loaded["small"], 16)
                act.wait_ge(loaded["small"], 64)
                act.activation(silu[:], condT, ACT.Exp, scale=-1.0).then_inc(silu_exp, 1)

            @block.gpsimd
            def _(pool):
                nc.gpsimd.memset(eps[:, 0:1], 1e-8).then_inc(normed, 1)
                nc.gpsimd.memset(eps[:, 1:2], -0.5).then_inc(normed, 1)
                nc.gpsimd.memset(acc[:], 0.0)
                pool.wait_ge(summed, 2)
                pool.wait_ge(normed, 2)
                nc.gpsimd.tensor_tensor(scratch[:, 2:4], scratch[:, 0:2], eps[:, 0:1].to_broadcast([P, 2]), ALU.add).then_inc(normed, 1)
                pool.wait_ge(normed, 3)
                nc.gpsimd.tensor_tensor(scratch[:, 0:2], scratch[:, 2:4], eps[:, 1:2].to_broadcast([P, 2]), ALU.pow).then_inc(normed, 1)

            @block.vector
            def _(dve):
                own_prep = Own()
                dve.wait_ge(loaded["small"], 64)
                nc.vector.tensor_copy(condx[:], condT.unsqueeze(2).to_broadcast([C, B, S]))
                nc.vector.tensor_tensor_reduce(out=squares[:, 0:4], in0=quat, in1=quat, scale=1.0, scalar=0.0,
                                               op0=ALU.mult, op1=ALU.add, accum_out=scratch[:, 0:1]).then_inc(summed, 1)
                dve.wait_ge(summed, 1)
                nc.vector.tensor_tensor_reduce(out=squares[:], in0=quat_all, in1=quat_all, scale=1.0, scalar=0.0,
                                               op0=ALU.mult, op1=ALU.add, accum_out=scratch[:, 1:2]).then_inc(summed, 1)
                dve.wait_ge(silu_exp, 1)
                nc.vector.tensor_scalar(silu[:], silu[:], 1.0, None, ALU.add).then_inc(prep, 1)
                dve.wait_ge(prep, own_prep.next())
                nc.vector.reciprocal(silu[:], silu[:]).then_inc(prep, 1)
                dve.wait_ge(prep, own_prep.next())
                nc.vector.tensor_tensor(silu[:], silu[:], condT, ALU.mult).then_inc(silu_exp, 1)
                nc.vector.tensor_scalar(maskb[:], mask[:].bitcast(U8), MASKED, None, ALU.mult)
                nc.vector.tensor_scalar(router_w[1], router_w[1], rms1, None, ALU.mult)
                nc.vector.tensor_tensor(genre_b, genre_b, router_b[1], ALU.add).then_inc(prep, 1)
                own_prep.next()
                dve.wait_ge(loaded["const"], 16)
                dve.wait_ge(normed, 4)
                nc.vector.scalar_tensor_tensor(out=quat, in0=quat, scalar=scratch[:, 0:1], in1=k["sign_r"],
                                               op0=ALU.mult, op1=ALU.mult).then_inc(prep, 1)
                own_prep.next()
                nc.vector.scalar_tensor_tensor(out=quat_l, in0=quat_l, scalar=scratch[:, 1:2], in1=k["sign_l"],
                                               op0=ALU.mult, op1=ALU.mult).then_inc(prep, 1)
                dve.wait_ge(prep, own_prep.next())
                nc.vector.tensor_scalar(quat, quat, sgate, None, ALU.mult).then_inc(prep, 1)
                dve.wait_ge(prep, own_prep.next())
                for q, r in ((quat, rot_r), (quat_l, rot_l)):
                    nc.vector.tensor_tensor(r[:], k["diag4"].unsqueeze(1).to_broadcast([P, 4, S]),
                                            q.unsqueeze(2).to_broadcast([P, 4, S]), ALU.mult)
                nc.vector.tensor_copy(ident_b[:], k["ident"])
                dve.wait_ge(modulated, 1)
                for n in range(2):
                    nc.vector.tensor_scalar(shift[n][:], bank(0, 0, 64 * n, 64 * n + 32), mod_b[n][:, 0:1], None, ALU.add)
                    nc.vector.tensor_scalar(gain[n][:], bank(0, 0, 64 * n + 32, 64 * n + 64), mod_b[n][:, 1:2], 1.0, ALU.add, ALU.add).then_inc(prep, 1)
                    own_prep.next()
                dve.wait_ge(prep, own_prep.count)
                for n in range(2):
                    nc.vector.tensor_scalar(gain[n][:], gain[n][:], rms_s[n], None, ALU.mult)
                nc.vector.tensor_tensor(genre[:], bank(0, 1, 0, 64).rearrange("p (n e) -> p n e", e=EXPERTS),
                                        genre_b.unsqueeze(1).to_broadcast([P, TILES, EXPERTS]), ALU.add)

            @block.tensor
            def _(pe):
                pe.wait_ge(silu_exp, 2)
                for n in range(2):
                    nc.tensor.matmul(bank(0, 0, 64 * n, 64 * n + 32), mod_w[n][:, 0:E], silu[:], start=True, stop=True)
                    nc.tensor.matmul(bank(0, 0, 64 * n + 32, 64 * n + 64), mod_w[n][:, E:2 * E], silu[:], start=True, stop=True)
                for n in range(TILES):
                    mm = nc.tensor.matmul(bank(0, 1, 8 * n, 8 * n + 8), condx[:, SEQ * n:SEQ * n + SEQ, :], genre_w, start=True, stop=True)
                mm.then_inc(modulated, 1)
                pe.wait_ge(loaded["x"], 16)
                pe.wait_ge(loaded["cond_w0"], 16)

        def run_in_time_order(period, steps):
            for _, n, j in sorted((period * n + steps[j][0], n, j) for n in range(TILES) for j in range(len(steps))):
                steps[j][1](n)

        def full(number, lo=0, hi=BANK):
            return PS[:, number * BANK + lo:number * BANK + hi]

        CS = 2
        cxs = [sb(f"cond_xs{s}", [P, P]) for s in range(CS)]
        cqkv = [sb(f"cond_qkv{s}", [P, 3 * P]) for s in range(CS)]
        ckbd = [sb(f"cond_kbd{s}", [P, CH, P]) for s in range(CS)]
        csm = [sb(f"cond_sm{s}", [P, CH, S]) for s in range(CS)]
        cptbd = [sb(f"cond_ptbd{s}", [P, CH, P]) for s in range(CS)]
        cmx, csums, crec = ([sb(f"cond_{n}{s}", [P, CH]) for s in range(CS)] for n in ("mx", "sums", "rec"))
        co, coT, czn = ([sb(f"cond_{n}{s}", [P, P]) for s in range(CS)] for n in ("o", "oT", "zn"))
        cst = [sb(f"cond_st{s}", [P, 4]) for s in range(CS)]
        c_xT_ps, c_xT_ready, c_qkv_ps, c_qkv_ready = sem("cond_xT_ps"), sem("cond_xT_ready"), sem("cond_qkv_ps"), sem("cond_qkv_ready")
        c_kbd_ready, c_scores_ps, c_scores_ready = sem("cond_kbd_ready"), sem("cond_scores_ps"), sem("cond_scores_ready")
        c_probs_ready, c_probsT_ready, c_o_ps, c_o_ready = sem("cond_probs_ready"), sem("cond_probsT_ready"), sem("cond_o_ps"), sem("cond_o_ready")
        c_oT_ps, c_oT_ready, c_z_ps, c_square_ready = sem("cond_oT_ps"), sem("cond_oT_ready"), sem("cond_z_ps"), sem("cond_square_ready")
        c_rstd_ready, c_zn_ready, c_znT_ps, c_done = sem("cond_rstd_ready"), sem("cond_zn_ready"), sem("cond_znT_ps"), sem("cond_done")
        c_zeroed = sem("cond_zeroed")

        def cond_pool(pool, layer, at, own, own_sem):
            base = layer * TILES

            def spread_keys(n):
                s = n % CS
                pool.wait_ge(c_qkv_ready, base + n + 1)
                nc.gpsimd.tensor_tensor(ckbd[s][:], cqkv[s][:, P:2 * P].unsqueeze(1).to_broadcast([P, CH, P]),
                                        k["headmask"].unsqueeze(2).to_broadcast([P, CH, P]), ALU.mult).then_inc(c_kbd_ready, 1)

            def inverse_rms(n):
                s = n % CS
                pool.wait_ge(c_square_ready, base + n + 1)
                nc.gpsimd.tensor_scalar(cst[s][:, 1:2], cst[s][:, 0:1], 1.0 / E, 1e-6, ALU.mult, ALU.add).then_inc(own_sem, 1)
                pool.wait_ge(own_sem, own.next())
                nc.gpsimd.tensor_tensor(cst[s][:, 2:3], cst[s][:, 1:2], eps[:, 1:2], ALU.pow).then_inc(c_rstd_ready, 1)

            return [(at["c_spread_keys"], spread_keys), (at["c_inverse_rms"], inverse_rms)]

        def cond_tensor(pe, layer, at, ready=None):
            base, w = layer * TILES, cond_w[layer]

            def transpose_x(n):
                s = n % CS
                if ready is not None:
                    pe.wait_ge(ready, n + 1)
                if base + n >= CS:
                    pe.wait_ge(c_done, base + n - CS + 1)
                nc.tensor.transpose(full(s, 0, P), xres[:, n, :], k["ident"]).then_inc(c_xT_ps, 1)

            def project(n):
                s = n % CS
                pe.wait_ge(c_xT_ready, base + n + 1)
                nc.tensor.matmul(full(s, P, 2 * P), w[:, 0:E], cxs[s][:], start=True, stop=True)
                nc.tensor.matmul(full(s, 2 * P, 3 * P), w[:, E:2 * E], cxs[s][:], start=True, stop=True)
                nc.tensor.matmul(full(s, 3 * P, 4 * P), cxs[s][:], w[:, 2 * E:3 * E], start=True, stop=True).then_inc(c_qkv_ps, 1)

            def scores(n):
                s = n % CS
                pe.wait_ge(c_kbd_ready, base + n + 1)
                for b in range(SEQ):
                    mm = nc.tensor.matmul(full(s)[S * b:S * b + S, :], cqkv[s][:, S * b:S * b + S],
                                          ckbd[s][:, :, S * b:S * b + S], start=True, stop=True)
                mm.then_inc(c_scores_ps, 1)

            def times_values(n):
                s = n % CS
                pe.wait_ge(c_probsT_ready, base + n + 1)
                for h in range(CH):
                    mm = nc.tensor.matmul(full(s, CD * h, CD * h + CD), cptbd[s][:, h, :],
                                          cqkv[s][:, 2 * P + CD * h:2 * P + CD * h + CD], start=True, stop=True)
                mm.then_inc(c_o_ps, 1)

            def transpose_o(n):
                s = n % CS
                pe.wait_ge(c_o_ready, base + n + 1)
                nc.tensor.transpose(full(s, P, 2 * P), co[s][:], k["ident"]).then_inc(c_oT_ps, 1)

            def project_o(n):
                s = n % CS
                pe.wait_ge(c_oT_ready, base + n + 1)
                nc.tensor.matmul(full(s, 2 * P, 3 * P), coT[s][:], w[:, 3 * E:4 * E], start=True, stop=True).then_inc(c_z_ps, 1)

            def transpose_z(n):
                s = n % CS
                pe.wait_ge(c_zn_ready, base + n + 1)
                nc.tensor.transpose(full(s, 3 * P, 4 * P), czn[s][:], k["ident"]).then_inc(c_znT_ps, 1)

            return [(at["c_transpose_x"], transpose_x), (at["c_project"], project), (at["c_scores"], scores),
                    (at["c_times_values"], times_values), (at["c_transpose_o"], transpose_o), (at["c_project_o"], project_o),
                    (at["c_transpose_z"], transpose_z)]

        def cond_scalar(act, layer, at):
            base = layer * TILES

            def copy_x(n):
                s = n % CS
                act.wait_ge(c_xT_ps, base + n + 1)
                nc.scalar.activation(cxs[s][:], full(s, 0, P), ACT.Copy).then_inc(c_xT_ready, 1)

            def copy_qkv(n):
                s = n % CS
                act.wait_ge(c_qkv_ps, base + n + 1)
                nc.scalar.activation(cqkv[s][:], full(s, P, 4 * P), ACT.Copy).then_inc(c_qkv_ready, 1)

            def exponentials(n):
                s = n % CS
                act.wait_ge(c_scores_ready, base + n + 1)
                nc.scalar.activation(csm[s][:], csm[s][:], ACT.Exp).then_inc(c_probs_ready, 1)

            def copy_oT(n):
                s = n % CS
                act.wait_ge(c_oT_ps, base + n + 1)
                nc.scalar.activation(coT[s][:], full(s, P, 2 * P), ACT.Copy).then_inc(c_oT_ready, 1)

            def squares(n):
                s = n % CS
                act.wait_ge(c_z_ps, base + n + 1)
                nc.scalar.activation(czn[s][:], full(s, 2 * P, 3 * P), ACT.Square, accum_out=cst[s][:, 0:1]).then_inc(c_square_ready, 1)

            def normalise(n):
                s = n % CS
                act.wait_ge(c_rstd_ready, base + n + 1)
                nc.scalar.activation(czn[s][:], full(s, 2 * P, 3 * P), ACT.Copy, scale=cst[s][:, 2:3]).then_inc(c_zn_ready, 1)

            def modulate(n):
                s = n % CS
                act.wait_ge(c_znT_ps, base + n + 1)
                for b in range(SEQ):
                    q = SEQ * n + b
                    ins = nc.scalar.activation(featT[:, P * n + S * b:P * n + S * b + S], full(s, 3 * P + S * b, 3 * P + S * b + S), ACT.Identity,
                                               scale=gain[layer][:, q:q + 1], bias=shift[layer][:, q:q + 1])
                ins.then_inc(c_done, 1)

            return [(at["c_modulate"], modulate), (at["c_copy_x"], copy_x), (at["c_copy_qkv"], copy_qkv), (at["c_exponentials"], exponentials),
                    (at["c_copy_oT"], copy_oT), (at["c_squares"], squares), (at["c_normalise"], normalise)]

        def cond_vector(dve, layer, at, own, own_sem):
            base = layer * TILES
            scale = float(CD) ** -0.5

            def softmax_in(n):
                s = n % CS
                dve.wait_ge(c_scores_ps, base + n + 1)
                nc.vector.scalar_tensor_tensor(out=csm[s][:], in0=full(s).rearrange("p (h t) -> p h t", t=S), scalar=scale,
                                               in1=maskb[:].unsqueeze(1).to_broadcast([P, CH, S]),
                                               op0=ALU.mult, op1=ALU.add).then_inc(own_sem, 1)
                dve.wait_ge(own_sem, own.next())
                nc.vector.tensor_reduce(cmx[s][:], csm[s][:], X, ALU.max).then_inc(own_sem, 1)
                dve.wait_ge(own_sem, own.next())
                nc.vector.tensor_tensor(csm[s][:], csm[s][:], cmx[s][:].unsqueeze(2).to_broadcast([P, CH, S]), ALU.subtract).then_inc(c_scores_ready, 1)

            def turn(n):
                s = n % CS
                dve.wait_ge(c_probs_ready, base + n + 1)
                for b in range(SEQ):
                    last = nc.vector.transpose(cptbd[s][S * b:S * b + S, :, S * b:S * b + S], csm[s][S * b:S * b + S, :, :])
                last.then_inc(c_probsT_ready, 1)
                nc.vector.tensor_reduce(csums[s][:], csm[s][:], X, ALU.add).then_inc(own_sem, 1)
                dve.wait_ge(own_sem, own.next())
                nc.vector.reciprocal(crec[s][:], csums[s][:]).then_inc(own_sem, 1)
                dve.wait_ge(own_sem, own.next())

            def divide(n):
                s = n % CS
                dve.wait_ge(c_o_ps, base + n + 1)
                nc.vector.tensor_tensor(co[s][:].rearrange("p (h c) -> p h c", c=CD), full(s, 0, P).rearrange("p (h c) -> p h c", c=CD),
                                        crec[s][:].unsqueeze(2).to_broadcast([P, CH, CD]), ALU.mult).then_inc(c_o_ready, 1)

            return [(at["c_softmax_in"], softmax_in), (at["c_turn"], turn), (at["c_divide"], divide)]

        logits = sb("logits", [P, TILES, EXPERTS])

        def attention0():
            with ExitStack() as scope:
                def lsb(name, shape, dt=F32):
                    return scope.enter_context(nc.sbuf_tensor("rot_" + name, shape, dt))

                def lsem(name):
                    return sem("rot_" + name)

                NC_ = AH * AD // P
                qk, sh = lsb("qk", [P, 2 * NC_, P]), lsb("sh", [P, 2 * NC_, P])
                v = lsb("v", [P, AH * AD])
                sm = lsb("sm", [P, AH, S])
                ptbd = lsb("ptbd", [P, AH, P])
                oT = lsb("oT", [P, NC_, P])
                mx, sums, rec = lsb("mx", [P, AH]), lsb("sums", [P, AH]), lsb("rec", [P, AH])
                mxT, mr1 = lsb("xT", [P, P]), lsb("r1", [P, P])
                zeroed, dve_step, pool_step = lsem("zeroed"), lsem("dve_step"), lsem("pool_step")
                q_ps, k_ps, v_ps = lsem("q_ps"), lsem("k_ps"), lsem("v_ps")
                qk_copied, shuffled, rotated, qk_ready = lsem("qk_copied"), lsem("shuffled"), lsem("rotated"), lsem("qk_ready")
                masked = lsem("masked")
                v_ready, low_ps, high_ps, low_read, high_read = lsem("v_ready"), lsem("low_ps"), lsem("high_ps"), lsem("low_read"), lsem("high_read")
                scores_ready, probs_ready, probsT_ready = lsem("scores_ready"), lsem("probs_ready"), lsem("probsT_ready")
                oT_ps, oT_ready, out_ps, x_ready = lsem("oT_ps"), lsem("oT_ready"), lsem("out_ps"), lsem("x_ready")
                xT_ps, xT_ready, r1_ps, r1_ready = lsem("xT_ps"), lsem("xT_ready"), lsem("r1_ps"), lsem("r1_ready")
                f_ps, f_ready, logit_ps, logit_ready = lsem("f_ps"), lsem("f_ready"), lsem("logit_ps"), lsem("logit_ready")
                scale = float(AD) ** -0.5
                swap = [(n + ROT // 2) % ROT for n in range(ROT)]
                PERIOD = 29.85
                at = dict(c_transpose_x=0, c_spread_keys=0.29, c_project=7.1, c_copy_x=12.19, c_copy_qkv=12.4,
                          c_scores=14.24, c_softmax_in=19.57, c_turn=28.85, c_exponentials=37.31,
                          c_times_values=40.62, c_divide=45.23, c_inverse_rms=49.38, c_transpose_o=51.01,
                          c_project_o=51.75, c_transpose_z=53.29, c_copy_oT=57.03, c_squares=58.79,
                          rotate_parts_0=60.65, c_normalise=64.57, queries=65.26, c_modulate=65.67,
                          partner_rows_0=69.04, rotate_parts_1=72.14, keys=72.27, partner_rows_1=74.42,
                          copy_queries=76.44, mask_scores=80.03, add_parts_0=81.57, add_parts_1=81.78,
                          copy_keys=86.59, scores=87.65, softmax_in=89.46, take_scores_0=97.5, values=98.34,
                          take_scores_1=100.48, softmax_out=102.77, times_values=109.05, copy_values=111.58,
                          output=111.96, add_output=112.04, transpose_x=113.58, exponentials=115.11, copy_oT=116.97,
                          rotate_right=118.24, take_logits=119.13, rotate_left=121.06, route=125.2, copy_xT=126.5,
                          copy_right=128.12, copy_left=129.62)
                QB, KB, VB = 2, 4, 6
                place = [8 * (h // 8) + 4 * (h % 2) + (h // 2) % 4 for h in range(AH)]

                with nc.Block() as block:
                    @block.gpsimd
                    def _(pool):
                        for s in range(CS):
                            nc.gpsimd.memset(cptbd[s][:], 0.0).then_inc(c_zeroed, 1)
                        nc.gpsimd.memset(ptbd[:], 0.0).then_inc(zeroed, 1)

                        def rotate_parts(part):
                            def step(n):
                                pool.wait_ge(shuffled, 2 * n + part + 1)
                                for buf, table in ((sh, "sin"), (qk, "cos")):
                                    at = buf[:, NC_ * part:NC_ * part + NC_, :].rearrange("p c (b t) -> p (c b) t", t=S)
                                    ins = nc.gpsimd.tensor_tensor(at, at, k[table].unsqueeze(1).to_broadcast([P, NC_ * SEQ, S]), ALU.mult)
                                ins.then_inc(rotated, 1)
                            return step

                        def mask_scores(n):
                            pool.wait_ge(high_read, n + 1)
                            nc.gpsimd.tensor_tensor(sm[:], sm[:], k["causal"].unsqueeze(1).to_broadcast([P, AH, S]), ALU.add).then_inc(masked, 1)

                        run_in_time_order(PERIOD, cond_pool(pool, 0, at, Own(), pool_step) + [(at["rotate_parts_0"], rotate_parts(0)), (at["rotate_parts_1"], rotate_parts(1)), (at["mask_scores"], mask_scores)])

                    @block.tensor
                    def _(pe):
                        def queries(n):
                            pe.wait_ge(c_done, n + 1)
                            if n:
                                pe.wait_ge(low_read, n)
                            for c in range(NC_):
                                mm = nc.tensor.matmul(full(QB + c // 4, P * (c % 4), P * (c % 4) + P), wqk[:, P * c:P * c + P], featT[:, P * n:P * n + P], start=True, stop=True)
                            mm.then_inc(q_ps, 1)

                        def keys(n):
                            if n:
                                pe.wait_ge(high_read, n)
                            for c in range(NC_):
                                mm = nc.tensor.matmul(full(KB + c // 4, P * (c % 4), P * (c % 4) + P), wqk[:, P * (NC_ + c):P * (NC_ + c) + P], featT[:, P * n:P * n + P], start=True, stop=True)
                            mm.then_inc(k_ps, 1)

                        def values(n):
                            if n:
                                pe.wait_ge(logit_ready, n)
                            for c in range(2):
                                mm = nc.tensor.matmul(full(VB + c), featT[:, P * n:P * n + P], wv[:, BANK * c:BANK * c + BANK], start=True, stop=True)
                            mm.then_inc(v_ps, 1)

                        def scores(n):
                            pe.wait_ge(qk_ready, 2 * n + 2)
                            for h in range(AH):
                                r, c = AD * (h % 2), h // 2
                                at, col = (QB if h < 8 else KB) + h % 2, P * (c % 4)
                                mm = nc.tensor.matmul(full(at, col, col + P), qk[r:r + AD, c, :], qk[r:r + AD, NC_ + c, :], start=True, stop=True)
                                if h == 7:
                                    mm.then_inc(low_ps, 1)
                            mm.then_inc(high_ps, 1)

                        def times_values(n):
                            pe.wait_ge(probsT_ready, n + 1)
                            pe.wait_ge(v_ready, n + 1)
                            for h in range(AH):
                                r, c = AD * (h % 2), h // 2
                                mm = nc.tensor.matmul(full(VB + c // 4, P * (c % 4), P * (c % 4) + P)[r:r + AD, :], v[:, AD * h:AD * h + AD], ptbd[:, place[h], :], start=True, stop=True)
                            mm.then_inc(oT_ps, 1)

                        def output(n):
                            pe.wait_ge(oT_ready, n + 1)
                            for c in range(NC_):
                                mm = nc.tensor.matmul(full(VB, 0, E), oT[:, c, :], wout[:, c, :], start=(c == 0), stop=(c == NC_ - 1))
                            mm.then_inc(out_ps, 1)

                        def transpose_x(n):
                            pe.wait_ge(x_ready, n + 1)
                            nc.tensor.transpose(full(VB, P, 2 * P), xres[:, n, :], k["ident"]).then_inc(xT_ps, 1)

                        def rotate_right(n):
                            pe.wait_ge(xT_ready, n + 1)
                            nc.tensor.matmul(full(VB, 2 * P, 3 * P), rot_r[:].rearrange("p a s -> p (a s)"), mxT[:], start=True, stop=True).then_inc(r1_ps, 1)

                        def rotate_left(n):
                            pe.wait_ge(r1_ready, n + 1)
                            nc.tensor.matmul(full(VB, 3 * P, 4 * P), rot_l[:].rearrange("p a s -> p (a s)"), mr1[:], start=True, stop=True).then_inc(f_ps, 1)

                        def route(n):
                            pe.wait_ge(f_ready, n + 1)
                            nc.tensor.matmul(full(VB + 1, 0, EXPERTS), featT[:, P * n:P * n + P], router_w[0], start=True, stop=True).then_inc(logit_ps, 1)

                        pe.wait_ge(loaded["attn"], 48)
                        run_in_time_order(PERIOD, cond_tensor(pe, 0, at) + [
                            (at["queries"], queries), (at["keys"], keys), (at["scores"], scores), (at["values"], values), (at["times_values"], times_values), (at["output"], output),
                            (at["transpose_x"], transpose_x), (at["rotate_right"], rotate_right), (at["rotate_left"], rotate_left), (at["route"], route)])

                    @block.scalar
                    def _(act):
                        def copy_queries(n):
                            act.wait_ge(q_ps, n + 1)
                            if n:
                                act.wait_ge(high_ps, n)
                            for c in range(2):
                                ins = nc.scalar.activation(qk[:, 4 * c:4 * c + 4, :].rearrange("p c t -> p (c t)"), full(QB + c), ACT.Copy)
                            ins.then_inc(qk_copied, 1)

                        def copy_keys(n):
                            act.wait_ge(k_ps, n + 1)
                            for c in range(2):
                                ins = nc.scalar.activation(qk[:, NC_ + 4 * c:NC_ + 4 * c + 4, :].rearrange("p c t -> p (c t)"), full(KB + c), ACT.Copy)
                            ins.then_inc(qk_copied, 1)

                        def copy_values(n):
                            act.wait_ge(v_ps, n + 1)
                            for c in range(2):
                                ins = nc.scalar.activation(v[:, BANK * c:BANK * c + BANK], full(VB + c), ACT.Copy)
                            ins.then_inc(v_ready, 1)

                        def take_scores(g):
                            def step(n):
                                if n and g == 0:
                                    act.wait_ge(probsT_ready, n)
                                act.wait_ge(low_ps if g == 0 else high_ps, n + 1)
                                src = PS[:, (QB + 2 * g) * BANK:(QB + 2 * g + 2) * BANK].rearrange("p (h t) -> p h t", t=P)
                                for b in range(SEQ):
                                    r = slice(S * b, S * b + S)
                                    ins = nc.scalar.activation(sm[r, 8 * g:8 * g + 8, :], src[r][:, :, S * b:S * b + S], ACT.Copy, scale=scale)
                                ins.then_inc(low_read if g == 0 else high_read, 1)
                            return step

                        def exponentials(n):
                            act.wait_ge(scores_ready, n + 1)
                            nc.scalar.activation(sm[:], sm[:], ACT.Exp).then_inc(probs_ready, 1)

                        def copy_oT(n):
                            act.wait_ge(oT_ps, n + 1)
                            for c in range(2):
                                ins = nc.scalar.activation(oT[:, 4 * c:4 * c + 4, :].rearrange("p c t -> p (c t)"), full(VB + c), ACT.Copy)
                            ins.then_inc(oT_ready, 1)

                        def copy_xT(n):
                            act.wait_ge(xT_ps, n + 1)
                            nc.scalar.activation(mxT[:], full(VB, P, 2 * P), ACT.Copy).then_inc(xT_ready, 1)

                        def copy_right(n):
                            act.wait_ge(r1_ps, n + 1)
                            nc.scalar.activation(mr1[:], full(VB, 2 * P, 3 * P), ACT.Copy).then_inc(r1_ready, 1)

                        def copy_left(n):
                            act.wait_ge(f_ps, n + 1)
                            nc.scalar.activation(featT[:, P * n:P * n + P], full(VB, 3 * P, 4 * P), ACT.Copy).then_inc(f_ready, 1)

                        run_in_time_order(PERIOD, cond_scalar(act, 0, at) + [
                            (at["copy_queries"], copy_queries), (at["copy_keys"], copy_keys), (at["copy_values"], copy_values), (at["take_scores_0"], take_scores(0)), (at["take_scores_1"], take_scores(1)), (at["exponentials"], exponentials), (at["copy_oT"], copy_oT),
                            (at["copy_xT"], copy_xT), (at["copy_right"], copy_right), (at["copy_left"], copy_left)])

                    @block.vector
                    def _(dve):
                        own = Own()

                        def partner_rows(part):
                            def step(n):
                                dve.wait_ge(qk_copied, 2 * n + part + 1)
                                here = slice(NC_ * part, NC_ * part + NC_)
                                nc.vector.stream_shuffle(sh[:, here, :], qk[:, here, :], swap).then_inc(shuffled, 1)
                            return step

                        def add_parts(part):
                            def step(n):
                                dve.wait_ge(rotated, 2 * n + part + 1)
                                here = slice(NC_ * part, NC_ * part + NC_)
                                nc.vector.tensor_tensor(qk[:, here, :], qk[:, here, :], sh[:, here, :], ALU.add).then_inc(qk_ready, 1)
                            return step

                        def softmax_in(n):
                            dve.wait_ge(masked, n + 1)
                            nc.vector.tensor_reduce(mx[:], sm[:], X, ALU.max).then_inc(dve_step, 1)
                            dve.wait_ge(dve_step, own.next())
                            nc.vector.tensor_tensor(sm[:], sm[:], mx[:].unsqueeze(2).to_broadcast([P, AH, S]), ALU.subtract).then_inc(scores_ready, 1)

                        def softmax_out(n):
                            dve.wait_ge(probs_ready, n + 1)
                            nc.vector.tensor_reduce(sums[:], sm[:], X, ALU.add).then_inc(dve_step, 1)
                            dve.wait_ge(dve_step, own.next())
                            nc.vector.reciprocal(rec[:], sums[:]).then_inc(dve_step, 1)
                            dve.wait_ge(dve_step, own.next())
                            nc.vector.tensor_tensor(sm[:], sm[:], rec[:].unsqueeze(2).to_broadcast([P, AH, S]), ALU.mult).then_inc(dve_step, 1)
                            dve.wait_ge(dve_step, own.next())
                            if n:
                                dve.wait_ge(oT_ps, n)
                            for b in range(SEQ):
                                last = nc.vector.transpose(ptbd[S * b:S * b + S, :, S * b:S * b + S], sm[S * b:S * b + S, :, :])
                            last.then_inc(probsT_ready, 1)

                        def add_output(n):
                            dve.wait_ge(out_ps, n + 1)
                            nc.vector.tensor_tensor(xres[:, n, :], xres[:, n, :], full(VB, 0, E), ALU.add).then_inc(x_ready, 1)

                        def take_logits(n):
                            dve.wait_ge(logit_ps, n + 1)
                            nc.vector.tensor_tensor(logits[:, n, :], full(VB + 1, 0, EXPERTS), router_b[0], ALU.add).then_inc(logit_ready, 1)

                        dve.wait_ge(c_zeroed, CS)
                        dve.wait_ge(zeroed, 1)
                        run_in_time_order(PERIOD, cond_vector(dve, 0, at, own, dve_step) + [
                            (at["partner_rows_0"], partner_rows(0)), (at["partner_rows_1"], partner_rows(1)), (at["add_parts_0"], add_parts(0)), (at["add_parts_1"], add_parts(1)),
                            (at["softmax_in"], softmax_in), (at["softmax_out"], softmax_out),
                            (at["add_output"], add_output), (at["take_logits"], take_logits)])

        def experts(layer):
            pre = f"moe{layer}_"
            ff = (FF0, FF1)[layer]
            nf = ff // P
            with ExitStack() as own_scope:
                def lsb(name, shape, dt=F32):
                    return own_scope.enter_context(nc.sbuf_tensor(pre + name, shape, dt))

                def lsem(name):
                    return ctx.enter_context(nc.semaphore(pre + name))

                target = (xres, acc)[layer]
                top = lsb("top", [P, TILES, 8])
                topi = lsb("topi", [P, TILES, 8], U32)
                topf = lsb("topf", [P, TILES, 2])
                chosen = lsb("chosen", [P, 2, TILES, EXPERTS])
                weight = lsb("weight", [P, TILES, EXPERTS])
                total, rtotal = lsb("total", [P, TILES]), lsb("rtotal", [P, TILES])
                st = lsb("st", [P, 3, TILES])
                sq = lsb("sq", [P, TILES, E])
                HALVES = TOK // BANK
                W, Bs = ws[layer], bs[layer]
                hid = [lsb(f"hid{h}", [P, nf, BANK]) for h in range(HALVES)]
                hid2 = [lsb(f"hid2{h}", [P, nf, BANK]) for h in range(HALVES)] if layer else hid
                w_free, hid_ps, hid_ready = lsem("w_free"), lsem("hid_ps"), lsem("hid_ready")
                out_ps, added, biased = lsem("out_ps"), lsem("added"), lsem("biased")
                g_step, exp_in, exp_out = lsem("gate_step"), lsem("exp_in"), lsem("exp_out")
                if layer:
                    xT_ps, xT_ready, logit_ps, rms_ready = lsem("xT_ps"), lsem("xT_ready"), lsem("logit_ps"), lsem("rms_ready")
                    mag_ready, mag_ps, pool_step, square_ready = lsem("mag_ready"), lsem("mag_ps"), lsem("pool_step"), lsem("square_ready")
                UNITS = 2 * HALVES * nf if layer else HALVES * nf
                NB = 4

                with nc.Block() as block:
                    @block.sync
                    def _(sp):
                        sp.sem_inc(hid_ready, NB)
                        sp.sem_inc(out_ps, HALVES)
                        sp.sem_inc(added, HALVES)
                        with sp.Fori(1, EXPERTS // 2) as i:
                            for s in range(2):
                                sp.wait_ge(w_free, 2 * i + s - 1)
                                load_expert(sp, layer, 2 * i + s, s)
                        if layer == 0:
                            for s in range(2):
                                load_expert(sp, 1, s, s)
                            sp.dma_start(wqk[:], d["attn1_qk"]).then_inc(loaded["wattn1"], 16)
                            sp.dma_start(wv[:], d["attn1_v"]).then_inc(loaded["wattn1"], 16)
                            sp.dma_start(wout[:], d["attn1_out"].rearrange("(c p) e -> p c e", p=P)).then_inc(loaded["wattn1"], 16)

                    if layer:
                        @block.gpsimd
                        def _(pool):
                            pool.wait_ge(square_ready, 1)
                            nc.gpsimd.tensor_scalar(st[:, 1, :], st[:, 0, :], 1.0 / E, 1e-6, ALU.mult, ALU.add).then_inc(pool_step, 1)
                            pool.wait_ge(pool_step, 1)
                            nc.gpsimd.tensor_tensor(st[:, 2, :], st[:, 1, :], eps[:, 1:2].to_broadcast([P, TILES]), ALU.pow).then_inc(rms_ready, 1)

                    @block.tensor
                    def _(pe):
                        if layer:
                            for n in range(TILES):
                                nc.tensor.transpose(full(n // 2, P * (n % 2), P * (n % 2) + P), xres[:, n, :], k["ident"]).then_inc(xT_ps, 1)
                            for n in range(TILES):
                                pe.wait_ge(xT_ready, n // 2 + 1)
                                mm = nc.tensor.matmul(full(6, EXPERTS * n, EXPERTS * n + EXPERTS), featT[:, P * n:P * n + P], router_w[1], start=True, stop=True)
                            mm.then_inc(logit_ps, 1)
                            pe.wait_ge(mag_ready, 2)
                            nc.tensor.matmul(full(7, 0, 2), k["ones"], wsum[:], start=True, stop=True).then_inc(mag_ps, 1)
                        with pe.Fori(0, EXPERTS // 2) as i:
                            for s in range(2):
                                e = 2 * i + s
                                pe.wait_ge(w_loaded[layer][s], 16 * (len(w_shapes[layer]) + 1) * (i + 1))
                                u = 0
                                for h in range(HALVES):
                                    for f in range(nf):
                                        pe.wait_ge(hid_ready, UNITS * e + u + 1)
                                        nc.tensor.matmul(bank(0, u % NB), W[s][0][:, 0, P * f:P * f + P], featT[:, BANK * h:BANK * h + BANK], start=True, stop=True).then_inc(hid_ps, 1)
                                        u += 1
                                if layer:
                                    for h in range(HALVES):
                                        pe.wait_ge(hid_ready, UNITS * e + NB + nf * (h + 1))
                                        for f in range(nf):
                                            pe.wait_ge(hid_ready, UNITS * e + u + 1)
                                            for c in range(nf):
                                                mm = nc.tensor.matmul(bank(0, u % NB), W[s][1][:, c, P * f:P * f + P], hid[h][:, c, :], start=(c == 0), stop=(c == nf - 1))
                                            mm.then_inc(hid_ps, 1)
                                            u += 1
                                for h in range(HALVES):
                                    pe.wait_ge(hid_ready, UNITS * e + NB + (UNITS - nf * HALVES) + nf * (h + 1))
                                    pe.wait_ge(added, HALVES * e + h + 1)
                                    for j in range(4):
                                        for c in range(nf):
                                            mm = nc.tensor.matmul(bank(1, h, E * j, E * j + E), hid2[h][:, c, P * j:P * j + P], W[s][-1][:, c, :], start=(c == 0), stop=(c == nf - 1))
                                    mm.then_inc(out_ps, 1)
                                pe.wait_ge(out_ps, HALVES * e + 2 * HALVES)
                                pe.sem_inc(w_free, 1)

                    @block.scalar
                    def _(act):
                        if layer:
                            for h in range(TILES // 2):
                                act.wait_ge(xT_ps, 2 * h + 2)
                                nc.scalar.activation(featT[:, 2 * P * h:2 * P * h + 2 * P], full(h, 0, 2 * P), ACT.Copy).then_inc(xT_ready, 1)
                        act.wait_ge(exp_in, 1)
                        nc.scalar.activation(weight[:], logits[:], ACT.Exp).then_inc(exp_out, 1)
                        with act.Fori(0, EXPERTS // 2) as i:
                            for s in range(2):
                                e = 2 * i + s
                                u = 0
                                for stage in range(2 if layer else 1):
                                    last_stage = stage == (1 if layer else 0)
                                    for h in range(HALVES):
                                        if last_stage:
                                            act.wait_ge(out_ps, HALVES * e + h + 1)
                                        for f in range(nf):
                                            act.wait_ge(hid_ps, UNITS * e + u + 1)
                                            nc.scalar.activation((hid2 if last_stage else hid)[h][:, f, :], bank(0, u % NB), ACT.Relu,
                                                                 bias=Bs[s][:, nf * stage + f:nf * stage + f + 1]).then_inc(hid_ready, 1)
                                            u += 1

                    @block.vector
                    def _(dve):
                        own = Own()
                        bc = [P, TILES, EXPERTS]
                        dve.wait_ge(loaded["late"], 16 * 6)
                        if layer:
                            nc.vector.tensor_tensor(sq[:], xres[:], xres[:], ALU.mult).then_inc(g_step, 1)
                            for n in range(2):
                                nc.vector.tensor_reduce(wsum[:, n:n + 1], ffn_w[n][:], X, ALU.add, apply_absolute_value=True).then_inc(mag_ready, 1)
                            dve.wait_ge(g_step, own.next())
                            nc.vector.tensor_reduce(st[:, 0, :], sq[:], X, ALU.add).then_inc(square_ready, 1)
                            dve.wait_ge(logit_ps, 1)
                            dve.wait_ge(rms_ready, 1)
                            nc.vector.tensor_tensor(logits[:], full(6, 0, TILES * EXPERTS).rearrange("p (n e) -> p n e", e=EXPERTS),
                                                    st[:, 2, :].unsqueeze(2).to_broadcast(bc), ALU.mult).then_inc(g_step, 1)
                            dve.wait_ge(g_step, own.next())
                            nc.vector.tensor_tensor(logits[:], logits[:], genre[:], ALU.add).then_inc(g_step, 1)
                            dve.wait_ge(g_step, own.next())
                        for n in range(TILES):
                            ins = nc.vector.max(top[:, n, :], logits[:, n, :])
                        ins.then_inc(g_step, 1)
                        dve.wait_ge(g_step, own.next())
                        for n in range(TILES):
                            ins = nc.vector.max_index(topi[:, n, :], top[:, n, :], logits[:, n, :])
                        ins.then_inc(g_step, 1)
                        dve.wait_ge(g_step, own.next())
                        nc.vector.tensor_tensor(logits[:], logits[:], top[:, :, 0:1].to_broadcast(bc), ALU.subtract).then_inc(exp_in, 1)
                        nc.vector.tensor_copy(topf[:], topi[:, :, 0:2]).then_inc(g_step, 1)
                        dve.wait_ge(g_step, own.next())
                        for j in range(2):
                            nc.vector.tensor_tensor(chosen[:, j], k["iota"].unsqueeze(1).to_broadcast(bc), topf[:, :, j:j + 1].to_broadcast(bc), ALU.is_equal).then_inc(g_step, 1)
                            own.next()
                        dve.wait_ge(g_step, own.count)
                        nc.vector.tensor_tensor(chosen[:, 0], chosen[:, 0], chosen[:, 1], ALU.add).then_inc(g_step, 1)
                        dve.wait_ge(g_step, own.next())
                        dve.wait_ge(exp_out, 1)
                        nc.vector.tensor_tensor(chosen[:, 0], chosen[:, 0], weight[:], ALU.mult).then_inc(g_step, 1)
                        dve.wait_ge(g_step, own.next())
                        nc.vector.tensor_reduce(total[:], chosen[:, 0] if layer == 0 else weight[:], X, ALU.add).then_inc(g_step, 1)
                        dve.wait_ge(g_step, own.next())
                        nc.vector.reciprocal(rtotal[:], total[:]).then_inc(g_step, 1)
                        dve.wait_ge(g_step, own.next())
                        nc.vector.tensor_tensor(weight[:], chosen[:, 0], rtotal[:].unsqueeze(2).to_broadcast(bc), ALU.mult).then_inc(g_step, 1)
                        dve.wait_ge(g_step, own.next())
                        if layer:
                            dve.wait_ge(mag_ps, 1)
                            nc.vector.tensor_scalar(wmean[:], full(7, 0, 2), 1.0 / (E * HID), 1e-5, ALU.mult, ALU.max).then_inc(g_step, 1)
                            dve.wait_ge(g_step, own.next())
                            nc.vector.reciprocal(wscale[:], wmean[:]).then_inc(g_step, 1)
                            dve.wait_ge(g_step, own.next())
                            for n in range(2):
                                nc.vector.tensor_scalar(ffn_t[:, n, :], ffn_w[n][:], wscale[:, n:n + 1], ROUND, ALU.mult, ALU.add).then_inc(g_step, 1)
                                own.next()
                            dve.wait_ge(g_step, own.count)
                            for n in range(2):
                                nc.vector.tensor_scalar(ffn_t[:, n, :], ffn_t[:, n, :], ROUND, 1.0, ALU.subtract, ALU.min).then_inc(g_step, 1)
                                own.next()
                            dve.wait_ge(g_step, own.count)
                            for n in range(2):
                                nc.vector.tensor_scalar(ffn_q[n][:], ffn_t[:, n, :], -1.0, None, ALU.max)
                        with dve.Fori(0, EXPERTS // 2) as i:
                            for s in range(2):
                                e = 2 * i + s
                                dve.wait_ge(added, HALVES * e + HALVES)
                                for n in range(TILES):
                                    ins = nc.vector.scalar_tensor_tensor(out=target[:, n, :], in0=last_b[layer][:, bass.ds(e, 1), :].rearrange("p a f -> p (a f)"),
                                                                         scalar=weight[:, n, bass.ds(e, 1)], in1=target[:, n, :],
                                                                         op0=ALU.mult, op1=ALU.add)
                                ins.then_inc(biased, 1)
                                for h in range(HALVES):
                                    dve.wait_ge(biased, e + 1)
                                    dve.wait_ge(out_ps, HALVES + HALVES * e + h + 1)
                                    for j in range(4):
                                        n = 4 * h + j
                                        ins = nc.vector.scalar_tensor_tensor(out=target[:, n, :], in0=bank(1, h, E * j, E * j + E),
                                                                             scalar=weight[:, n, bass.ds(e, 1)], in1=target[:, n, :],
                                                                             op0=ALU.mult, op1=ALU.add)
                                    ins.then_inc(added, 1)

        def attention1():
            with ExitStack() as scope:
                def lsb(name, shape, dt=F32):
                    return scope.enter_context(nc.sbuf_tensor("log_" + name, shape, dt))

                def lsem(name):
                    return sem("log_" + name)

                uT = lsb("uT", [P, TOK])
                z, za = lsb("z", [P, TILES, NSMALL]), lsb("za", [P, TILES, NSMALL])
                qk, v = lsb("qk", [P, 2 * LH, P]), lsb("v", [P, LH * LD])
                gtri, decay, lamw, a = lsb("gtri", [P, LH, S]), lsb("decay", [P, LH, S]), lsb("lamw", [P, LH, S]), lsb("a", [P, LH, S])
                abd, yT = lsb("abd", [P, LH, P]), lsb("yT", [P, LH, P])
                out = lsb("out", [P, E])
                bn, mv, st = lsb("bn", [P, 6]), lsb("mv", [P, 2]), lsb("st", [P, 2])
                uT_ps, uT_ready, small_ps, z_abs, z_exp, z_log = lsem("uT_ps"), lsem("uT_ready"), lsem("small_ps"), lsem("z_abs"), lsem("z_exp"), lsem("z_log")
                zeroed, dve_step, pool_step = lsem("zeroed"), lsem("dve_step"), lsem("pool_step")
                own = Own()

                with nc.Block() as block:
                    @block.gpsimd
                    def _(pool):
                        nc.gpsimd.memset(abd[:], 0.0).then_inc(zeroed, 1)
                        nc.gpsimd.memset(lamw[:], 0.0).then_inc(zeroed, 1)

                    @block.tensor
                    def _(pe):
                        for n in range(TILES):
                            nc.tensor.transpose(full(n // 2, P * (n % 2), P * (n % 2) + P), acc[:, n, :], k["ident"]).then_inc(uT_ps, 1)
                        for n in range(TILES):
                            pe.wait_ge(uT_ready, n // 2 + 1)
                            mm = nc.tensor.matmul(full(4, NSMALL * n, NSMALL * n + NSMALL), uT[:, P * n:P * n + P], small_w, start=True, stop=True)
                        mm.then_inc(small_ps, 1)

                    @block.scalar
                    def _(act):
                        for h in range(TILES // 2):
                            act.wait_ge(uT_ps, 2 * h + 2)
                            nc.scalar.activation(uT[:, 2 * P * h:2 * P * h + 2 * P], full(h, 0, 2 * P), ACT.Copy).then_inc(uT_ready, 1)
                        act.wait_ge(z_abs, 1)
                        nc.scalar.activation(za[:], za[:], ACT.Exp).then_inc(z_exp, 1)
                        act.wait_ge(z_exp, 1)
                        nc.scalar.activation(za[:], za[:], ACT.Ln, bias=1.0).then_inc(z_log, 1)

                    @block.vector
                    def _(dve):
                        dve.wait_ge(small_ps, 1)
                        nc.vector.tensor_tensor(z[:], full(4, 0, TILES * NSMALL).rearrange("p (n c) -> p n c", c=NSMALL),
                                                small_b.unsqueeze(1).to_broadcast([P, TILES, NSMALL]), ALU.add).then_inc(dve_step, 1)
                        dve.wait_ge(dve_step, own.next())
                        nc.vector.scalar_tensor_tensor(out=za[:], in0=z[:], scalar=-1.0, in1=z[:], op0=ALU.mult, op1=ALU.min).then_inc(z_abs, 1)
                        dve.wait_ge(z_log, 1)
                        nc.vector.scalar_tensor_tensor(out=z[:], in0=z[:], scalar=0.0, in1=za[:], op0=ALU.max, op1=ALU.add)

                gtri_ready, decay_ps, decay_ready, weight_ready = lsem("gtri_ready"), lsem("decay_ps"), lsem("decay_ready"), lsem("weight_ready")
                q_ps, k_ps, v_ps, q_ready, k_ready, v_ready = lsem("q_ps"), lsem("k_ps"), lsem("v_ps"), lsem("q_ready"), lsem("k_ready"), lsem("v_ready")
                scores_ps, a_ready, aT_ready, yT_ps, yT_ready, out_ps = lsem("scores_ps"), lsem("a_ready"), lsem("aT_ready"), lsem("yT_ps"), lsem("yT_ready"), lsem("out_ps")
                out_read, x_biased, var_ready, rstd_ready, x_ready = lsem("out_read"), lsem("x_biased"), lsem("var_ready"), lsem("rstd_ready"), lsem("x_ready")

                def fsb(name, shape, dt=F32):
                    return scope.enter_context(nc.sbuf_tensor("ffn_" + name, shape, dt))

                def fsem(name):
                    return sem("ffn_" + name)

                NF = HID // P
                xr, xq, xqT = fsb("xr", [P, P]), fsb("xq", [P, P], BF16), fsb("xqT", [P, P], BF16)
                m1, m2 = fsb("m1", [P, 4]), fsb("m2", [P, 4])
                dg, sbc = fsb("dg", [P, P]), fsb("sbc", [P, P])
                hp = fsb("hp", [P, NF, SEQ, S + 2])
                y, ys = fsb("y", [P, NF, SEQ, S]), fsb("ys", [P, NF, P])
                yr, yq, yqT = fsb("yr", [P, HID]), fsb("yq", [P, HID], BF16), fsb("yqT", [P, NF, P], BF16)
                outb = [fsb(f"outb{s}", [P, E]) for s in range(2)]
                stored = [fsem(f"stored{s}") for s in range(2)]
                f_zeroed, ct_ps, xq_ready, xqT_ps, xqT_ready = fsem("zeroed"), fsem("ct_ps"), fsem("xq_ready"), fsem("xqT_ps"), fsem("xqT_ready")
                diag_ready, sbc_ps, sbc_ready, h_ps, h_ready = fsem("diag_ready"), fsem("sbc_ps"), fsem("sbc_ready"), fsem("h_ps"), fsem("h_ready")
                mid_ready, conv_ready, silu_ready, yt_ps, yq_ready = fsem("mid_ready"), fsem("conv_ready"), fsem("silu_ready"), fsem("yt_ps"), fsem("yq_ready")
                yqT_ps, yqT_ready, o_ps, o_ready = fsem("yqT_ps"), fsem("yqT_ready"), fsem("o_ps"), fsem("out_ready")

                scale = 1.0 / float(np.sqrt(LD))
                PERIOD = 22.62
                at = dict(spread_gates=0, sum_gates=11.28, exp_decay=14.56, queries=14.87, level_weights=16,
                          keys=17.11, copy_queries=18.6, weigh_decay=18.65, copy_keys=19.59, scores=21.41,
                          bias_x=22.01, values=23.48, weigh_scores=23.66, copy_values=24.38, times_values=26.54,
                          copy_yT=28.98, output=30.15, norm_in=32.95, inverse_deviation=33.97, norm_out=34.6,
                          c_transpose_x=35.99, c_copy_x=36.42, c_project=36.78, c_copy_qkv=38.72,
                          c_spread_keys=39.29, c_scores=43.05, c_softmax_in=44.16, c_exponentials=46.41,
                          c_turn=49.81, c_times_values=54.47, c_divide=56.82, c_transpose_o=57.35, c_copy_oT=57.75,
                          c_project_o=58.82, c_squares=59.44, c_inverse_rms=59.89, c_normalise=61.69,
                          c_transpose_z=62.21, c_modulate=62.88, transpose_c=64.95, quantise_x=65.27,
                          scale_diagonal=66.85, transpose_xq=68.32, spread_scale=68.4, copy_xqT=68.57,
                          copy_scale=68.81, hidden=70.37, pad_hidden=71.74, middle_tap=72.56, outer_taps=75.73,
                          silus=79.56, transpose_y=80.27, quantise_y=81.32, transpose_yq=84.66, copy_yqT=85.06,
                          down=86.76, finish=86.86)
                QB, KB, FB, GB = 2, 4, 6, 7

                with nc.Block() as block:
                    @block.sync
                    def _(sp):
                        for n in range(TILES):
                            sp.wait_ge(o_ready, n + 1)
                            sp.dma_start(d["out"][n], outb[n % 2][:]).then_inc(stored[n % 2], 16)
                        for s in range(2):
                            sp.wait_ge(stored[s], 16 * (TILES // 2))

                    @block.gpsimd
                    def _(pool):
                        own_pool = Own()
                        nc.gpsimd.memset(hp[:], 0.0).then_inc(f_zeroed, 1)

                        def spread_gates(n):
                            if n:
                                pool.wait_ge(decay_ps, n)
                            nc.gpsimd.tensor_tensor(gtri[:], z[:, n, 0:LH].unsqueeze(2).to_broadcast([P, LH, S]),
                                                    k["negafter"].unsqueeze(1).to_broadcast([P, LH, S]), ALU.mult).then_inc(gtri_ready, 1)

                        def bias_x(n):
                            nc.gpsimd.tensor_tensor(xres[:, n, :], xres[:, n, :], ln[:, 1, :], ALU.add).then_inc(x_biased, 1)

                        def inverse_deviation(n):
                            pool.wait_ge(var_ready, n + 1)
                            nc.gpsimd.tensor_scalar(st[:, 0:1], mv[:, 1:2], 1e-5, 1.0, ALU.add, ALU.mult).then_inc(pool_step, 1)
                            pool.wait_ge(pool_step, own_pool.next())
                            nc.gpsimd.tensor_tensor(st[:, 1:2], st[:, 0:1], eps[:, 1:2], ALU.pow).then_inc(rstd_ready, 1)

                        def scale_diagonal(n):
                            pool.wait_ge(xq_ready, n + 1)
                            nc.gpsimd.tensor_tensor(dg[:], k["ident"], m1[:, 3:4].to_broadcast([P, P]), ALU.mult).then_inc(diag_ready, 1)

                        run_in_time_order(PERIOD, cond_pool(pool, 1, at, own_pool, pool_step) + [
                            (at["spread_gates"], spread_gates), (at["bias_x"], bias_x), (at["inverse_deviation"], inverse_deviation), (at["scale_diagonal"], scale_diagonal)])

                    @block.tensor
                    def _(pe):
                        def sum_gates(n):
                            pe.wait_ge(gtri_ready, n + 1)
                            if n:
                                pe.wait_ge(out_read, n)
                            nc.tensor.matmul(full(KB + 1, 0, LH * S), k["upto"], gtri[:].rearrange("p h t -> p (h t)"), start=True, stop=True).then_inc(decay_ps, 1)

                        def queries(n):
                            if n:
                                pe.wait_ge(yT_ready, n)
                            for c in range(LH):
                                mm = nc.tensor.matmul(full(QB + c // 4, P * (c % 4), P * (c % 4) + P), wqk[:, P * c:P * c + P], uT[:, P * n:P * n + P], start=True, stop=True)
                            mm.then_inc(q_ps, 1)

                        def keys(n):
                            pe.wait_ge(decay_ready, n + 1)
                            for c in range(LH):
                                mm = nc.tensor.matmul(full(KB + c // 4, P * (c % 4), P * (c % 4) + P), wqk[:, P * (LH + c):P * (LH + c) + P], uT[:, P * n:P * n + P], start=True, stop=True)
                            mm.then_inc(k_ps, 1)

                        def scores(n):
                            pe.wait_ge(k_ready, n + 1)
                            pe.wait_ge(q_ready, n + 1)
                            for h in range(LH):
                                mm = nc.tensor.matmul(full(QB + h // 4, P * (h % 4), P * (h % 4) + P), qk[:, h, :], qk[:, LH + h, :], start=True, stop=True)
                            mm.then_inc(scores_ps, 1)

                        def values(n):
                            for c in range(2):
                                mm = nc.tensor.matmul(full(KB + c), uT[:, P * n:P * n + P], wv[:, BANK * c:BANK * c + BANK], start=True, stop=True)
                            mm.then_inc(v_ps, 1)

                        def times_values(n):
                            pe.wait_ge(aT_ready, n + 1)
                            pe.wait_ge(v_ready, n + 1)
                            for h in range(LH):
                                mm = nc.tensor.matmul(full(QB + h // 4, P * (h % 4), P * (h % 4) + P), v[:, LD * h:LD * h + LD], abd[:, h, :], start=True, stop=True)
                            mm.then_inc(yT_ps, 1)

                        def output(n):
                            pe.wait_ge(yT_ready, n + 1)
                            for c in range(LH):
                                mm = nc.tensor.matmul(full(KB, 0, E), yT[:, c, :], wout[:, c, :], start=(c == 0), stop=(c == LH - 1))
                            mm.then_inc(out_ps, 1)

                        def transpose_c(n):
                            pe.wait_ge(c_done, TILES + n + 1)
                            if n:
                                pe.wait_ge(o_ready, n)
                            nc.tensor.transpose(full(GB, 0, P), featT[:, P * n:P * n + P], k["ident"]).then_inc(ct_ps, 1)

                        def transpose_xq(n):
                            pe.wait_ge(xq_ready, n + 1)
                            nc.tensor.transpose(full(GB, P, P + P // 2).bitcast(BF16), xq[:], ident_b[:]).then_inc(xqT_ps, 1)

                        def spread_scale(n):
                            pe.wait_ge(diag_ready, n + 1)
                            nc.tensor.matmul(full(FB, 0, P), k["ones"], dg[:], start=True, stop=True).then_inc(sbc_ps, 1)

                        def hidden(n):
                            pe.wait_ge(xqT_ready, n + 1)
                            pe.wait_ge(sbc_ready, n + 1)
                            for f in range(NF):
                                mm = nc.tensor.matmul(full(FB, P * f, P * f + P), ffn_q[0][:, P * f:P * f + P], xqT[:], start=True, stop=True)
                            mm.then_inc(h_ps, 1)

                        def transpose_y(n):
                            pe.wait_ge(silu_ready, n + 1)
                            for f in range(NF):
                                mm = nc.tensor.transpose(full(FB, P * f, P * f + P), ys[:, f, :], k["ident"])
                            mm.then_inc(yt_ps, 1)

                        def transpose_yq(n):
                            pe.wait_ge(yq_ready, n + 1)
                            for f in range(NF):
                                mm = nc.tensor.transpose(full(GB, P // 2 * f, P // 2 * (f + 1)).bitcast(BF16), yq[:, P * f:P * f + P], ident_b[:])
                            mm.then_inc(yqT_ps, 1)

                        def down(n):
                            pe.wait_ge(yqT_ready, n + 1)
                            for f in range(NF):
                                mm = nc.tensor.matmul(full(GB, 5 * P // 2, 7 * P // 2), yqT[:, f, :], ffn_q[1][:, P * f:P * f + P], start=(f == 0), stop=(f == NF - 1))
                            mm.then_inc(o_ps, 1)

                        pe.wait_ge(loaded["wattn1"], 48)
                        run_in_time_order(PERIOD, cond_tensor(pe, 1, at, x_ready) + [
                            (at["sum_gates"], sum_gates), (at["queries"], queries), (at["keys"], keys), (at["scores"], scores), (at["values"], values), (at["times_values"], times_values), (at["output"], output),
                            (at["transpose_c"], transpose_c), (at["transpose_xq"], transpose_xq), (at["spread_scale"], spread_scale), (at["hidden"], hidden),
                            (at["transpose_y"], transpose_y), (at["transpose_yq"], transpose_yq), (at["down"], down)])

                    @block.scalar
                    def _(act):
                        def exp_decay(n):
                            act.wait_ge(decay_ps, n + 1)
                            if n:
                                act.wait_ge(a_ready, n)
                            nc.scalar.activation(decay[:].rearrange("p h t -> p (h t)"), full(KB + 1, 0, LH * S), ACT.Exp).then_inc(decay_ready, 1)

                        def copy_queries(n):
                            act.wait_ge(q_ps, n + 1)
                            if n:
                                act.wait_ge(scores_ps, n)
                            for c in range(2):
                                ins = nc.scalar.activation(qk[:, 4 * c:4 * c + 4, :].rearrange("p c t -> p (c t)"), full(QB + c), ACT.Copy)
                            ins.then_inc(q_ready, 1)

                        def copy_keys(n):
                            act.wait_ge(k_ps, n + 1)
                            for c in range(2):
                                ins = nc.scalar.activation(qk[:, LH + 4 * c:LH + 4 * c + 4, :].rearrange("p c t -> p (c t)"), full(KB + c), ACT.Copy)
                            ins.then_inc(k_ready, 1)

                        def copy_values(n):
                            act.wait_ge(v_ps, n + 1)
                            if n:
                                act.wait_ge(yT_ps, n)
                            for c in range(2):
                                ins = nc.scalar.activation(v[:, BANK * c:BANK * c + BANK], full(KB + c), ACT.Copy)
                            ins.then_inc(v_ready, 1)

                        def copy_yT(n):
                            act.wait_ge(yT_ps, n + 1)
                            if n:
                                act.wait_ge(out_ps, n)
                            for c in range(2):
                                ins = nc.scalar.activation(yT[:, 4 * c:4 * c + 4, :].rearrange("p c t -> p (c t)"), full(QB + c), ACT.Copy)
                            ins.then_inc(yT_ready, 1)

                        def copy_xqT(n):
                            act.wait_ge(xqT_ps, n + 1)
                            nc.scalar.activation(xqT[:], full(GB, P, P + P // 2).bitcast(BF16), ACT.Copy).then_inc(xqT_ready, 1)

                        def copy_scale(n):
                            act.wait_ge(sbc_ps, n + 1)
                            nc.scalar.activation(sbc[:], full(FB, 0, P), ACT.Copy).then_inc(sbc_ready, 1)

                        def middle_tap(n):
                            act.wait_ge(h_ready, n + 1)
                            for f in range(NF):
                                ins = nc.scalar.activation(y[:, f], hp[:, f, :, 1:S + 1], ACT.Identity, bias=conv[:, f, 3:4], scale=conv[:, f, 1:2])
                            ins.then_inc(mid_ready, 1)

                        def silus(n):
                            act.wait_ge(conv_ready, n + 1)
                            nc.scalar.activation(ys[:].rearrange("p f t -> p (f t)"), y[:].rearrange("p f b t -> p (f b t)"), ACT.Silu).then_inc(silu_ready, 1)

                        def copy_yqT(n):
                            act.wait_ge(yqT_ps, n + 1)
                            nc.scalar.activation(yqT[:].rearrange("p f t -> p (f t)"), full(GB, 0, P // 2 * NF).bitcast(BF16), ACT.Copy).then_inc(yqT_ready, 1)

                        run_in_time_order(PERIOD, cond_scalar(act, 1, at) + [
                            (at["exp_decay"], exp_decay), (at["copy_queries"], copy_queries), (at["copy_keys"], copy_keys), (at["copy_values"], copy_values), (at["copy_yT"], copy_yT),
                            (at["copy_xqT"], copy_xqT), (at["copy_scale"], copy_scale), (at["middle_tap"], middle_tap), (at["silus"], silus), (at["copy_yqT"], copy_yqT)])

                    @block.vector
                    def _(dve):
                        def level_weights(n):
                            if n:
                                dve.wait_ge(weight_ready, n)
                            for l in range(LEVELS):
                                nc.vector.copy_predicated(lamw[:], levelmask[:, l, :].unsqueeze(1).to_broadcast([P, LH, S]),
                                                          z[:, n, LH * (l + 1):LH * (l + 2)].unsqueeze(2).to_broadcast([P, LH, S])).then_inc(dve_step, 1)
                                dve.wait_ge(dve_step, own.next())

                        def weigh_decay(n):
                            dve.wait_ge(decay_ready, n + 1)
                            nc.vector.tensor_tensor(decay[:], decay[:], lamw[:], ALU.mult).then_inc(weight_ready, 1)

                        def weigh_scores(n):
                            dve.wait_ge(weight_ready, n + 1)
                            dve.wait_ge(scores_ps, n + 1)
                            src = PS[:, QB * BANK:(QB + 2) * BANK].rearrange("p (h t) -> p h t", t=P)
                            for b in range(SEQ):
                                r = slice(S * b, S * b + S)
                                ins = nc.vector.scalar_tensor_tensor(out=a[r], in0=src[r][:, :, S * b:S * b + S], scalar=scale, in1=decay[r],
                                                                     op0=ALU.mult, op1=ALU.mult)
                            ins.then_inc(a_ready, 1)
                            dve.wait_ge(a_ready, n + 1)
                            if n:
                                dve.wait_ge(yT_ps, n)
                            for b in range(SEQ):
                                ins = nc.vector.transpose(abd[S * b:S * b + S, :, S * b:S * b + S], a[S * b:S * b + S, :, :])
                            ins.then_inc(aT_ready, 1)

                        def norm_in(n):
                            if n:
                                dve.wait_ge(x_ready, n)
                            dve.wait_ge(out_ps, n + 1)
                            nc.vector.tensor_tensor(out[:], full(KB, 0, E), acc[:, n, :], ALU.add).then_inc(out_read, 1)
                            dve.wait_ge(out_read, n + 1)
                            nc.vector.bn_stats(bn[:], out[:]).then_inc(dve_step, 1)
                            dve.wait_ge(dve_step, own.next())
                            nc.vector.bn_aggr(mv[:], bn[:]).then_inc(var_ready, 1)
                            dve.wait_ge(var_ready, n + 1)
                            nc.vector.scalar_tensor_tensor(out=out[:], in0=out[:], scalar=mv[:, 0:1], in1=ln[:, 0, :],
                                                           op0=ALU.subtract, op1=ALU.mult).then_inc(dve_step, 1)
                            dve.wait_ge(dve_step, own.next())

                        def norm_out(n):
                            dve.wait_ge(rstd_ready, n + 1)
                            dve.wait_ge(x_biased, n + 1)
                            nc.vector.scalar_tensor_tensor(out=xres[:, n, :], in0=out[:], scalar=st[:, 1:2], in1=xres[:, n, :],
                                                           op0=ALU.mult, op1=ALU.add).then_inc(x_ready, 1)

                        def quantise(ps_ready, src, m, r, q, w, signal):
                            def step(n):
                                dve.wait_ge(ps_ready, n + 1)
                                nc.vector.tensor_reduce(m[:, 0:1], src, X, ALU.max, apply_absolute_value=True).then_inc(dve_step, 1)
                                dve.wait_ge(dve_step, own.next())
                                nc.vector.tensor_scalar(m[:, 1:2], m[:, 0:1], 1e-5, 1.0 / QMAX, ALU.max, ALU.mult).then_inc(dve_step, 1)
                                dve.wait_ge(dve_step, own.next())
                                nc.vector.reciprocal(m[:, 2:3], m[:, 1:2]).then_inc(dve_step, 1)
                                dve.wait_ge(dve_step, own.next())
                                nc.vector.tensor_scalar(r[:], src, m[:, 2:3], ROUND, ALU.mult, ALU.add).then_inc(dve_step, 1)
                                nc.vector.tensor_scalar(m[:, 3:4], m[:, 1:2], wmean[:, w:w + 1], None, ALU.mult)
                                dve.wait_ge(dve_step, own.next())
                                nc.vector.tensor_scalar(q[:], r[:], ROUND, None, ALU.subtract).then_inc(signal, 1)
                            return step

                        def pad_hidden(n):
                            dve.wait_ge(h_ps, n + 1)
                            dve.wait_ge(sbc_ready, n + 1)
                            nc.vector.tensor_tensor(hp[:, :, :, 1:S + 1], full(FB).rearrange("p (f b t) -> p f b t", f=NF, b=SEQ),
                                                    sbc[:].rearrange("p (b t) -> p b t", t=S).unsqueeze(1).to_broadcast([P, NF, SEQ, S]), ALU.mult).then_inc(h_ready, 1)

                        def outer_taps(n):
                            dve.wait_ge(mid_ready, n + 1)
                            for f in range(NF):
                                ins = nc.vector.scalar_tensor_tensor(out=y[:, f], in0=hp[:, f, :, 0:S], scalar=conv[:, f, 0:1], in1=y[:, f], op0=ALU.mult, op1=ALU.add)
                            ins.then_inc(dve_step, 1)
                            dve.wait_ge(dve_step, own.next())
                            for f in range(NF):
                                ins = nc.vector.scalar_tensor_tensor(out=y[:, f], in0=hp[:, f, :, 2:S + 2], scalar=conv[:, f, 2:3], in1=y[:, f], op0=ALU.mult, op1=ALU.add)
                            ins.then_inc(conv_ready, 1)

                        def finish(n):
                            dve.wait_ge(o_ps, n + 1)
                            if n >= 2:
                                dve.wait_ge(stored[n % 2], 16 * (n // 2))
                            nc.vector.scalar_tensor_tensor(out=outb[n % 2][:], in0=full(GB, 5 * P // 2, 7 * P // 2), scalar=m2[:, 3:4],
                                                           in1=xres[:, n, :], op0=ALU.mult, op1=ALU.add).then_inc(o_ready, 1)

                        dve.wait_ge(f_zeroed, 1)
                        dve.wait_ge(zeroed, 2)
                        run_in_time_order(PERIOD, cond_vector(dve, 1, at, own, dve_step) + [
                            (at["level_weights"], level_weights), (at["weigh_decay"], weigh_decay), (at["weigh_scores"], weigh_scores), (at["norm_in"], norm_in), (at["norm_out"], norm_out),
                            (at["quantise_x"], quantise(ct_ps, full(GB, 0, P), m1, xr, xq, 0, xq_ready)), (at["pad_hidden"], pad_hidden), (at["outer_taps"], outer_taps),
                            (at["quantise_y"], quantise(yt_ps, full(FB), m2, yr, yq, 1, yq_ready)), (at["finish"], finish)])

        for stage in (attention0, lambda: experts(0), lambda: experts(1), attention1):
            stage()


def kernel(**inp):
    import concourse.bacc as _bacc
    from concourse.bass_utils import run_bass_kernel_spmd as _run

    a = {n: np.asarray(v) for n, v in inp.items()}
    cat = np.concatenate
    rows = lambda v: np.tile(v.reshape(1, -1), (P, 1))
    lay = {"x": a["x"].reshape(TOK, E)}
    small = {"condT": a["cond_256"].T, "genre_w": a["L1_cond_gg_W"]}
    for n, pre in enumerate(("L0_cond_", "L1_cond2_")):
        lay[f"cond_w{n}"] = cat([a[pre + w].T for w in ("Wq", "Wk", "Wv", "Wo")], axis=1)
        small[f"mod_w{n}"] = a[pre + "Wc"].T
        small[f"mod_b{n}"] = a[pre + "bc"].reshape(2, E).T
        small[f"rms_s{n}"] = a[pre + "rms_scale"][:, None]
    lay["mask"] = np.tile(np.ascontiguousarray(a["mask_SxS_bk1"]).view(np.int32), (SEQ, 1))
    lay["attn0_qk"] = cat([a["L0_attn_w_q"], a["L0_attn_w_kv"][:, :AH * AD]], axis=1)
    lay["attn0_v"] = a["L0_attn_w_kv"][:, AH * AD:]
    lay["attn0_out"] = a["L0_attn_w_out"]
    lay["attn1_qk"] = cat([a["L1_attn_Wq"].T, a["L1_attn_Wk"].T], axis=1)
    lay["attn1_v"] = a["L1_attn_Wv"].T
    lay["attn1_out"] = a["L1_attn_Wo"].T
    pair = np.arange(4)[:, None] ^ np.arange(4)[None, :]
    small["quat"] = a["L0_cond2_q_right"][pair].transpose(0, 2, 1).reshape(P, 4)
    small["quat_l"] = a["cond_256"][pair].transpose(0, 2, 1).reshape(P, 4)
    small["quat_all"] = np.tile(a["cond_256"].T, (4, 1))
    small["sgate"] = np.tile(a["L0_cond2_spectral_gate"].reshape(S, 1), (4, 1))
    small["router_w0"], small["router_b0"] = a["L0_ffn_W_router"], rows(a["L0_ffn_b_router"])
    small["router_w1"], small["router_b1"] = a["L1_cond_wg_W"], rows(a["L1_cond_wg_b"])
    small["genre_b"] = rows(a["L1_cond_gg_b"])
    small["rms1"] = a["L1_cond_rms_w"][:, None]
    lay["ffn_w0"] = a["L1_ffn_w1"].T
    lay["ffn_w1"] = a["L1_ffn_w2"].T.reshape(HID // P, P, E).transpose(1, 0, 2).reshape(P, HID)
    taps = cat([a["L1_ffn_conv_w"][:, 0, :], a["L1_ffn_conv_b"][:, None]], axis=1)
    small["conv"] = taps.reshape(HID // P, P, 4).transpose(1, 0, 2).reshape(P, HID // P * 4)
    lay["moe0_b"] = a["L0_ffn_b1"].reshape(EXPERTS, -1, P).transpose(0, 2, 1)
    lay["moe1_b"] = cat([a["L1_cond_b1"], a["L1_cond_b2"]], axis=1).reshape(EXPERTS, -1, P).transpose(0, 2, 1)
    lay["moe0_last_b"], lay["moe1_last_b"] = rows(a["L0_ffn_b2"]), rows(a["L1_cond_b3"])
    levels = a["L1_attn_Wdl"].reshape(LH, -1, E)[:, :LEVELS].transpose(1, 0, 2).reshape(LH * LEVELS, E)
    small["small_w"] = cat([a["L1_attn_Wg"], levels], axis=0).T
    small["small_b"] = rows(cat([a["L1_attn_bg"], a["L1_attn_Lparam"][:, :LEVELS].T.reshape(-1)]))
    small["ln"] = rows(cat([a["L1_attn_ln_g"], a["L1_attn_ln_b"]]))
    for name, where in (("feat", FEAT), ("cond", COND), ("rows", ROWS)):
        lay[name] = cat([small[n] for n in where], axis=1)
    lay["moe0_w1"], lay["moe0_w2"] = a["L0_ffn_W1"], a["L0_ffn_W2"]
    lay["moe1_w1"], lay["moe1_w2"], lay["moe1_w3"] = a["L1_cond_W1"], a["L1_cond_W2"], a["L1_cond_W3"]
    lay["const"], lay["levelmask"] = constants()

    nc = _bacc.Bacc("TRN2", target_bir_lowering=False, num_devices=1)
    arrays, d = {}, {}
    for name, v in lay.items():
        v = np.ascontiguousarray(v)
        arrays[f"in_{name}_dram"] = v
        d[name] = nc.dram_tensor(f"in_{name}_dram", v.shape, mybir.dt.from_np(v.dtype), kind="ExternalInput").ap()
    d["out"] = nc.dram_tensor("out_dram", (TILES, P, E), F32, kind="ExternalOutput").ap()
    build(nc, d)
    r = _run(nc, [arrays], core_ids=[0])
    return r.results[0]["out_dram"].reshape(B, S, E)
```

```python
from contextlib import ExitStack

import numpy as np

import concourse.bass as bass
from concourse import mybir

F32 = mybir.dt.float32
BF16 = mybir.dt.bfloat16
I32 = mybir.dt.int32
U32 = mybir.dt.uint32
U8 = mybir.dt.uint8
ALU = mybir.AluOpType
ACT = mybir.ActivationFunctionType
X = mybir.AxisListType.X

P = 128
B, S, E = 32, 32, 128
C = 32
TOK = B * S
TILES = TOK // P
HT = TILES // 2
SEQ = P // S
BANK = 512
CH, CD = 16, 8
AH, AD, ROT = 16, 64, 32
LH, LD = 8, 128
LEVELS = (S - 1).bit_length() + 1
NSMALL = LH + LH * LEVELS
EXPERTS = 8
FF0 = 512
FF1 = 256
HID = 512
ROUND = 1.5 * 2.0 ** 23
QMAX = 127.0
MASKED = -3.0e38

CONST, _at = {}, 0
for _name, _width in (("ident", P), ("ones", P), ("upto", P), ("headmask", CH), ("ownquarter", 4 * CH), ("causal", S),
                      ("cos", S), ("sin", S), ("negafter", S), ("diag4", S), ("sign_r", 4),
                      ("sign_l", 4), ("iota", EXPERTS)):
    CONST[_name] = (_at, _at + _width)
    _at += _width
NCONST = _at


def columns(*fields):
    at, where = 0, {}
    for name, width in fields:
        where[name] = (at, at + width)
        at += width
    return where, at


FEAT, NFEAT = columns(("mod_b0", 2), ("mod_b1", 2), ("rms_s0", 1), ("rms_s1", 1), ("rms1", 1), ("sgate", 1), ("quat", 4), ("quat_l", 4),
                      ("quat_all", B), ("router_w0", EXPERTS), ("router_w1", EXPERTS), ("small_w", NSMALL), ("conv", HID // P * 4))
COND, NCOND = columns(("condT", B), ("mod_w0", 2 * E), ("mod_w1", 2 * E), ("genre_w", EXPERTS))
ROWS, NROWS = columns(("router_b0", EXPERTS), ("router_b1", EXPERTS), ("genre_b", EXPERTS), ("small_b", NSMALL), ("ln", 2 * E))


def constants():
    p = np.arange(P)
    t, seq = p % S, p // S
    c = {}
    c["ident"] = np.eye(P)
    c["ones"] = np.ones((P, P))
    c["upto"] = (seq[:, None] == seq[None, :]) & (t[:, None] <= t[None, :])
    c["headmask"] = (p[:, None] // CD) == np.arange(CH)[None, :]
    c["ownquarter"] = np.broadcast_to((np.arange(CH)[:, None] % 4 == np.arange(4)).reshape(-1), (P, 4 * CH))
    c["causal"] = np.where(np.arange(S)[None, :] <= t[:, None], 0.0, MASKED)
    inv = (np.float32(1.0) / np.power(np.float32(10000.0),
                                      np.arange(0, ROT, 2, dtype=np.float32) / np.float32(ROT))).astype(np.float32)
    ang = np.arange(S, dtype=np.float32)[:, None] * inv[None, :]
    d = p % AD
    rot = d < ROT
    a = ang[:, d % (ROT // 2)].T.astype(np.float64)
    c["cos"] = np.where(rot[:, None], np.cos(a), 1.0)
    c["sin"] = np.where(rot[:, None], np.where(d[:, None] < ROT // 2, -np.sin(a), np.sin(a)), 0.0)
    c["negafter"] = -1.0 * (t[:, None] > np.arange(S)[None, :])
    c["diag4"] = t[:, None] == np.arange(S)[None, :]
    right = np.array([[1, 1, 1, 1], [-1, 1, -1, 1], [-1, 1, 1, -1], [-1, -1, 1, 1]], float)
    left = np.array([[1, 1, 1, 1], [-1, 1, 1, -1], [-1, -1, 1, 1], [-1, 1, -1, 1]], float)
    comp = np.arange(4)
    conj = np.where((comp[:, None] ^ comp[None, :]) == 0, 1.0, -1.0)
    c["sign_r"] = (right * conj)[p // S]
    c["sign_l"] = left[p // S]
    c["iota"] = np.broadcast_to(np.arange(EXPERTS), (P, EXPERTS))
    table = np.concatenate([np.asarray(c[n], np.float32) for n in CONST], axis=1)
    dist = t[:, None] - np.arange(S)[None, :]
    level = np.where(dist <= 0, 0, np.floor(np.log2(np.maximum(dist, 1))).astype(int) + 1)
    masks = np.stack([(level == n) & (dist >= 0) for n in range(LEVELS)], 1).astype(np.int32)
    return np.ascontiguousarray(table), np.ascontiguousarray(masks.reshape(P, LEVELS * S))


def build(nc, d):
    ctx = ExitStack()
    with ctx:
        def sb(name, shape, dt=F32):
            return ctx.enter_context(nc.sbuf_tensor(name, shape, dt))

        def sem(name):
            return ctx.enter_context(nc.semaphore(name))

        PS = ctx.enter_context(nc.psum_tensor("PS", [P, 8 * BANK], F32))

        def bank(number, lo=0, hi=BANK):
            return PS[:, number * BANK + lo:number * BANK + hi]

        const = sb("const", [P, NCONST])
        k = {n: const[:, lo:hi] for n, (lo, hi) in CONST.items()}
        levelmask = sb("levelmask", [P, LEVELS, S], I32)
        xres = sb("xres", [P, TILES, E])
        featT = sb("featT", [P, TOK])
        acc = sb("acc", [P, TILES, E])
        cond_w = [sb(f"cond_w{n}", [P, 4 * E]) for n in range(2)]
        feat, cond, rows = sb("feat", [P, NFEAT]), sb("cond", [C, NCOND]), sb("rows", [P, NROWS])
        part = {n: t[:, lo:hi] for t, where in ((feat, FEAT), (cond, COND), (rows, ROWS)) for n, (lo, hi) in where.items()}
        mod_w, mod_b, rms_s = ([part[f"{n}{l}"] for l in range(2)] for n in ("mod_w", "mod_b", "rms_s"))
        router_w, router_b = ([part[f"{n}{l}"] for l in range(2)] for n in ("router_w", "router_b"))
        condT, genre_w, genre_b, rms1, sgate = part["condT"], part["genre_w"], part["genre_b"], part["rms1"], part["sgate"]
        quat, quat_l, quat_all = part["quat"], part["quat_l"], part["quat_all"]
        small_w, small_b = part["small_w"], part["small_b"]
        conv = part["conv"].rearrange("p (c k) -> p c k", k=4)
        ln = part["ln"].rearrange("p (a e) -> p a e", a=2)
        gain = [sb(f"gain{n}", [P, B]) for n in range(2)]
        shift = [sb(f"shift{n}", [P, B]) for n in range(2)]
        silu = sb("silu", [C, B])
        condx = sb("condx", [C, B, S])
        mask = sb("mask", [P, S // 4], I32)
        maskb = sb("maskb", [P, S])
        logits = sb("logits", [P, TILES, EXPERTS])
        wqk = sb("wqk", [P, 2 * AH * AD])
        wv = sb("wv", [P, AH * AD])
        wout = sb("wout", [P, AH * AD // P, E])
        rot_r = sb("rot_r", [P, 4, S])
        rot_l = sb("rot_l", [P, 4, S])
        genre = sb("genre", [P, TILES, EXPERTS])
        ffn_w = [sb(f"ffn_w{n}", [P, HID]) for n in range(2)]
        ffn_q = [sb(f"ffn_q{n}", [P, HID], BF16) for n in range(2)]
        ffn_t = sb("ffn_t", [P, 2, HID])
        wsum = sb("wsum", [P, 2])
        wmean = sb("wmean", [P, 2])
        wscale = sb("wscale", [P, 2])
        last_b = [sb(f"last_b{n}", [P, EXPERTS, E]) for n in range(2)]
        squares = sb("squares", [P, B])
        scratch = sb("scratch", [P, 4])
        eps = sb("eps", [P, 2])
        ident_b = sb("ident_b", [P, P], BF16)
        uT = sb("uT", [P, TOK])
        z, za = sb("z", [P, TILES, NSMALL]), sb("za", [P, HT, NSMALL])

        class Own:
            def __init__(self):
                self.count = 0

            def next(self):
                self.count += 1
                return self.count

        RING = (1, 7)
        WB = 3
        W = [sb(f"expert_w{n}", [P, FF0 + FF0 // P * E]) for n in range(WB)]
        WBIAS = [sb(f"expert_b{n}", [P, FF0 // P]) for n in range(WB)]
        hid = [sb(f"hid{n}", [P, FF0 // P, BANK]) for n in range(2)]
        top, topi, topf = sb("top", [P, HT, 8]), sb("topi", [P, HT, 8], U32), sb("topf", [P, HT, 2])
        chosen, gatew = sb("chosen", [P, 2, HT, EXPERTS]), sb("gatew", [P, HT, EXPERTS])
        total, rtotal = sb("total", [P, HT]), sb("rtotal", [P, HT])
        st8, sq = sb("st8", [P, 3, HT]), sb("sq", [P, HT, E])
        w_loaded = [sem(f"expert_w_loaded{n}") for n in range(WB)]
        unit_ps, added = sem("unit_ps"), sem("added")
        ring_read = [sem(f"ring_read{b}") for b in range(2)]
        exp_in, exp_out, gate_ready = sem("gate_exp_in"), sem("gate_exp_out"), sem("gate_ready")
        square_ready, rms_ready, mean_ready = sem("gate_square_ready"), sem("gate_rms_ready"), sem("mean_ready")
        z_abs, z_exp, z_log, z_ready = sem("z_abs"), sem("z_exp"), sem("z_log"), sem("z_ready")
        mix_step, mix_pool_step = sem("mixture_dve_step"), sem("mixture_pool_step")
        own_mix, own_mix_pool = Own(), Own()

        def load_expert(sp, g):
            layer, e, w = g // EXPERTS % 2, g % EXPERTS, W[g % WB]
            fields = ((("w1", 1, FF0), ("w2", FF0 // P, E)), (("w1", 1, FF1), ("w2", FF1 // P, FF1), ("w3", FF1 // P, E)))[layer]
            at = 0
            for n, a, b in fields:
                sp.dma_start(w[:, at:at + a * b].rearrange("p (a b) -> p a b", a=a),
                             d[f"moe{layer}_{n}"][e].rearrange("(c p) f -> p c f", p=P)).then_inc(w_loaded[g % WB], 16)
                at += a * b
            sp.dma_start(WBIAS[g % WB][:], d[f"moe{layer}_b"][e]).then_inc(w_loaded[g % WB], 16)

        def loads_up_to(g):
            return sum(16 * (3, 4)[m // EXPERTS % 2] for m in range(g % WB, g + 1, WB))

        loaded = {n: sem(f"loaded_{n}") for n in ("x", "const", "cond_w0", "small", "attn", "late", "wattn1")}
        prep = sem("prep_step")
        silu_exp, modulated, normed, summed = sem("silu_exp"), sem("modulated"), sem("normed"), sem("summed")

        with nc.Block() as block:
            @block.sync
            def _(sp):
                sp.dma_start(const[:], d["const"]).then_inc(loaded["const"], 16)
                sp.dma_start(xres[:], d["x"].rearrange("(n p) e -> p n e", p=P)).then_inc(loaded["x"], 16)
                sp.dma_start(cond_w[0][:], d["cond_w0"]).then_inc(loaded["cond_w0"], 16)
                sp.dma_start(wqk[:], d["attn0_qk"]).then_inc(loaded["attn"], 16)
                sp.dma_start(wv[:], d["attn0_v"]).then_inc(loaded["attn"], 16)
                sp.dma_start(wout[:], d["attn0_out"].rearrange("(c p) e -> p c e", p=P)).then_inc(loaded["attn"], 16)
                for g in range(WB):
                    load_expert(sp, g)
                sp.dma_start(last_b[0][:], d["moe0_last_b"].rearrange("p (e f) -> p e f", f=E)).then_inc(loaded["late"], 16)
                for n in range(2):
                    sp.dma_start(ffn_w[n][:], d[f"ffn_w{n}"]).then_inc(loaded["late"], 16)
                sp.dma_start(cond_w[1][:], d["cond_w1"]).then_inc(loaded["late"], 16)
                sp.dma_start(levelmask[:], d["levelmask"].rearrange("p (l s) -> p l s", l=LEVELS)).then_inc(loaded["late"], 16)
                sp.dma_start(last_b[1][:], d["moe1_last_b"].rearrange("p (e f) -> p e f", f=E)).then_inc(loaded["late"], 16)

            @block.scalar
            def _(act):
                act.dma_start(cond[:], d["cond"]).then_inc(loaded["small"], 16)
                act.dma_start(feat[:], d["feat"]).then_inc(loaded["small"], 16)
                act.dma_start(mask[:], d["mask"]).then_inc(loaded["small"], 16)
                act.dma_start(rows[:], d["rows"]).then_inc(loaded["small"], 16)
                act.wait_ge(loaded["small"], 64)
                act.activation(silu[:], condT, ACT.Exp, scale=-1.0).then_inc(silu_exp, 1)

            @block.gpsimd
            def _(pool):
                nc.gpsimd.memset(eps[:, 0:1], 1e-8).then_inc(normed, 1)
                nc.gpsimd.memset(eps[:, 1:2], -0.5).then_inc(normed, 1)
                nc.gpsimd.memset(acc[:], 0.0)
                pool.wait_ge(summed, 2)
                pool.wait_ge(normed, 2)
                nc.gpsimd.tensor_tensor(scratch[:, 2:4], scratch[:, 0:2], eps[:, 0:1].to_broadcast([P, 2]), ALU.add).then_inc(normed, 1)
                pool.wait_ge(normed, 3)
                nc.gpsimd.tensor_tensor(scratch[:, 0:2], scratch[:, 2:4], eps[:, 1:2].to_broadcast([P, 2]), ALU.pow).then_inc(normed, 1)

            @block.vector
            def _(dve):
                own_prep = Own()
                dve.wait_ge(loaded["small"], 64)
                nc.vector.tensor_copy(condx[:], condT.unsqueeze(2).to_broadcast([C, B, S]))
                nc.vector.tensor_tensor_reduce(out=squares[:, 0:4], in0=quat, in1=quat, scale=1.0, scalar=0.0,
                                               op0=ALU.mult, op1=ALU.add, accum_out=scratch[:, 0:1]).then_inc(summed, 1)
                dve.wait_ge(summed, 1)
                nc.vector.tensor_tensor_reduce(out=squares[:], in0=quat_all, in1=quat_all, scale=1.0, scalar=0.0,
                                               op0=ALU.mult, op1=ALU.add, accum_out=scratch[:, 1:2]).then_inc(summed, 1)
                dve.wait_ge(silu_exp, 1)
                nc.vector.tensor_scalar(silu[:], silu[:], 1.0, None, ALU.add).then_inc(prep, 1)
                dve.wait_ge(prep, own_prep.next())
                nc.vector.reciprocal(silu[:], silu[:]).then_inc(prep, 1)
                dve.wait_ge(prep, own_prep.next())
                nc.vector.tensor_tensor(silu[:], silu[:], condT, ALU.mult).then_inc(silu_exp, 1)
                nc.vector.tensor_scalar(maskb[:], mask[:].bitcast(U8), MASKED, None, ALU.mult)
                nc.vector.tensor_scalar(router_w[1], router_w[1], rms1, None, ALU.mult)
                nc.vector.tensor_tensor(genre_b, genre_b, router_b[1], ALU.add).then_inc(prep, 1)
                own_prep.next()
                dve.wait_ge(loaded["const"], 16)
                dve.wait_ge(normed, 4)
                nc.vector.scalar_tensor_tensor(out=quat, in0=quat, scalar=scratch[:, 0:1], in1=k["sign_r"],
                                               op0=ALU.mult, op1=ALU.mult).then_inc(prep, 1)
                own_prep.next()
                nc.vector.scalar_tensor_tensor(out=quat_l, in0=quat_l, scalar=scratch[:, 1:2], in1=k["sign_l"],
                                               op0=ALU.mult, op1=ALU.mult).then_inc(prep, 1)
                dve.wait_ge(prep, own_prep.next())
                nc.vector.tensor_scalar(quat, quat, sgate, None, ALU.mult).then_inc(prep, 1)
                dve.wait_ge(prep, own_prep.next())
                for q, r in ((quat, rot_r), (quat_l, rot_l)):
                    nc.vector.tensor_tensor(r[:], k["diag4"].unsqueeze(1).to_broadcast([P, 4, S]),
                                            q.unsqueeze(2).to_broadcast([P, 4, S]), ALU.mult)
                nc.vector.tensor_copy(ident_b[:], k["ident"])
                dve.wait_ge(modulated, 1)
                for n in range(2):
                    nc.vector.tensor_scalar(shift[n][:], bank(0, 64 * n, 64 * n + 32), mod_b[n][:, 0:1], None, ALU.add)
                    nc.vector.tensor_scalar(gain[n][:], bank(0, 64 * n + 32, 64 * n + 64), mod_b[n][:, 1:2], 1.0, ALU.add, ALU.add).then_inc(prep, 1)
                    own_prep.next()
                dve.wait_ge(prep, own_prep.count)
                for n in range(2):
                    nc.vector.tensor_scalar(gain[n][:], gain[n][:], rms_s[n], None, ALU.mult)
                nc.vector.tensor_tensor(genre[:], bank(1, 0, 64).rearrange("p (n e) -> p n e", e=EXPERTS),
                                        genre_b.unsqueeze(1).to_broadcast([P, TILES, EXPERTS]), ALU.add)

            @block.tensor
            def _(pe):
                pe.wait_ge(silu_exp, 2)
                for n in range(2):
                    nc.tensor.matmul(bank(0, 64 * n, 64 * n + 32), mod_w[n][:, 0:E], silu[:], start=True, stop=True)
                    nc.tensor.matmul(bank(0, 64 * n + 32, 64 * n + 64), mod_w[n][:, E:2 * E], silu[:], start=True, stop=True)
                for n in range(TILES):
                    mm = nc.tensor.matmul(bank(1, 8 * n, 8 * n + 8), condx[:, SEQ * n:SEQ * n + SEQ, :], genre_w, start=True, stop=True)
                mm.then_inc(modulated, 1)
                pe.wait_ge(loaded["x"], 16)
                pe.wait_ge(loaded["cond_w0"], 16)

        def run_in_time_order(starts, steps, others=()):
            todo = [(starts[n] + time, n, step) for time, step in steps for n in range(TILES)] + list(others)
            for time, n, step in sorted(todo, key=lambda entry: entry[0]):
                step(n)

        def mixture_sync(sp, experts):
            outs = [u[5] for half in range(2) for u in mixture_plan(half, ((0.0, 1.0),) * 3) if u[1] == "out"]
            for g in experts:
                sp.wait_ge(unit_ps, outs[g - WB] + 1)
                load_expert(sp, g)

        def mixture_plan(half, jobs):
            rows = [[("mean", 0, 0, 0)] if half == 0 else [], [("transpose", 1, 0, 0), ("route", 1, 0, 0)], [("transpose_u", 1, 0, 0), ("gates", 1, 0, 0)]]
            first = [[("hidden", 0, e, f) for f in range(FF0 // P)] for e in range(EXPERTS)]
            rows[0] += first[0]
            for e in range(EXPERTS):
                rows[0] += (first[e + 1] if e + 1 < EXPERTS else []) + [("out", 0, e, 0)]
            inner = [[("hidden", 1, e, f) for f in range(FF1 // P)] for e in range(EXPERTS)]
            rows[1] += inner[0]
            for e in range(EXPERTS):
                rows[1] += [("hidden2", 1, e, f) for f in range(FF1 // P)] + (inner[e + 1] if e + 1 < EXPERTS else []) + [("out", 1, e, 0)]
            cost = {"hidden": 0.9, "hidden2": 1.75, "transpose": 0.9, "route": 0.5, "transpose_u": 0.9, "gates": 0.9, "mean": 0.2}
            plan, end, number = [], 0.0, half * ((1 + 2 * 5 * EXPERTS + 4))
            for row, (start, stretch) in zip(rows, jobs):
                time, start = 0.0, max(start, end)
                for kind, layer, e, f in row:
                    plan.append((half, kind, layer, e, f, number, start + stretch * time))
                    time += cost.get(kind, (3.5, 1.75)[layer])
                    if kind in ("route", "transpose"):
                        time += 2.0
                    number += 1
                end = start + stretch * time + 2.0
            return plan

        def read_of(number):
            return ring_read[number % 2], number // 2 + 1

        def mixture_tensor(pe, plan, logit_ready):
            numbers = {u[1:5]: u[5] for u in plan}

            def step(unit):
                half, kind, layer, e, f, number, _ = unit
                g = (2 * half + layer) * EXPERTS + e
                w, at, h = W[g % WB], RING[number % 2], hid[e % 2]
                tiles = range(HT * half, HT * half + HT)
                if number >= 2:
                    pe.wait_ge(ring_read[number % 2], number // 2)
                if kind == "mean":
                    pe.wait_ge(logit_ready, HT)
                    pe.wait_ge(mean_ready, 2)
                    mm = nc.tensor.matmul(bank(at, 0, 2), k["ones"], wsum[:], start=True, stop=True)
                elif kind == "transpose":
                    pe.wait_ge(added, g)
                    for n in tiles:
                        mm = nc.tensor.transpose(bank(at, P * (n % HT), P * (n % HT) + P), xres[:, n, :], k["ident"])
                elif kind == "transpose_u":
                    pe.wait_ge(added, g + EXPERTS)
                    for n in tiles:
                        mm = nc.tensor.transpose(bank(at, P * (n % HT), P * (n % HT) + P), acc[:, n, :], k["ident"])
                elif kind == "route":
                    pe.wait_ge(*read_of(number - 1))
                    for n in tiles:
                        mm = nc.tensor.matmul(bank(at, EXPERTS * (n % HT), EXPERTS * (n % HT) + EXPERTS), featT[:, P * n:P * n + P], router_w[1], start=True, stop=True)
                elif kind == "gates":
                    pe.wait_ge(*read_of(number - 1))
                    for n in tiles:
                        mm = nc.tensor.matmul(bank(at, NSMALL * (n % HT), NSMALL * (n % HT) + NSMALL), uT[:, P * n:P * n + P], small_w, start=True, stop=True)
                elif kind == "hidden":
                    pe.wait_ge(w_loaded[g % WB], loads_up_to(g))
                    mm = nc.tensor.matmul(bank(at), w[:, P * f:P * f + P], featT[:, BANK * half:BANK * half + BANK], start=True, stop=True)
                elif kind == "hidden2":
                    for c in range(FF1 // P):
                        pe.wait_ge(*read_of(numbers["hidden", 1, e, c]))
                    for c in range(FF1 // P):
                        lo = FF1 + FF1 * c + P * f
                        mm = nc.tensor.matmul(bank(at), w[:, lo:lo + P], h[:, c, :], start=(c == 0), stop=(c == FF1 // P - 1))
                else:
                    nf = (FF0, FF1)[layer] // P
                    for c in range(nf - 2, nf):
                        pe.wait_ge(*read_of(numbers["hidden2" if layer else "hidden", layer, e, c]))
                    for j in range(HT):
                        for c in range(nf):
                            lo = (FF0, FF1 + 2 * FF1)[layer] + E * c
                            mm = nc.tensor.matmul(bank(at, E * j, E * j + E), h[:, 2 * layer + c, P * j:P * j + P], w[:, lo:lo + E], start=(c == 0), stop=(c == nf - 1))
                mm.then_inc(unit_ps, 1)

            return [(u[6], u, step) for u in plan]

        def mixture_scalar(act, plan):
            def step(unit):
                half, kind, layer, e, f, number, _ = unit
                at = RING[number % 2]
                act.wait_ge(unit_ps, number + 1)
                if kind in ("transpose", "transpose_u"):
                    dst = featT if kind == "transpose" else uT
                    nc.scalar.activation(dst[:, BANK * half:BANK * half + BANK], bank(at), ACT.Copy).then_inc(ring_read[number % 2], 1)
                else:
                    g = (2 * half + layer) * EXPERTS + e
                    c = f + (2 if kind == "hidden2" else 0)
                    nc.scalar.activation(hid[e % 2][:, c, :], bank(at), ACT.Relu, bias=WBIAS[g % WB][:, c:c + 1]).then_inc(ring_read[number % 2], 1)

            def gate_exp(job):
                act.wait_ge(exp_in, job + 1)
                half = job // 2
                nc.scalar.activation(gatew[:], logits[:, HT * half:HT * half + HT, :], ACT.Exp).then_inc(exp_out, 1)

            def softplus(half):
                act.wait_ge(z_abs, half + 1)
                nc.scalar.activation(za[:], za[:], ACT.Exp).then_inc(z_exp, 1)
                act.wait_ge(z_exp, half + 1)
                nc.scalar.activation(za[:], za[:], ACT.Ln, bias=1.0).then_inc(z_log, 1)

            steps = [(u[6] + (1.9 if u[1] == "hidden2" else 1.0), u, step) for u in plan if u[1] in ("transpose", "transpose_u", "hidden", "hidden2")]
            return steps + gate_times(plan, 3.0, gate_exp, 2.0) + [(plan[-1][6] + 2.5, plan[-1][0], softplus)]

        def gate_times(plan, late0, step, late1):
            half = plan[0][0]
            routed = [u for u in plan if u[1] == "route"][0]
            return [(plan[0][6] + late0, 2 * half, step), (routed[6] + late1, 2 * half + 1, step)]

        def mixture_pool(pool, plan):
            def inverse_rms(half):
                pool.wait_ge(square_ready, half + 1)
                nc.gpsimd.tensor_scalar(st8[:, 1, :], st8[:, 0, :], 1.0 / E, 1e-6, ALU.mult, ALU.add).then_inc(mix_pool_step, 1)
                pool.wait_ge(mix_pool_step, own_mix_pool.next())
                nc.gpsimd.tensor_tensor(st8[:, 2, :], st8[:, 1, :], eps[:, 1:2].to_broadcast([P, HT]), ALU.pow).then_inc(rms_ready, 1)

            return [([u for u in plan if u[1] == "transpose"][0][6] + 1.5, plan[0][0], inverse_rms)]

        def mixture_vector(dve, plan, logit_ready=None):
            step_of = {}

            def sums(unit):
                half, kind, layer, e, f, number, _ = unit
                at, g = RING[number % 2], (2 * half + layer) * EXPERTS + e
                target = (xres, acc)[layer]
                dve.wait_ge(unit_ps, number + 1)
                if g:
                    dve.wait_ge(added, g)
                for j in range(HT):
                    n = HT * half + j
                    ins = nc.vector.scalar_tensor_tensor(out=target[:, n, :], in0=bank(at, E * j, E * j + E), scalar=gatew[:, j, e:e + 1],
                                                         in1=target[:, n, :], op0=ALU.mult, op1=ALU.add)
                ins.then_inc(ring_read[number % 2], 1)
                dve.wait_ge(*read_of(number))
                for j in range(HT):
                    n = HT * half + j
                    ins = nc.vector.scalar_tensor_tensor(out=target[:, n, :], in0=last_b[layer][:, e, :], scalar=gatew[:, j, e:e + 1],
                                                         in1=target[:, n, :], op0=ALU.mult, op1=ALU.add)
                ins.then_inc(added, 1)

            def magnitudes(_):
                dve.wait_ge(loaded["late"], 16 * 6)
                for n in range(2):
                    nc.vector.tensor_reduce(wsum[:, n:n + 1], ffn_w[n][:], X, ALU.add, apply_absolute_value=True).then_inc(mean_ready, 1)

            def means(unit):
                number = unit[5]
                dve.wait_ge(unit_ps, number + 1)
                nc.vector.tensor_scalar(wmean[:], bank(RING[number % 2], 0, 2), 1.0 / (E * HID), 1e-5, ALU.mult, ALU.max).then_inc(ring_read[number % 2], 1)
                dve.wait_ge(*read_of(number))
                nc.vector.reciprocal(wscale[:], wmean[:]).then_inc(mix_step, 1)
                dve.wait_ge(mix_step, own_mix.next())
                for n in range(2):
                    nc.vector.tensor_scalar(ffn_t[:, n, :], ffn_w[n][:], wscale[:, n:n + 1], ROUND, ALU.mult, ALU.add).then_inc(mix_step, 1)
                    own_mix.next()
                dve.wait_ge(mix_step, own_mix.count)
                for n in range(2):
                    nc.vector.tensor_scalar(ffn_t[:, n, :], ffn_t[:, n, :], ROUND, 1.0, ALU.subtract, ALU.min).then_inc(mix_step, 1)
                    own_mix.next()
                dve.wait_ge(mix_step, own_mix.count)
                for n in range(2):
                    nc.vector.tensor_scalar(ffn_q[n][:], ffn_t[:, n, :], -1.0, None, ALU.max)

            def squares(half):
                dve.wait_ge(added, (2 * half + 1) * EXPERTS)
                nc.vector.tensor_tensor(sq[:], xres[:, HT * half:HT * half + HT, :], xres[:, HT * half:HT * half + HT, :], ALU.mult).then_inc(mix_step, 1)
                dve.wait_ge(mix_step, own_mix.next())
                nc.vector.tensor_reduce(st8[:, 0, :], sq[:], X, ALU.add).then_inc(square_ready, 1)

            def choose(job):
                half, layer = job // 2, job % 2
                bc = [P, HT, EXPERTS]
                here = logits[:, HT * half:HT * half + HT, :]
                if job == 0:
                    dve.wait_ge(logit_ready, HT)
                if layer:
                    number = [u for u in plan if u[1] == "route"][0][5]
                    dve.wait_ge(unit_ps, number + 1)
                    dve.wait_ge(rms_ready, half + 1)
                    nc.vector.tensor_tensor(here, bank(RING[number % 2], 0, HT * EXPERTS).rearrange("p (n e) -> p n e", e=EXPERTS),
                                            st8[:, 2, :].unsqueeze(2).to_broadcast(bc), ALU.mult).then_inc(ring_read[number % 2], 1)
                    dve.wait_ge(*read_of(number))
                    nc.vector.tensor_tensor(here, here, genre[:, HT * half:HT * half + HT, :], ALU.add).then_inc(mix_step, 1)
                    dve.wait_ge(mix_step, own_mix.next())
                for n in range(HT):
                    ins = nc.vector.max(top[:, n, :], logits[:, HT * half + n, :])
                ins.then_inc(mix_step, 1)
                dve.wait_ge(mix_step, own_mix.next())
                for n in range(HT):
                    ins = nc.vector.max_index(topi[:, n, :], top[:, n, :], logits[:, HT * half + n, :])
                ins.then_inc(mix_step, 1)
                dve.wait_ge(mix_step, own_mix.next())
                nc.vector.tensor_tensor(here, here, top[:, :, 0:1].to_broadcast(bc), ALU.subtract).then_inc(exp_in, 1)
                nc.vector.tensor_copy(topf[:], topi[:, :, 0:2]).then_inc(mix_step, 1)
                dve.wait_ge(mix_step, own_mix.next())
                for j in range(2):
                    nc.vector.tensor_tensor(chosen[:, j], k["iota"].unsqueeze(1).to_broadcast(bc), topf[:, :, j:j + 1].to_broadcast(bc), ALU.is_equal).then_inc(mix_step, 1)
                    own_mix.next()
                dve.wait_ge(mix_step, own_mix.count)
                nc.vector.tensor_tensor(chosen[:, 0], chosen[:, 0], chosen[:, 1], ALU.add).then_inc(mix_step, 1)
                step_of[job] = own_mix.next()

            def weigh(job):
                layer = job % 2
                dve.wait_ge(mix_step, step_of[job])
                dve.wait_ge(exp_out, job + 1)
                nc.vector.tensor_tensor(chosen[:, 0], chosen[:, 0], gatew[:], ALU.mult).then_inc(mix_step, 1)
                dve.wait_ge(mix_step, own_mix.next())
                nc.vector.tensor_reduce(total[:], chosen[:, 0] if layer == 0 else gatew[:], X, ALU.add).then_inc(mix_step, 1)
                dve.wait_ge(mix_step, own_mix.next())
                nc.vector.reciprocal(rtotal[:], total[:]).then_inc(mix_step, 1)
                dve.wait_ge(mix_step, own_mix.next())
                nc.vector.tensor_tensor(gatew[:], chosen[:, 0], rtotal[:].unsqueeze(2).to_broadcast([P, HT, EXPERTS]), ALU.mult).then_inc(gate_ready, 1)
                dve.wait_ge(gate_ready, job + 1)

            def gates_in(unit):
                half, number = unit[0], unit[5]
                here = z[:, HT * half:HT * half + HT, :]
                dve.wait_ge(unit_ps, number + 1)
                nc.vector.tensor_tensor(here, bank(RING[number % 2], 0, HT * NSMALL).rearrange("p (n c) -> p n c", c=NSMALL),
                                        small_b.unsqueeze(1).to_broadcast([P, HT, NSMALL]), ALU.add).then_inc(ring_read[number % 2], 1)
                dve.wait_ge(*read_of(number))
                nc.vector.scalar_tensor_tensor(out=za[:], in0=here, scalar=-1.0, in1=here, op0=ALU.mult, op1=ALU.min).then_inc(z_abs, 1)

            def gates_out(half):
                here = z[:, HT * half:HT * half + HT, :]
                dve.wait_ge(z_log, half + 1)
                nc.vector.scalar_tensor_tensor(out=here, in0=here, scalar=0.0, in1=za[:], op0=ALU.max, op1=ALU.add).then_inc(z_ready, 1)

            half = plan[0][0]
            moved = [u for u in plan if u[1] == "transpose"][0]
            steps = [(u[6] + (3.8, 2.2)[u[2]], u, sums) for u in plan if u[1] == "out"]
            steps += [(u[6] + 0.5, u, means) for u in plan if u[1] == "mean"]
            steps += [(moved[6] + 0.2, half, squares), (plan[-1][6] + 1.5, plan[-1], gates_in), (plan[-1][6] + 4.0, half, gates_out)]
            if half == 0:
                steps.append((max(plan[0][6] - 3.0, 0.0), 0, magnitudes))
            return steps + gate_times(plan, 1.0, choose, 1.0) + gate_times(plan, 4.0, weigh, 3.5)

        CS = 2
        COND_BANKS = ((0, 1) * 2 + (0,) * 4, (0,) * 4 + (0, 1) * 2)
        cxs = [sb(f"cond_xs{s}", [P, P]) for s in range(CS)]
        cqkv = [sb(f"cond_qkv{s}", [P, 3 * P]) for s in range(CS)]
        ckbd = [sb(f"cond_kbd{s}", [P, CH, P]) for s in range(CS)]
        csm = [sb(f"cond_sm{s}", [P, CH, S]) for s in range(CS)]
        cvbd = [sb(f"cond_vbd{s}", [P, CH, 4, CD]) for s in range(CS)]
        cptbd = [sb(f"cond_ptbd{s}", [P, CH, P]) for s in range(CS)]
        cmx, csums, crec = ([sb(f"cond_{n}{s}", [P, CH]) for s in range(CS)] for n in ("mx", "sums", "rec"))
        coT, czn = ([sb(f"cond_{n}{s}", [P, P]) for s in range(CS)] for n in ("oT", "zn"))
        cst = [sb(f"cond_st{s}", [P, 4]) for s in range(CS)]
        c_xT_ps, c_xT_ready, c_qkv_ps, c_qkv_ready = sem("cond_xT_ps"), sem("cond_xT_ready"), sem("cond_qkv_ps"), sem("cond_qkv_ready")
        c_kbd_ready, c_scores_ps, c_scores_ready = sem("cond_kbd_ready"), sem("cond_scores_ps"), sem("cond_scores_ready")
        c_probs_ready, c_probsT_ready, c_vbd_ready = sem("cond_probs_ready"), sem("cond_probsT_ready"), sem("cond_vbd_ready")
        c_oT_ps, c_oT_ready, c_z_ps, c_square_ready = sem("cond_oT_ps"), sem("cond_oT_ready"), sem("cond_z_ps"), sem("cond_square_ready")
        c_rstd_ready, c_zn_ready, c_znT_ps, c_done = sem("cond_rstd_ready"), sem("cond_zn_ready"), sem("cond_znT_ps"), sem("cond_done")
        c_zeroed = sem("cond_zeroed")

        def cond_pool(pool, layer, at, own, own_sem):
            base = layer * TILES

            def spread_keys(n):
                s = n % CS
                pool.wait_ge(c_qkv_ready, base + n + 1)
                nc.gpsimd.tensor_tensor(ckbd[s][:], cqkv[s][:, P:2 * P].unsqueeze(1).to_broadcast([P, CH, P]),
                                        k["headmask"].unsqueeze(2).to_broadcast([P, CH, P]), ALU.mult).then_inc(c_kbd_ready, 1)

            def spread_values(n):
                s = n % CS
                nc.gpsimd.tensor_tensor(cvbd[s][:], cqkv[s][:, 2 * P:3 * P].rearrange("p (h c) -> p h c", c=CD).unsqueeze(2).to_broadcast([P, CH, 4, CD]),
                                        k["ownquarter"].rearrange("p (h j) -> p h j", j=4).unsqueeze(3).to_broadcast([P, CH, 4, CD]), ALU.mult).then_inc(c_vbd_ready, 1)

            def inverse_rms(n):
                s = n % CS
                pool.wait_ge(c_square_ready, base + n + 1)
                nc.gpsimd.tensor_scalar(cst[s][:, 1:2], cst[s][:, 0:1], 1.0 / E, 1e-6, ALU.mult, ALU.add).then_inc(own_sem, 1)
                pool.wait_ge(own_sem, own.next())
                nc.gpsimd.tensor_tensor(cst[s][:, 2:3], cst[s][:, 1:2], eps[:, 1:2], ALU.pow).then_inc(c_rstd_ready, 1)

            return [(at["c_spread_keys"], spread_keys), (at["c_spread_values"], spread_values), (at["c_inverse_rms"], inverse_rms)]

        def cond_tensor(pe, layer, at, ready=None):
            base, w = layer * TILES, cond_w[layer]

            def transpose_x(n):
                s = n % CS
                if ready is not None:
                    pe.wait_ge(ready, n + 1)
                before = [m for m in range(n) if m == n - CS or COND_BANKS[layer][m] == COND_BANKS[layer][n]]
                if before:
                    pe.wait_ge(c_done, base + max(before) + 1)
                nc.tensor.transpose(bank(COND_BANKS[layer][n], 0, P), xres[:, n, :], k["ident"]).then_inc(c_xT_ps, 1)

            def project(n):
                s = n % CS
                pe.wait_ge(c_xT_ready, base + n + 1)
                nc.tensor.matmul(bank(COND_BANKS[layer][n], P, 2 * P), w[:, 0:E], cxs[s][:], start=True, stop=True)
                nc.tensor.matmul(bank(COND_BANKS[layer][n], 2 * P, 3 * P), w[:, E:2 * E], cxs[s][:], start=True, stop=True)
                nc.tensor.matmul(bank(COND_BANKS[layer][n], 3 * P, 4 * P), cxs[s][:], w[:, 2 * E:3 * E], start=True, stop=True).then_inc(c_qkv_ps, 1)

            def scores(n):
                s = n % CS
                pe.wait_ge(c_kbd_ready, base + n + 1)
                for b in range(SEQ):
                    mm = nc.tensor.matmul(bank(COND_BANKS[layer][n])[S * b:S * b + S, :], cqkv[s][:, S * b:S * b + S],
                                          ckbd[s][:, :, S * b:S * b + S], start=True, stop=True)
                mm.then_inc(c_scores_ps, 1)

            def times_values(n):
                s = n % CS
                pe.wait_ge(c_probsT_ready, base + n + 1)
                pe.wait_ge(c_vbd_ready, base + n + 1)
                for m in range(4):
                    for g in range(4):
                        h = 4 * g + m
                        mm = nc.tensor.matmul(bank(COND_BANKS[layer][n], P, 2 * P)[S * g:S * g + S, :], cvbd[s][:, h].rearrange("p j c -> p (j c)"),
                                              cptbd[s][:, h, :], start=(m == 0), stop=(m == 3))
                mm.then_inc(c_oT_ps, 1)

            def project_o(n):
                s = n % CS
                pe.wait_ge(c_oT_ready, base + n + 1)
                nc.tensor.matmul(bank(COND_BANKS[layer][n], 2 * P, 3 * P), coT[s][:], w[:, 3 * E:4 * E], start=True, stop=True).then_inc(c_z_ps, 1)

            def transpose_z(n):
                s = n % CS
                pe.wait_ge(c_zn_ready, base + n + 1)
                nc.tensor.transpose(bank(COND_BANKS[layer][n], 3 * P, 4 * P), czn[s][:], k["ident"]).then_inc(c_znT_ps, 1)

            return [(at["c_transpose_x"], transpose_x), (at["c_project"], project), (at["c_scores"], scores),
                    (at["c_times_values"], times_values), (at["c_project_o"], project_o),
                    (at["c_transpose_z"], transpose_z)]

        def cond_scalar(act, layer, at):
            base = layer * TILES

            def copy_x(n):
                s = n % CS
                act.wait_ge(c_xT_ps, base + n + 1)
                nc.scalar.activation(cxs[s][:], bank(COND_BANKS[layer][n], 0, P), ACT.Copy).then_inc(c_xT_ready, 1)

            def copy_qkv(n):
                s = n % CS
                act.wait_ge(c_qkv_ps, base + n + 1)
                nc.scalar.activation(cqkv[s][:], bank(COND_BANKS[layer][n], P, 4 * P), ACT.Copy).then_inc(c_qkv_ready, 1)

            def exponentials(n):
                s = n % CS
                act.wait_ge(c_scores_ready, base + n + 1)
                nc.scalar.activation(csm[s][:], csm[s][:], ACT.Exp).then_inc(c_probs_ready, 1)

            def copy_oT(n):
                s = n % CS
                act.wait_ge(c_oT_ps, base + n + 1)
                nc.scalar.activation(coT[s][:], bank(COND_BANKS[layer][n], P, 2 * P), ACT.Copy).then_inc(c_oT_ready, 1)

            def squares(n):
                s = n % CS
                act.wait_ge(c_z_ps, base + n + 1)
                nc.scalar.activation(czn[s][:], bank(COND_BANKS[layer][n], 2 * P, 3 * P), ACT.Square, accum_out=cst[s][:, 0:1]).then_inc(c_square_ready, 1)

            def normalise(n):
                s = n % CS
                act.wait_ge(c_rstd_ready, base + n + 1)
                nc.scalar.activation(czn[s][:], bank(COND_BANKS[layer][n], 2 * P, 3 * P), ACT.Copy, scale=cst[s][:, 2:3]).then_inc(c_zn_ready, 1)

            def modulate(n):
                s = n % CS
                act.wait_ge(c_znT_ps, base + n + 1)
                for b in range(SEQ):
                    q = SEQ * n + b
                    ins = nc.scalar.activation(featT[:, P * n + S * b:P * n + S * b + S], bank(COND_BANKS[layer][n], 3 * P + S * b, 3 * P + S * b + S), ACT.Identity,
                                               scale=gain[layer][:, q:q + 1], bias=shift[layer][:, q:q + 1])
                ins.then_inc(c_done, 1)

            return [(at["c_modulate"], modulate), (at["c_copy_x"], copy_x), (at["c_copy_qkv"], copy_qkv), (at["c_exponentials"], exponentials),
                    (at["c_copy_oT"], copy_oT), (at["c_squares"], squares), (at["c_normalise"], normalise)]

        def cond_vector(dve, layer, at, own, own_sem):
            base = layer * TILES
            scale = float(CD) ** -0.5

            def softmax_in(n):
                s = n % CS
                dve.wait_ge(c_scores_ps, base + n + 1)
                nc.vector.scalar_tensor_tensor(out=csm[s][:], in0=bank(COND_BANKS[layer][n]).rearrange("p (h t) -> p h t", t=S), scalar=scale,
                                               in1=maskb[:].unsqueeze(1).to_broadcast([P, CH, S]),
                                               op0=ALU.mult, op1=ALU.add).then_inc(own_sem, 1)
                dve.wait_ge(own_sem, own.next())
                nc.vector.tensor_reduce(cmx[s][:], csm[s][:], X, ALU.max).then_inc(own_sem, 1)
                dve.wait_ge(own_sem, own.next())
                nc.vector.tensor_tensor(csm[s][:], csm[s][:], cmx[s][:].unsqueeze(2).to_broadcast([P, CH, S]), ALU.subtract).then_inc(c_scores_ready, 1)

            def turn(n):
                s = n % CS
                dve.wait_ge(c_probs_ready, base + n + 1)
                nc.vector.tensor_reduce(csums[s][:], csm[s][:], X, ALU.add).then_inc(own_sem, 1)
                dve.wait_ge(own_sem, own.next())
                nc.vector.reciprocal(crec[s][:], csums[s][:]).then_inc(own_sem, 1)
                dve.wait_ge(own_sem, own.next())
                nc.vector.tensor_tensor(csm[s][:], csm[s][:], crec[s][:].unsqueeze(2).to_broadcast([P, CH, S]), ALU.mult).then_inc(own_sem, 1)
                dve.wait_ge(own_sem, own.next())
                for b in range(SEQ):
                    last = nc.vector.transpose(cptbd[s][S * b:S * b + S, :, S * b:S * b + S], csm[s][S * b:S * b + S, :, :])
                last.then_inc(c_probsT_ready, 1)

            return [(at["c_softmax_in"], softmax_in), (at["c_turn"], turn)]

        def first_phase():
            with ExitStack() as scope:
                def lsb(name, shape, dt=F32):
                    return scope.enter_context(nc.sbuf_tensor("rot_" + name, shape, dt))

                def lsem(name):
                    return sem("rot_" + name)

                NC_ = AH * AD // P
                SLOTS = 2
                qk, sh = lsb("qk", [P, SLOTS, 2 * NC_, P]), lsb("sh", [P, SLOTS, 2 * NC_, P])
                v = lsb("v", [P, AH * AD])
                sm = lsb("sm", [P, AH, S])
                ptbd = lsb("ptbd", [P, AH, P])
                oT = lsb("oT", [P, NC_, P])
                mx, sums, rec = lsb("mx", [P, AH]), lsb("sums", [P, AH]), lsb("rec", [P, AH])
                mxT, mr1 = lsb("xT", [P, P]), lsb("r1", [P, P])
                zeroed, dve_step, pool_step = lsem("zeroed"), lsem("dve_step"), lsem("pool_step")
                q_ps, k_ps, v_ps = lsem("q_ps"), lsem("k_ps"), lsem("v_ps")
                qk_copied, shuffled, rotated, qk_ready = lsem("qk_copied"), lsem("shuffled"), lsem("rotated"), lsem("qk_ready")
                masked = lsem("masked")
                v_ready, low_ps, high_ps, low_read, high_read = lsem("v_ready"), lsem("low_ps"), lsem("high_ps"), lsem("low_read"), lsem("high_read")
                scores_ready, probs_ready, probsT_ready = lsem("scores_ready"), lsem("probs_ready"), lsem("probsT_ready")
                oT_ps, oT_ready, out_ps, x_ready = lsem("oT_ps"), lsem("oT_ready"), lsem("out_ps"), lsem("x_ready")
                xT_ps, xT_ready, r1_ps, r1_ready = lsem("xT_ps"), lsem("xT_ready"), lsem("r1_ps"), lsem("r1_ready")
                f_ps, f_ready, logit_ps, logit_ready = lsem("f_ps"), lsem("f_ready"), lsem("logit_ps"), lsem("logit_ready")
                scale = float(AD) ** -0.5
                swap = [(n + ROT // 2) % ROT for n in range(ROT)]
                starts = (-105.6, -64.9, -25.1, 15.3, 119.6, 199.6, 290.2, 365.9)
                jobs = ((202.3, 1), (261.2, 3.97), (508.3, 7.49))
                at = dict(c_spread_keys=0, c_transpose_x=3.23, c_copy_x=6.92, c_project=8.73, c_copy_qkv=9.96,
                          c_scores=24.68, c_softmax_in=30.24, c_exponentials=35.25, c_turn=35.67,
                          c_spread_values=39.43, c_times_values=56.22, c_copy_oT=56.71, c_inverse_rms=57.19,
                          c_project_o=63.08, c_squares=64.38, c_normalise=71.45, c_transpose_z=74.03,
                          c_modulate=74.38, rotate_parts_0=82.62, rotate_parts_1=85.97, queries=86.62,
                          partner_rows_0=89.56, keys=90.07, copy_queries=90.54, copy_keys=90.98,
                          partner_rows_1=94.17, add_parts_0=94.88, add_parts_1=102.74, scores=115.25,
                          take_scores_0=115.85, take_scores_1=115.94, mask_scores=115.97, values=117.09,
                          copy_values=119.48, softmax_in=120.81, exponentials=123.62, softmax_out=125.46,
                          copy_oT_0=134.42, times_values_0=141.46, times_values_1=142.5, copy_oT_1=144.16,
                          add_output=151.34, output=153.84, copy_xT=163.68, transpose_x=163.78, rotate_right=168.92,
                          copy_right=170.69, rotate_left=176.79, copy_left=177.12, route=184.91, take_logits=187.21)
                QB, KB = 2, 4
                MB = (6, RING[1]) * (HT // 2) + (6,) * HT
                place = [8 * (h // 8) + 4 * (h % 2) + (h // 2) % 4 for h in range(AH)]

                plan = mixture_plan(0, jobs)

                with nc.Block() as block:
                    @block.sync
                    def _(sp):
                        mixture_sync(sp, range(WB, EXPERTS * 2 + WB))

                    @block.gpsimd
                    def _(pool):
                        for s in range(CS):
                            nc.gpsimd.memset(cptbd[s][:], 0.0).then_inc(c_zeroed, 1)
                        nc.gpsimd.memset(ptbd[:], 0.0).then_inc(zeroed, 1)

                        def rotate_parts(part):
                            def step(n):
                                pool.wait_ge(shuffled, 2 * n + part + 1)
                                here = sh[:, n % SLOTS, NC_ * part:NC_ * part + NC_, :].rearrange("p c (b t) -> p (c b) t", t=S)
                                nc.gpsimd.tensor_tensor(here, here, k["sin"].unsqueeze(1).to_broadcast([P, NC_ * SEQ, S]), ALU.mult).then_inc(rotated, 1)
                            return step

                        def mask_scores(n):
                            pool.wait_ge(high_read, n + 1)
                            nc.gpsimd.tensor_tensor(sm[:], sm[:], k["causal"].unsqueeze(1).to_broadcast([P, AH, S]), ALU.add).then_inc(masked, 1)

                        run_in_time_order(starts, cond_pool(pool, 0, at, Own(), pool_step) + [(at["rotate_parts_0"], rotate_parts(0)), (at["rotate_parts_1"], rotate_parts(1)), (at["mask_scores"], mask_scores)], mixture_pool(pool, plan))

                    @block.tensor
                    def _(pe):
                        def queries(n):
                            pe.wait_ge(c_done, n + 1)
                            if n:
                                pe.wait_ge(v_ready, n)
                            for c in range(NC_):
                                mm = nc.tensor.matmul(bank(QB + c // 4, P * (c % 4), P * (c % 4) + P), wqk[:, P * c:P * c + P], featT[:, P * n:P * n + P], start=True, stop=True)
                            mm.then_inc(q_ps, 1)

                        def keys(n):
                            if n:
                                pe.wait_ge(high_read, n)
                            for c in range(NC_):
                                mm = nc.tensor.matmul(bank(KB + c // 4, P * (c % 4), P * (c % 4) + P), wqk[:, P * (NC_ + c):P * (NC_ + c) + P], featT[:, P * n:P * n + P], start=True, stop=True)
                            mm.then_inc(k_ps, 1)

                        def values(n):
                            pe.wait_ge(low_read, n + 1)
                            for c in range(2):
                                mm = nc.tensor.matmul(bank(QB + c), featT[:, P * n:P * n + P], wv[:, BANK * c:BANK * c + BANK], start=True, stop=True)
                            mm.then_inc(v_ps, 1)

                        def scores(n):
                            pe.wait_ge(qk_ready, 2 * n + 2)
                            for h in range(AH):
                                r, c = AD * (h % 2), h // 2
                                at, col = (QB if h < 8 else KB) + h % 2, P * (c % 4)
                                mm = nc.tensor.matmul(bank(at, col, col + P), qk[r:r + AD, n % SLOTS, c, :], qk[r:r + AD, n % SLOTS, NC_ + c, :], start=True, stop=True)
                                if h == 7:
                                    mm.then_inc(low_ps, 1)
                            mm.then_inc(high_ps, 1)

                        def times_values(part):
                            def step(n):
                                if part == 0:
                                    pe.wait_ge(probsT_ready, n + 1)
                                    pe.wait_ge(v_ready, n + 1)
                                    before = [m for m in range(n) if MB[m] == MB[n]]
                                    if before:
                                        pe.wait_ge(logit_ready, max(before) + 1)
                                else:
                                    pe.wait_ge(oT_ready, 2 * n + 1)
                                for h in range(8 * part, 8 * part + 8):
                                    r, c = AD * (h % 2), h // 2
                                    mm = nc.tensor.matmul(bank(MB[n], P * (c % 4), P * (c % 4) + P)[r:r + AD, :], v[:, AD * h:AD * h + AD], ptbd[:, place[h], :], start=True, stop=True)
                                mm.then_inc(oT_ps, 1)
                            return step

                        def output(n):
                            pe.wait_ge(oT_ready, 2 * n + 2)
                            for c in range(NC_):
                                mm = nc.tensor.matmul(bank(MB[n], 0, E), oT[:, c, :], wout[:, c, :], start=(c == 0), stop=(c == NC_ - 1))
                            mm.then_inc(out_ps, 1)

                        def transpose_x(n):
                            pe.wait_ge(x_ready, n + 1)
                            nc.tensor.transpose(bank(MB[n], P, 2 * P), xres[:, n, :], k["ident"]).then_inc(xT_ps, 1)

                        def rotate_right(n):
                            pe.wait_ge(xT_ready, n + 1)
                            nc.tensor.matmul(bank(MB[n], 2 * P, 3 * P), rot_r[:].rearrange("p a s -> p (a s)"), mxT[:], start=True, stop=True).then_inc(r1_ps, 1)

                        def rotate_left(n):
                            pe.wait_ge(r1_ready, n + 1)
                            nc.tensor.matmul(bank(MB[n], 3 * P, 4 * P), rot_l[:].rearrange("p a s -> p (a s)"), mr1[:], start=True, stop=True).then_inc(f_ps, 1)

                        def route(n):
                            pe.wait_ge(f_ready, n + 1)
                            nc.tensor.matmul(bank(MB[n], 0, EXPERTS), featT[:, P * n:P * n + P], router_w[0], start=True, stop=True).then_inc(logit_ps, 1)

                        pe.wait_ge(loaded["attn"], 48)
                        run_in_time_order(starts, cond_tensor(pe, 0, at) + [
                            (at["queries"], queries), (at["keys"], keys), (at["scores"], scores), (at["values"], values), (at["times_values_0"], times_values(0)), (at["times_values_1"], times_values(1)), (at["output"], output),
                            (at["transpose_x"], transpose_x), (at["rotate_right"], rotate_right), (at["rotate_left"], rotate_left), (at["route"], route)], mixture_tensor(pe, plan, logit_ready))

                    @block.scalar
                    def _(act):
                        def copy_queries(n):
                            act.wait_ge(q_ps, n + 1)
                            if n >= SLOTS:
                                act.wait_ge(high_ps, n - SLOTS + 1)
                            for c in range(2):
                                ins = nc.scalar.activation(qk[:, n % SLOTS, 4 * c:4 * c + 4, :].rearrange("p c t -> p (c t)"), bank(QB + c), ACT.Copy)
                            ins.then_inc(qk_copied, 1)

                        def copy_keys(n):
                            act.wait_ge(k_ps, n + 1)
                            for c in range(2):
                                ins = nc.scalar.activation(qk[:, n % SLOTS, NC_ + 4 * c:NC_ + 4 * c + 4, :].rearrange("p c t -> p (c t)"), bank(KB + c), ACT.Copy)
                            ins.then_inc(qk_copied, 1)

                        def copy_values(n):
                            act.wait_ge(v_ps, n + 1)
                            if n:
                                act.wait_ge(oT_ps, 2 * n)
                            for c in range(2):
                                ins = nc.scalar.activation(v[:, BANK * c:BANK * c + BANK], bank(QB + c), ACT.Copy)
                            ins.then_inc(v_ready, 1)

                        def take_scores(g):
                            def step(n):
                                if n and g == 0:
                                    act.wait_ge(probsT_ready, n)
                                act.wait_ge(low_ps if g == 0 else high_ps, n + 1)
                                src = PS[:, (QB + 2 * g) * BANK:(QB + 2 * g + 2) * BANK].rearrange("p (h t) -> p h t", t=P)
                                for b in range(SEQ):
                                    r = slice(S * b, S * b + S)
                                    ins = nc.scalar.activation(sm[r, 8 * g:8 * g + 8, :], src[r][:, :, S * b:S * b + S], ACT.Copy, scale=scale)
                                ins.then_inc(low_read if g == 0 else high_read, 1)
                            return step

                        def exponentials(n):
                            act.wait_ge(scores_ready, n + 1)
                            nc.scalar.activation(sm[:], sm[:], ACT.Exp).then_inc(probs_ready, 1)

                        def copy_oT(part):
                            def step(n):
                                act.wait_ge(oT_ps, 2 * n + part + 1)
                                if n and part == 0:
                                    act.wait_ge(out_ps, n)
                                nc.scalar.activation(oT[:, 4 * part:4 * part + 4, :].rearrange("p c t -> p (c t)"), bank(MB[n]), ACT.Copy).then_inc(oT_ready, 1)
                            return step

                        def copy_xT(n):
                            act.wait_ge(xT_ps, n + 1)
                            if n:
                                act.wait_ge(r1_ps, n)
                            nc.scalar.activation(mxT[:], bank(MB[n], P, 2 * P), ACT.Copy).then_inc(xT_ready, 1)

                        def copy_right(n):
                            act.wait_ge(r1_ps, n + 1)
                            if n:
                                act.wait_ge(f_ps, n)
                            nc.scalar.activation(mr1[:], bank(MB[n], 2 * P, 3 * P), ACT.Copy).then_inc(r1_ready, 1)

                        def copy_left(n):
                            act.wait_ge(f_ps, n + 1)
                            nc.scalar.activation(featT[:, P * n:P * n + P], bank(MB[n], 3 * P, 4 * P), ACT.Copy).then_inc(f_ready, 1)

                        run_in_time_order(starts, cond_scalar(act, 0, at) + [
                            (at["copy_queries"], copy_queries), (at["copy_keys"], copy_keys), (at["copy_values"], copy_values), (at["take_scores_0"], take_scores(0)), (at["take_scores_1"], take_scores(1)), (at["exponentials"], exponentials), (at["copy_oT_0"], copy_oT(0)), (at["copy_oT_1"], copy_oT(1)),
                            (at["copy_xT"], copy_xT), (at["copy_right"], copy_right), (at["copy_left"], copy_left)], mixture_scalar(act, plan))

                    @block.vector
                    def _(dve):
                        own = Own()

                        def partner_rows(part):
                            def step(n):
                                dve.wait_ge(qk_copied, 2 * n + part + 1)
                                here = slice(NC_ * part, NC_ * part + NC_)
                                nc.vector.stream_shuffle(sh[:, n % SLOTS, here, :], qk[:, n % SLOTS, here, :], swap).then_inc(shuffled, 1)
                                cosines = qk[:, n % SLOTS, here, :].rearrange("p c (b t) -> p (c b) t", t=S)
                                nc.vector.tensor_tensor(cosines, cosines, k["cos"].unsqueeze(1).to_broadcast([P, NC_ * SEQ, S]), ALU.mult).then_inc(dve_step, 1)
                                dve.wait_ge(dve_step, own.next())
                            return step

                        def add_parts(part):
                            def step(n):
                                dve.wait_ge(rotated, 2 * n + part + 1)
                                here = slice(NC_ * part, NC_ * part + NC_)
                                nc.vector.tensor_tensor(qk[:, n % SLOTS, here, :], qk[:, n % SLOTS, here, :], sh[:, n % SLOTS, here, :], ALU.add).then_inc(qk_ready, 1)
                            return step

                        def softmax_in(n):
                            dve.wait_ge(masked, n + 1)
                            nc.vector.tensor_reduce(mx[:], sm[:], X, ALU.max).then_inc(dve_step, 1)
                            dve.wait_ge(dve_step, own.next())
                            nc.vector.tensor_tensor(sm[:], sm[:], mx[:].unsqueeze(2).to_broadcast([P, AH, S]), ALU.subtract).then_inc(scores_ready, 1)

                        def softmax_out(n):
                            dve.wait_ge(probs_ready, n + 1)
                            nc.vector.tensor_reduce(sums[:], sm[:], X, ALU.add).then_inc(dve_step, 1)
                            dve.wait_ge(dve_step, own.next())
                            nc.vector.reciprocal(rec[:], sums[:]).then_inc(dve_step, 1)
                            dve.wait_ge(dve_step, own.next())
                            nc.vector.tensor_tensor(sm[:], sm[:], rec[:].unsqueeze(2).to_broadcast([P, AH, S]), ALU.mult).then_inc(dve_step, 1)
                            dve.wait_ge(dve_step, own.next())
                            if n:
                                dve.wait_ge(oT_ps, 2 * n)
                            for b in range(SEQ):
                                last = nc.vector.transpose(ptbd[S * b:S * b + S, :, S * b:S * b + S], sm[S * b:S * b + S, :, :])
                            last.then_inc(probsT_ready, 1)

                        def add_output(n):
                            dve.wait_ge(out_ps, n + 1)
                            nc.vector.tensor_tensor(xres[:, n, :], xres[:, n, :], bank(MB[n], 0, E), ALU.add).then_inc(x_ready, 1)

                        def take_logits(n):
                            dve.wait_ge(logit_ps, n + 1)
                            nc.vector.tensor_tensor(logits[:, n, :], bank(MB[n], 0, EXPERTS), router_b[0], ALU.add).then_inc(logit_ready, 1)

                        dve.wait_ge(c_zeroed, CS)
                        dve.wait_ge(zeroed, 1)
                        run_in_time_order(starts, cond_vector(dve, 0, at, own, dve_step) + [
                            (at["partner_rows_0"], partner_rows(0)), (at["partner_rows_1"], partner_rows(1)), (at["add_parts_0"], add_parts(0)), (at["add_parts_1"], add_parts(1)),
                            (at["softmax_in"], softmax_in), (at["softmax_out"], softmax_out),
                            (at["add_output"], add_output), (at["take_logits"], take_logits)], mixture_vector(dve, plan, logit_ready))

        def second_phase():
            with ExitStack() as scope:
                def lsb(name, shape, dt=F32):
                    return scope.enter_context(nc.sbuf_tensor("log_" + name, shape, dt))

                def lsem(name):
                    return sem("log_" + name)

                qk, v = lsb("qk", [P, 2 * LH, P]), lsb("v", [P, LH * LD])
                gtri, decay, lamw, a = lsb("gtri", [P, LH, S]), lsb("decay", [P, LH, S]), lsb("lamw", [P, LH, S]), lsb("a", [P, LH, S])
                abd, yT = lsb("abd", [P, LH, P]), lsb("yT", [P, LH, P])
                out = lsb("out", [P, E])
                bn, mv, st = lsb("bn", [P, 6]), lsb("mv", [P, 2]), lsb("st", [P, 2])
                zeroed, dve_step, pool_step = lsem("zeroed"), lsem("dve_step"), lsem("pool_step")
                own = Own()

                gtri_ready, decay_ps, decay_ready, weight_ready = lsem("gtri_ready"), lsem("decay_ps"), lsem("decay_ready"), lsem("weight_ready")
                q_ps, k_ps, v_ps, q_ready, k_ready, v_ready = lsem("q_ps"), lsem("k_ps"), lsem("v_ps"), lsem("q_ready"), lsem("k_ready"), lsem("v_ready")
                scores_ps, a_ready, aT_ready, yT_ps, yT_ready, out_ps = lsem("scores_ps"), lsem("a_ready"), lsem("aT_ready"), lsem("yT_ps"), lsem("yT_ready"), lsem("out_ps")
                out_read, x_biased, var_ready, rstd_ready, x_ready = lsem("out_read"), lsem("x_biased"), lsem("var_ready"), lsem("rstd_ready"), lsem("x_ready")

                def fsb(name, shape, dt=F32):
                    return scope.enter_context(nc.sbuf_tensor("ffn_" + name, shape, dt))

                def fsem(name):
                    return sem("ffn_" + name)

                NF = HID // P
                xr, xq, xqT = fsb("xr", [P, P]), fsb("xq", [P, P], BF16), fsb("xqT", [P, P], BF16)
                m1, m2 = fsb("m1", [P, 4]), fsb("m2", [P, 4])
                dg, sbc = fsb("dg", [P, P]), fsb("sbc", [P, P])
                hp = fsb("hp", [P, NF, SEQ, S + 2])
                y, ys = fsb("y", [P, NF, SEQ, S]), fsb("ys", [P, NF, P])
                yr, yq, yqT = fsb("yr", [P, HID]), fsb("yq", [P, HID], BF16), fsb("yqT", [P, NF, P], BF16)
                outb = [fsb(f"outb{s}", [P, E]) for s in range(2)]
                stored = [fsem(f"stored{s}") for s in range(2)]
                f_zeroed, ct_ps, xq_ready, xqT_ps, xqT_ready = fsem("zeroed"), fsem("ct_ps"), fsem("xq_ready"), fsem("xqT_ps"), fsem("xqT_ready")
                diag_ready, sbc_ps, sbc_ready, h_ps, h_ready = fsem("diag_ready"), fsem("sbc_ps"), fsem("sbc_ready"), fsem("h_ps"), fsem("h_ready")
                mid_ready, conv_ready, silu_ready, yt_ps, yq_ready = fsem("mid_ready"), fsem("conv_ready"), fsem("silu_ready"), fsem("yt_ps"), fsem("yq_ready")
                yqT_ps, yqT_ready, o_ps, o_ready = fsem("yqT_ps"), fsem("yqT_ready"), fsem("o_ps"), fsem("out_ready")

                scale = 1.0 / float(np.sqrt(LD))
                starts = (-9.6, 56, 134.4, 202.4, 268.4, 334.2, 400.2, 467.1)
                jobs = ((0, 0.96), (57.4, 3.38), (268.6, 3.86))
                at = dict(spread_gates=0, sum_gates=12.64, exp_decay=17.13, queries=23.45, level_weights=23.65,
                          keys=32.6, copy_queries=32.75, weigh_decay=38.6, copy_keys=39.74, scores=47.99,
                          weigh_scores=51.84, values=52.55, copy_values=57.5, times_values=61.91, copy_yT=67.27,
                          output=76.33, bias_x=79.4, norm_in=85.08, inverse_deviation=99.17, norm_out=100.41,
                          c_spread_keys=103.65, c_copy_x=105.52, c_transpose_x=107.44, c_project=109.87,
                          c_copy_qkv=111.92, c_spread_values=114.78, c_scores=122.88, c_softmax_in=124.14,
                          c_exponentials=132.38, c_turn=140.02, c_times_values=146.27, c_inverse_rms=149.18,
                          c_copy_oT=150, c_project_o=151.65, c_squares=152.19, c_normalise=158.84,
                          c_transpose_z=161.79, c_modulate=166.07, scale_diagonal=169.48, transpose_c=175.25,
                          quantise_x=175.48, transpose_xq=182.54, copy_xqT=183.07, copy_scale=184.52,
                          pad_hidden=187.46, spread_scale=187.49, hidden=188.59, middle_tap=192.53,
                          outer_taps=195.57, silus=203.82, transpose_y=211.29, quantise_y=212.59,
                          transpose_yq=220.87, copy_yqT=221.32, down=223.53, finish=234.71)
                plan = mixture_plan(1, jobs)
                QB, KB, FB = 2, 4, 6
                OUT_BANKS = (KB,) * HT + (RING[1],) * HT

                with nc.Block() as block:
                    @block.sync
                    def _(sp):
                        sp.dma_start(wqk[:], d["attn1_qk"]).then_inc(loaded["wattn1"], 16)
                        sp.dma_start(wv[:], d["attn1_v"]).then_inc(loaded["wattn1"], 16)
                        sp.dma_start(wout[:], d["attn1_out"].rearrange("(c p) e -> p c e", p=P)).then_inc(loaded["wattn1"], 16)
                        mixture_sync(sp, range(EXPERTS * 2 + WB, EXPERTS * 4))
                        for n in range(TILES):
                            sp.wait_ge(o_ready, n + 1)
                            sp.dma_start(d["out"][n], outb[n % 2][:]).then_inc(stored[n % 2], 16)
                        for s in range(2):
                            sp.wait_ge(stored[s], 16 * (TILES // 2))

                    @block.gpsimd
                    def _(pool):
                        own_pool = Own()
                        nc.gpsimd.memset(hp[:], 0.0).then_inc(f_zeroed, 1)
                        nc.gpsimd.memset(abd[:], 0.0).then_inc(zeroed, 1)
                        nc.gpsimd.memset(lamw[:], 0.0).then_inc(zeroed, 1)

                        def spread_gates(n):
                            pool.wait_ge(z_ready, n // HT + 1)
                            if n:
                                pool.wait_ge(decay_ps, n)
                            nc.gpsimd.tensor_tensor(gtri[:], z[:, n, 0:LH].unsqueeze(2).to_broadcast([P, LH, S]),
                                                    k["negafter"].unsqueeze(1).to_broadcast([P, LH, S]), ALU.mult).then_inc(gtri_ready, 1)

                        def bias_x(n):
                            nc.gpsimd.tensor_tensor(xres[:, n, :], xres[:, n, :], ln[:, 1, :], ALU.add).then_inc(x_biased, 1)

                        def inverse_deviation(n):
                            pool.wait_ge(var_ready, n + 1)
                            nc.gpsimd.tensor_scalar(st[:, 0:1], mv[:, 1:2], 1e-5, 1.0, ALU.add, ALU.mult).then_inc(pool_step, 1)
                            pool.wait_ge(pool_step, own_pool.next())
                            nc.gpsimd.tensor_tensor(st[:, 1:2], st[:, 0:1], eps[:, 1:2], ALU.pow).then_inc(rstd_ready, 1)

                        def scale_diagonal(n):
                            pool.wait_ge(xq_ready, n + 1)
                            nc.gpsimd.tensor_tensor(dg[:], k["ident"], m1[:, 3:4].to_broadcast([P, P]), ALU.mult).then_inc(diag_ready, 1)

                        run_in_time_order(starts, cond_pool(pool, 1, at, own_pool, pool_step) + [
                            (at["spread_gates"], spread_gates), (at["bias_x"], bias_x), (at["inverse_deviation"], inverse_deviation), (at["scale_diagonal"], scale_diagonal)], mixture_pool(pool, plan))

                    @block.tensor
                    def _(pe):
                        def sum_gates(n):
                            pe.wait_ge(gtri_ready, n + 1)
                            if n:
                                pe.wait_ge(v_ready, n)
                            nc.tensor.matmul(bank(KB + 1, 0, LH * S), k["upto"], gtri[:].rearrange("p h t -> p (h t)"), start=True, stop=True).then_inc(decay_ps, 1)

                        def queries(n):
                            if n == 0:
                                pe.wait_ge(loaded["wattn1"], 48)
                            pe.wait_ge(z_ready, n // HT + 1)
                            if n:
                                pe.wait_ge(yT_ready, n)
                            for c in range(LH):
                                mm = nc.tensor.matmul(bank(QB + c // 4, P * (c % 4), P * (c % 4) + P), wqk[:, P * c:P * c + P], uT[:, P * n:P * n + P], start=True, stop=True)
                            mm.then_inc(q_ps, 1)

                        def keys(n):
                            pe.wait_ge(decay_ready, n + 1)
                            if n and OUT_BANKS[n - 1] == KB:
                                pe.wait_ge(out_read, n)
                            for c in range(LH):
                                mm = nc.tensor.matmul(bank(KB + c // 4, P * (c % 4), P * (c % 4) + P), wqk[:, P * (LH + c):P * (LH + c) + P], uT[:, P * n:P * n + P], start=True, stop=True)
                            mm.then_inc(k_ps, 1)

                        def scores(n):
                            pe.wait_ge(k_ready, n + 1)
                            pe.wait_ge(q_ready, n + 1)
                            for h in range(LH):
                                mm = nc.tensor.matmul(bank(QB + h // 4, P * (h % 4), P * (h % 4) + P), qk[:, h, :], qk[:, LH + h, :], start=True, stop=True)
                            mm.then_inc(scores_ps, 1)

                        def values(n):
                            for c in range(2):
                                mm = nc.tensor.matmul(bank(KB + c), uT[:, P * n:P * n + P], wv[:, BANK * c:BANK * c + BANK], start=True, stop=True)
                            mm.then_inc(v_ps, 1)

                        def times_values(n):
                            pe.wait_ge(aT_ready, n + 1)
                            pe.wait_ge(v_ready, n + 1)
                            for h in range(LH):
                                mm = nc.tensor.matmul(bank(QB + h // 4, P * (h % 4), P * (h % 4) + P), v[:, LD * h:LD * h + LD], abd[:, h, :], start=True, stop=True)
                            mm.then_inc(yT_ps, 1)

                        def output(n):
                            pe.wait_ge(yT_ready, n + 1)
                            if n and OUT_BANKS[n - 1] == OUT_BANKS[n]:
                                pe.wait_ge(out_read, n)
                            for c in range(LH):
                                mm = nc.tensor.matmul(bank(OUT_BANKS[n], 0, E), yT[:, c, :], wout[:, c, :], start=(c == 0), stop=(c == LH - 1))
                            mm.then_inc(out_ps, 1)

                        def transpose_c(n):
                            pe.wait_ge(c_done, TILES + n + 1)
                            if n:
                                pe.wait_ge(o_ready, n)
                            nc.tensor.transpose(bank(FB, 0, P), featT[:, P * n:P * n + P], k["ident"]).then_inc(ct_ps, 1)

                        def transpose_xq(n):
                            pe.wait_ge(xq_ready, n + 1)
                            nc.tensor.transpose(bank(FB, P, P + P // 2).bitcast(BF16), xq[:], ident_b[:]).then_inc(xqT_ps, 1)

                        def spread_scale(n):
                            pe.wait_ge(diag_ready, n + 1)
                            pe.wait_ge(xqT_ready, n + 1)
                            nc.tensor.matmul(bank(FB, 3 * P // 2, 5 * P // 2), k["ones"], dg[:], start=True, stop=True).then_inc(sbc_ps, 1)

                        def hidden(n):
                            pe.wait_ge(sbc_ready, n + 1)
                            for f in range(NF):
                                mm = nc.tensor.matmul(bank(FB, P * f, P * f + P), ffn_q[0][:, P * f:P * f + P], xqT[:], start=True, stop=True)
                            mm.then_inc(h_ps, 1)

                        def transpose_y(n):
                            pe.wait_ge(silu_ready, n + 1)
                            for f in range(NF):
                                mm = nc.tensor.transpose(bank(FB, P * f, P * f + P), ys[:, f, :], k["ident"])
                            mm.then_inc(yt_ps, 1)

                        def transpose_yq(n):
                            pe.wait_ge(yq_ready, n + 1)
                            for f in range(NF):
                                mm = nc.tensor.transpose(bank(FB, P // 2 * f, P // 2 * (f + 1)).bitcast(BF16), yq[:, P * f:P * f + P], ident_b[:])
                            mm.then_inc(yqT_ps, 1)

                        def down(n):
                            pe.wait_ge(yqT_ready, n + 1)
                            for f in range(NF):
                                mm = nc.tensor.matmul(bank(FB, 5 * P // 2, 7 * P // 2), yqT[:, f, :], ffn_q[1][:, P * f:P * f + P], start=(f == 0), stop=(f == NF - 1))
                            mm.then_inc(o_ps, 1)

                        run_in_time_order(starts, cond_tensor(pe, 1, at, x_ready) + [
                            (at["sum_gates"], sum_gates), (at["queries"], queries), (at["keys"], keys), (at["scores"], scores), (at["values"], values), (at["times_values"], times_values), (at["output"], output),
                            (at["transpose_c"], transpose_c), (at["transpose_xq"], transpose_xq), (at["spread_scale"], spread_scale), (at["hidden"], hidden),
                            (at["transpose_y"], transpose_y), (at["transpose_yq"], transpose_yq), (at["down"], down)], mixture_tensor(pe, plan, None))

                    @block.scalar
                    def _(act):
                        def exp_decay(n):
                            act.wait_ge(decay_ps, n + 1)
                            if n:
                                act.wait_ge(a_ready, n)
                            nc.scalar.activation(decay[:].rearrange("p h t -> p (h t)"), bank(KB + 1, 0, LH * S), ACT.Exp).then_inc(decay_ready, 1)

                        def copy_queries(n):
                            act.wait_ge(q_ps, n + 1)
                            if n:
                                act.wait_ge(scores_ps, n)
                            for c in range(2):
                                ins = nc.scalar.activation(qk[:, 4 * c:4 * c + 4, :].rearrange("p c t -> p (c t)"), bank(QB + c), ACT.Copy)
                            ins.then_inc(q_ready, 1)

                        def copy_keys(n):
                            act.wait_ge(k_ps, n + 1)
                            for c in range(2):
                                ins = nc.scalar.activation(qk[:, LH + 4 * c:LH + 4 * c + 4, :].rearrange("p c t -> p (c t)"), bank(KB + c), ACT.Copy)
                            ins.then_inc(k_ready, 1)

                        def copy_values(n):
                            act.wait_ge(v_ps, n + 1)
                            if n:
                                act.wait_ge(yT_ps, n)
                            for c in range(2):
                                ins = nc.scalar.activation(v[:, BANK * c:BANK * c + BANK], bank(KB + c), ACT.Copy)
                            ins.then_inc(v_ready, 1)

                        def copy_yT(n):
                            act.wait_ge(yT_ps, n + 1)
                            if n:
                                act.wait_ge(out_ps, n)
                            for c in range(2):
                                ins = nc.scalar.activation(yT[:, 4 * c:4 * c + 4, :].rearrange("p c t -> p (c t)"), bank(QB + c), ACT.Copy)
                            ins.then_inc(yT_ready, 1)

                        def copy_xqT(n):
                            act.wait_ge(xqT_ps, n + 1)
                            nc.scalar.activation(xqT[:], bank(FB, P, P + P // 2).bitcast(BF16), ACT.Copy).then_inc(xqT_ready, 1)

                        def copy_scale(n):
                            act.wait_ge(sbc_ps, n + 1)
                            nc.scalar.activation(sbc[:], bank(FB, 3 * P // 2, 5 * P // 2), ACT.Copy).then_inc(sbc_ready, 1)

                        def middle_tap(n):
                            act.wait_ge(h_ready, n + 1)
                            for f in range(NF):
                                ins = nc.scalar.activation(y[:, f], hp[:, f, :, 1:S + 1], ACT.Identity, bias=conv[:, f, 3:4], scale=conv[:, f, 1:2])
                            ins.then_inc(mid_ready, 1)

                        def silus(n):
                            act.wait_ge(conv_ready, n + 1)
                            nc.scalar.activation(ys[:].rearrange("p f t -> p (f t)"), y[:].rearrange("p f b t -> p (f b t)"), ACT.Silu).then_inc(silu_ready, 1)

                        def copy_yqT(n):
                            act.wait_ge(yqT_ps, n + 1)
                            nc.scalar.activation(yqT[:].rearrange("p f t -> p (f t)"), bank(FB, 0, P // 2 * NF).bitcast(BF16), ACT.Copy).then_inc(yqT_ready, 1)

                        run_in_time_order(starts, cond_scalar(act, 1, at) + [
                            (at["exp_decay"], exp_decay), (at["copy_queries"], copy_queries), (at["copy_keys"], copy_keys), (at["copy_values"], copy_values), (at["copy_yT"], copy_yT),
                            (at["copy_xqT"], copy_xqT), (at["copy_scale"], copy_scale), (at["middle_tap"], middle_tap), (at["silus"], silus), (at["copy_yqT"], copy_yqT)], mixture_scalar(act, plan))

                    @block.vector
                    def _(dve):
                        def level_weights(n):
                            dve.wait_ge(z_ready, n // HT + 1)
                            if n:
                                dve.wait_ge(weight_ready, n)
                            for l in range(LEVELS):
                                nc.vector.copy_predicated(lamw[:], levelmask[:, l, :].unsqueeze(1).to_broadcast([P, LH, S]),
                                                          z[:, n, LH * (l + 1):LH * (l + 2)].unsqueeze(2).to_broadcast([P, LH, S])).then_inc(dve_step, 1)
                                dve.wait_ge(dve_step, own.next())

                        def weigh_decay(n):
                            dve.wait_ge(decay_ready, n + 1)
                            nc.vector.tensor_tensor(decay[:], decay[:], lamw[:], ALU.mult).then_inc(weight_ready, 1)

                        def weigh_scores(n):
                            dve.wait_ge(weight_ready, n + 1)
                            dve.wait_ge(scores_ps, n + 1)
                            src = PS[:, QB * BANK:(QB + 2) * BANK].rearrange("p (h t) -> p h t", t=P)
                            for b in range(SEQ):
                                r = slice(S * b, S * b + S)
                                ins = nc.vector.scalar_tensor_tensor(out=a[r], in0=src[r][:, :, S * b:S * b + S], scalar=scale, in1=decay[r],
                                                                     op0=ALU.mult, op1=ALU.mult)
                            ins.then_inc(a_ready, 1)
                            dve.wait_ge(a_ready, n + 1)
                            if n:
                                dve.wait_ge(yT_ps, n)
                            for b in range(SEQ):
                                ins = nc.vector.transpose(abd[S * b:S * b + S, :, S * b:S * b + S], a[S * b:S * b + S, :, :])
                            ins.then_inc(aT_ready, 1)

                        def norm_in(n):
                            if n:
                                dve.wait_ge(x_ready, n)
                            dve.wait_ge(out_ps, n + 1)
                            nc.vector.tensor_tensor(out[:], bank(OUT_BANKS[n], 0, E), acc[:, n, :], ALU.add).then_inc(out_read, 1)
                            dve.wait_ge(out_read, n + 1)
                            nc.vector.bn_stats(bn[:], out[:]).then_inc(dve_step, 1)
                            dve.wait_ge(dve_step, own.next())
                            nc.vector.bn_aggr(mv[:], bn[:]).then_inc(var_ready, 1)
                            dve.wait_ge(var_ready, n + 1)
                            nc.vector.scalar_tensor_tensor(out=out[:], in0=out[:], scalar=mv[:, 0:1], in1=ln[:, 0, :],
                                                           op0=ALU.subtract, op1=ALU.mult).then_inc(dve_step, 1)
                            dve.wait_ge(dve_step, own.next())

                        def norm_out(n):
                            dve.wait_ge(rstd_ready, n + 1)
                            dve.wait_ge(x_biased, n + 1)
                            nc.vector.scalar_tensor_tensor(out=xres[:, n, :], in0=out[:], scalar=st[:, 1:2], in1=xres[:, n, :],
                                                           op0=ALU.mult, op1=ALU.add).then_inc(x_ready, 1)

                        def quantise(ps_ready, src, m, r, q, w, signal):
                            def step(n):
                                dve.wait_ge(ps_ready, n + 1)
                                nc.vector.tensor_reduce(m[:, 0:1], src, X, ALU.max, apply_absolute_value=True).then_inc(dve_step, 1)
                                dve.wait_ge(dve_step, own.next())
                                nc.vector.tensor_scalar(m[:, 1:2], m[:, 0:1], 1e-5, 1.0 / QMAX, ALU.max, ALU.mult).then_inc(dve_step, 1)
                                dve.wait_ge(dve_step, own.next())
                                nc.vector.reciprocal(m[:, 2:3], m[:, 1:2]).then_inc(dve_step, 1)
                                dve.wait_ge(dve_step, own.next())
                                nc.vector.tensor_scalar(r[:], src, m[:, 2:3], ROUND, ALU.mult, ALU.add).then_inc(dve_step, 1)
                                nc.vector.tensor_scalar(m[:, 3:4], m[:, 1:2], wmean[:, w:w + 1], None, ALU.mult)
                                dve.wait_ge(dve_step, own.next())
                                nc.vector.tensor_scalar(q[:], r[:], ROUND, None, ALU.subtract).then_inc(signal, 1)
                            return step

                        def pad_hidden(n):
                            dve.wait_ge(h_ps, n + 1)
                            dve.wait_ge(sbc_ready, n + 1)
                            nc.vector.tensor_tensor(hp[:, :, :, 1:S + 1], bank(FB).rearrange("p (f b t) -> p f b t", f=NF, b=SEQ),
                                                    sbc[:].rearrange("p (b t) -> p b t", t=S).unsqueeze(1).to_broadcast([P, NF, SEQ, S]), ALU.mult).then_inc(h_ready, 1)

                        def outer_taps(n):
                            dve.wait_ge(mid_ready, n + 1)
                            for f in range(NF):
                                ins = nc.vector.scalar_tensor_tensor(out=y[:, f], in0=hp[:, f, :, 0:S], scalar=conv[:, f, 0:1], in1=y[:, f], op0=ALU.mult, op1=ALU.add)
                            ins.then_inc(dve_step, 1)
                            dve.wait_ge(dve_step, own.next())
                            for f in range(NF):
                                ins = nc.vector.scalar_tensor_tensor(out=y[:, f], in0=hp[:, f, :, 2:S + 2], scalar=conv[:, f, 2:3], in1=y[:, f], op0=ALU.mult, op1=ALU.add)
                            ins.then_inc(conv_ready, 1)

                        def finish(n):
                            dve.wait_ge(o_ps, n + 1)
                            if n >= 2:
                                dve.wait_ge(stored[n % 2], 16 * (n // 2))
                            nc.vector.scalar_tensor_tensor(out=outb[n % 2][:], in0=bank(FB, 5 * P // 2, 7 * P // 2), scalar=m2[:, 3:4],
                                                           in1=xres[:, n, :], op0=ALU.mult, op1=ALU.add).then_inc(o_ready, 1)

                        dve.wait_ge(f_zeroed, 1)
                        dve.wait_ge(zeroed, 2)
                        run_in_time_order(starts, cond_vector(dve, 1, at, own, dve_step) + [
                            (at["level_weights"], level_weights), (at["weigh_decay"], weigh_decay), (at["weigh_scores"], weigh_scores), (at["norm_in"], norm_in), (at["norm_out"], norm_out),
                            (at["quantise_x"], quantise(ct_ps, bank(FB, 0, P), m1, xr, xq, 0, xq_ready)), (at["pad_hidden"], pad_hidden), (at["outer_taps"], outer_taps),
                            (at["quantise_y"], quantise(yt_ps, bank(FB), m2, yr, yq, 1, yq_ready)), (at["finish"], finish)], mixture_vector(dve, plan))

        first_phase()
        second_phase()


def kernel(**inp):
    import concourse.bacc as _bacc
    from concourse.bass_utils import run_bass_kernel_spmd as _run

    a = {n: np.asarray(v) for n, v in inp.items()}
    cat = np.concatenate
    rows = lambda v: np.tile(v.reshape(1, -1), (P, 1))
    lay = {"x": a["x"].reshape(TOK, E)}
    small = {"condT": a["cond_256"].T, "genre_w": a["L1_cond_gg_W"]}
    for n, pre in enumerate(("L0_cond_", "L1_cond2_")):
        lay[f"cond_w{n}"] = cat([a[pre + w].T for w in ("Wq", "Wk", "Wv", "Wo")], axis=1)
        small[f"mod_w{n}"] = a[pre + "Wc"].T
        small[f"mod_b{n}"] = a[pre + "bc"].reshape(2, E).T
        small[f"rms_s{n}"] = a[pre + "rms_scale"][:, None]
    lay["mask"] = np.tile(np.ascontiguousarray(a["mask_SxS_bk1"]).view(np.int32), (SEQ, 1))
    lay["attn0_qk"] = cat([a["L0_attn_w_q"], a["L0_attn_w_kv"][:, :AH * AD]], axis=1)
    lay["attn0_v"] = a["L0_attn_w_kv"][:, AH * AD:]
    lay["attn0_out"] = a["L0_attn_w_out"]
    lay["attn1_qk"] = cat([a["L1_attn_Wq"].T, a["L1_attn_Wk"].T], axis=1)
    lay["attn1_v"] = a["L1_attn_Wv"].T
    lay["attn1_out"] = a["L1_attn_Wo"].T
    pair = np.arange(4)[:, None] ^ np.arange(4)[None, :]
    small["quat"] = a["L0_cond2_q_right"][pair].transpose(0, 2, 1).reshape(P, 4)
    small["quat_l"] = a["cond_256"][pair].transpose(0, 2, 1).reshape(P, 4)
    small["quat_all"] = np.tile(a["cond_256"].T, (4, 1))
    small["sgate"] = np.tile(a["L0_cond2_spectral_gate"].reshape(S, 1), (4, 1))
    small["router_w0"], small["router_b0"] = a["L0_ffn_W_router"], rows(a["L0_ffn_b_router"])
    small["router_w1"], small["router_b1"] = a["L1_cond_wg_W"], rows(a["L1_cond_wg_b"])
    small["genre_b"] = rows(a["L1_cond_gg_b"])
    small["rms1"] = a["L1_cond_rms_w"][:, None]
    lay["ffn_w0"] = a["L1_ffn_w1"].T
    lay["ffn_w1"] = a["L1_ffn_w2"].T.reshape(HID // P, P, E).transpose(1, 0, 2).reshape(P, HID)
    taps = cat([a["L1_ffn_conv_w"][:, 0, :], a["L1_ffn_conv_b"][:, None]], axis=1)
    small["conv"] = taps.reshape(HID // P, P, 4).transpose(1, 0, 2).reshape(P, HID // P * 4)
    lay["moe0_b"] = a["L0_ffn_b1"].reshape(EXPERTS, -1, P).transpose(0, 2, 1)
    lay["moe1_b"] = cat([a["L1_cond_b1"], a["L1_cond_b2"]], axis=1).reshape(EXPERTS, -1, P).transpose(0, 2, 1)
    lay["moe0_last_b"], lay["moe1_last_b"] = rows(a["L0_ffn_b2"]), rows(a["L1_cond_b3"])
    levels = a["L1_attn_Wdl"].reshape(LH, -1, E)[:, :LEVELS].transpose(1, 0, 2).reshape(LH * LEVELS, E)
    small["small_w"] = cat([a["L1_attn_Wg"], levels], axis=0).T
    small["small_b"] = rows(cat([a["L1_attn_bg"], a["L1_attn_Lparam"][:, :LEVELS].T.reshape(-1)]))
    small["ln"] = rows(cat([a["L1_attn_ln_g"], a["L1_attn_ln_b"]]))
    for name, where in (("feat", FEAT), ("cond", COND), ("rows", ROWS)):
        lay[name] = cat([small[n] for n in where], axis=1)
    lay["moe0_w1"], lay["moe0_w2"] = a["L0_ffn_W1"], a["L0_ffn_W2"]
    lay["moe1_w1"], lay["moe1_w2"], lay["moe1_w3"] = a["L1_cond_W1"], a["L1_cond_W2"], a["L1_cond_W3"]
    lay["const"], lay["levelmask"] = constants()

    nc = _bacc.Bacc("TRN2", target_bir_lowering=False, num_devices=1)
    arrays, d = {}, {}
    for name, v in lay.items():
        v = np.ascontiguousarray(v)
        arrays[f"in_{name}_dram"] = v
        d[name] = nc.dram_tensor(f"in_{name}_dram", v.shape, mybir.dt.from_np(v.dtype), kind="ExternalInput").ap()
    d["out"] = nc.dram_tensor("out_dram", (TILES, P, E), F32, kind="ExternalOutput").ap()
    build(nc, d)
    r = _run(nc, [arrays], core_ids=[0])
    return r.results[0]["out_dram"].reshape(B, S, E)
```
